# Optimizing a Trainium2 kernel written in Bass

```python
import numpy as np
import jax
import jax.numpy as jnp

def _softmax(x, axis=-1):
    return jax.nn.softmax(x, axis=axis)

def _gelu(x):
    return jax.nn.gelu(x, approximate=True)

def _silu(x):
    return jax.nn.silu(x)

def _sigmoid(x):
    return jax.nn.sigmoid(x)

def _layernorm(x, axis=-1, eps=1e-05):
    m = jnp.mean(x, axis=axis, keepdims=True)
    v = jnp.var(x, axis=axis, keepdims=True)
    return (x - m) / jnp.sqrt(v + eps)

def _scatter_add(tgt, idx, src, axis=0):
    return tgt.at[idx].add(src)

def _segment_sum(src, seg, n):
    return jax.ops.segment_sum(src, seg, n)
kernel_name = 'mk_xattn_ffn_d2_seqx_r4_192779'

def setup_inputs(seed: int=0):
    np.random.seed(seed)
    _w = jnp.asarray

    def _rec_inputs():
        import jax
        import jax.numpy as jnp
        _rk = jax.random.key(seed)
        x = 0.01048 + 0.1018 * jax.random.normal(jax.random.fold_in(_rk, 1), (4, 512, 512), jnp.float32)
        _lenS = 512 - jax.random.randint(jax.random.fold_in(_rk, 7), (4,), 0, max(1, 512 // 4) + 1, jnp.int32)
        _lenS2 = 512 - jax.random.randint(jax.random.fold_in(_rk, 8), (4,), 0, max(1, 512 // 4) + 1, jnp.int32)
        _ctx_512P = jax.random.normal(jax.random.fold_in(_rk, 11), (4, 16, 128), jnp.float32)
        _ctx_512c = jax.random.dirichlet(jax.random.fold_in(_rk, 511), 0.3 * jnp.ones((16,), jnp.float32), (4, 512))
        _ctx_512t = jnp.einsum('bsk,bkd->bsd', _ctx_512c, _ctx_512P)
        _ctx_512t = _ctx_512t * jax.lax.rsqrt(jnp.mean(jnp.square(_ctx_512t)) + 1e-12) * 0.953939
        ctx_512 = -0.000292821 + 1.00034 * (_ctx_512t + 0.3 * jax.random.normal(jax.random.fold_in(_rk, 611), (4, 512, 128), jnp.float32))
        return (x, ctx_512)
    x, ctx_512 = _rec_inputs()

    def _L0_xattn_setup():
        import jax, jax.numpy as jnp
        import numpy as np
        LRELU_ALPHA = 0.2
        MASK_VAL = -10000000000.0
        B, N, F_IN = (4, 512, 128)
        H, F_OUT = (8, 64)
        F_HID = H * F_OUT

        def gat_layer(x, adj, W, a_self, a_neigh, b):
            feat = jnp.einsum('nf,hfo->hno', x, W)
            attn_self = jnp.einsum('hno,ho->hn', feat, a_self)
            attn_neigh = jnp.einsum('hno,ho->hn', feat, a_neigh)
            e = attn_self[:, :, None] + attn_neigh[:, None, :]
            e = jax.nn.leaky_relu(e, LRELU_ALPHA)
            e = e + MASK_VAL * (1.0 - adj)[None, :, :]
            alpha = jax.nn.softmax(e, axis=-1)
            out = jnp.einsum('hnm,hmo->hno', alpha, feat) + b[:, None, :]
            out = jnp.transpose(out, (1, 0, 2)).reshape(out.shape[1], -1)
            return jax.nn.elu(out)
        key = jax.random.key(seed)
        ks = jax.random.split(key, 10)
        feats = jax.random.normal(ks[0], (B, N, F_IN), dtype=jnp.float32)
        a = (jax.random.uniform(ks[1], (B, N, N)) < 0.01).astype(jnp.float32)
        adj = jnp.maximum(a, jnp.eye(N, dtype=jnp.float32)[None])
        s0 = 1.0 / np.sqrt(F_IN)
        s1 = 1.0 / np.sqrt(F_HID)
        return {'feats': feats, 'adj': adj, 'W0': jax.random.normal(ks[2], (H, F_IN, F_OUT), dtype=jnp.float32) * s0, 'a_self0': jax.random.normal(ks[3], (H, F_OUT), dtype=jnp.float32) * 0.1, 'a_neigh0': jax.random.normal(ks[4], (H, F_OUT), dtype=jnp.float32) * 0.1, 'b0': jnp.zeros((H, F_OUT), dtype=jnp.float32), 'W1': jax.random.normal(ks[5], (H, F_HID, F_OUT), dtype=jnp.float32) * s1, 'a_self1': jax.random.normal(ks[6], (H, F_OUT), dtype=jnp.float32) * 0.1, 'a_neigh1': jax.random.normal(ks[7], (H, F_OUT), dtype=jnp.float32) * 0.1, 'b1': jnp.zeros((H, F_OUT), dtype=jnp.float32)}
    _L0_xattn_all = _L0_xattn_setup()
    _L0_xattn_in = {k: v for k, v in _L0_xattn_all.items() if k in ('W0', 'a_self0', 'a_neigh0', 'b0', 'W1', 'a_self1', 'a_neigh1', 'b1')}
    del _L0_xattn_all

    def _L0_ffn_setup():
        import jax, jax.numpy as jnp
        import numpy as np
        B, T, D = (1, 256, 512)
        F_DIM = 352
        E = 8
        TOPK = 2
        key = jax.random.key(seed)
        ks = jax.random.split(key, 5)
        x = jax.random.normal(ks[0], (B, T, D), dtype=jnp.float32)
        gate_w = jax.random.normal(ks[1], (E, D), dtype=jnp.float32) * 0.02
        gate_proj = jax.random.normal(ks[2], (E, F_DIM, D), dtype=jnp.float32) * 0.02
        up_proj = jax.random.normal(ks[3], (E, F_DIM, D), dtype=jnp.float32) * 0.02
        down_proj = jax.random.normal(ks[4], (E, D, F_DIM), dtype=jnp.float32) * 0.02
        return {'x': x, 'gate_w': gate_w, 'gate_proj': gate_proj, 'up_proj': up_proj, 'down_proj': down_proj}
    _L0_ffn_all = _L0_ffn_setup()
    _L0_ffn_in = {k: v for k, v in _L0_ffn_all.items() if k in ('gate_w', 'gate_proj', 'up_proj', 'down_proj')}
    del _L0_ffn_all

    def _L1_xattn_setup():
        import jax, jax.numpy as jnp
        import numpy as np
        EPS = 1e-06
        IMAGE_DIMS = 512
        key = jax.random.key(seed)
        k1, k2, k3 = jax.random.split(key, 3)
        B, I, J, D = (16, 512, 512, 128)
        p = jax.random.normal(k1, (B, I, J), dtype=jnp.float32)
        k_v = jax.random.normal(k2, (B, J, D), dtype=jnp.float32)
        W_k = jax.random.normal(k3, (D, D), dtype=jnp.float32) * (1.0 / np.sqrt(D))
        b_k = jnp.zeros((D,), dtype=jnp.float32)
        ln_gamma = jnp.ones((J,), dtype=jnp.float32)
        ln_beta = jnp.zeros((J,), dtype=jnp.float32)
        return {'p': p, 'k_v': k_v, 'W_k': W_k, 'b_k': b_k, 'ln_gamma': ln_gamma, 'ln_beta': ln_beta}
    _L1_xattn_all = _L1_xattn_setup()
    _L1_xattn_in = {k: v for k, v in _L1_xattn_all.items() if k in ('W_k', 'b_k', 'ln_gamma', 'ln_beta')}
    del _L1_xattn_all

    def _L1_ffn_setup():
        import jax, jax.numpy as jnp
        import numpy as np

        def _sparsify_2to4(h):
            B, S, I = h.shape
            g = h.reshape(B, S, I // 4, 4)
            a = jnp.abs(g)
            _, idx = jax.lax.top_k(a, 2)
            pos = jnp.arange(4)
            mask = (pos == idx[..., 0:1]) | (pos == idx[..., 1:2])
            return (g * mask.astype(g.dtype)).reshape(B, S, I)
        key = jax.random.key(seed)
        k1, k2, k3, k4 = jax.random.split(key, 4)
        B, S, H, I = (4, 512, 512, 2048)
        x = jax.random.normal(k1, (B, S, H), dtype=jnp.float32)
        w_gate = jax.random.normal(k2, (H, I), dtype=jnp.float32) / np.sqrt(H)
        w_up = jax.random.normal(k3, (H, I), dtype=jnp.float32) / np.sqrt(H)
        w_down = jax.random.normal(k4, (I, H), dtype=jnp.float32) / np.sqrt(I)
        return {'x': x, 'w_gate': w_gate, 'w_up': w_up, 'w_down': w_down}
    _L1_ffn_all = _L1_ffn_setup()
    _L1_ffn_in = {k: v for k, v in _L1_ffn_all.items() if k in ('w_gate', 'w_up', 'w_down')}
    del _L1_ffn_all
    return {'x': x, 'ctx_512': ctx_512, 'L0_xattn_W0': _L0_xattn_in['W0'], 'L0_xattn_a_self0': _L0_xattn_in['a_self0'], 'L0_xattn_a_neigh0': _L0_xattn_in['a_neigh0'], 'L0_xattn_b0': _L0_xattn_in['b0'], 'L0_xattn_W1': _L0_xattn_in['W1'], 'L0_xattn_a_self1': _L0_xattn_in['a_self1'], 'L0_xattn_a_neigh1': _L0_xattn_in['a_neigh1'], 'L0_xattn_b1': _L0_xattn_in['b1'], 'L0_ffn_gate_w': _L0_ffn_in['gate_w'], 'L0_ffn_gate_proj': _L0_ffn_in['gate_proj'], 'L0_ffn_up_proj': _L0_ffn_in['up_proj'], 'L0_ffn_down_proj': _L0_ffn_in['down_proj'], 'L1_xattn_W_k': _L1_xattn_in['W_k'], 'L1_xattn_b_k': _L1_xattn_in['b_k'], 'L1_xattn_ln_gamma': _L1_xattn_in['ln_gamma'], 'L1_xattn_ln_beta': _L1_xattn_in['ln_beta'], 'L1_ffn_w_gate': _L1_ffn_in['w_gate'], 'L1_ffn_w_up': _L1_ffn_in['w_up'], 'L1_ffn_w_down': _L1_ffn_in['w_down']}

def reference(x, ctx_512, L0_xattn_W0, L0_xattn_a_self0, L0_xattn_a_neigh0, L0_xattn_b0, L0_xattn_W1, L0_xattn_a_self1, L0_xattn_a_neigh1, L0_xattn_b1, L0_ffn_gate_w, L0_ffn_gate_proj, L0_ffn_up_proj, L0_ffn_down_proj, L1_xattn_W_k, L1_xattn_b_k, L1_xattn_ln_gamma, L1_xattn_ln_beta, L1_ffn_w_gate, L1_ffn_w_up, L1_ffn_w_down):
    import jax
    import jax.numpy as jnp

    def _L0_xattn_ref(feats, adj, W0, a_self0, a_neigh0, b0, W1, a_self1, a_neigh1, b1):
        import jax, jax.numpy as jnp
        import numpy as np
        LRELU_ALPHA = 0.2
        MASK_VAL = -10000000000.0
        B, N, F_IN = (4, 512, 128)
        H, F_OUT = (8, 64)
        F_HID = H * F_OUT

        def gat_layer(x, adj, W, a_self, a_neigh, b):
            feat = jnp.einsum('nf,hfo->hno', x, W)
            attn_self = jnp.einsum('hno,ho->hn', feat, a_self)
            attn_neigh = jnp.einsum('hno,ho->hn', feat, a_neigh)
            e = attn_self[:, :, None] + attn_neigh[:, None, :]
            e = jax.nn.leaky_relu(e, LRELU_ALPHA)
            e = e + MASK_VAL * (1.0 - adj)[None, :, :]
            alpha = jax.nn.softmax(e, axis=-1)
            out = jnp.einsum('hnm,hmo->hno', alpha, feat) + b[:, None, :]
            out = jnp.transpose(out, (1, 0, 2)).reshape(out.shape[1], -1)
            return jax.nn.elu(out)

        def per_graph(x, a):
            h = gat_layer(x, a, W0, a_self0, a_neigh0, b0)
            return gat_layer(h, a, W1, a_self1, a_neigh1, b1)
        return jax.vmap(per_graph)(feats, adj)

    def _L0_ffn_ref(x, gate_w, gate_proj, up_proj, down_proj):
        import jax, jax.numpy as jnp
        import numpy as np
        B, T, D = (1, 256, 512)
        F_DIM = 352
        E = 8
        TOPK = 2
        b, t, d = x.shape
        x_flat = x.reshape(-1, d)
        n = x_flat.shape[0]
        router_logits = x_flat @ gate_w.T
        top_w, sel = jax.lax.top_k(router_logits, TOPK)
        top_w = jax.nn.softmax(top_w, axis=-1)
        tok_ids = jnp.arange(n)[:, None]
        tw = jnp.zeros((n, E), dtype=x.dtype).at[tok_ids, sel].add(top_w)
        g = jnp.einsum('nd,efd->enf', x_flat, gate_proj)
        u = jnp.einsum('nd,efd->enf', x_flat, up_proj)
        h = jax.nn.silu(g) * u
        eo = jnp.einsum('enf,edf->end', h, down_proj)
        out = jnp.einsum('end,ne->nd', eo, tw)
        return out.reshape(b, t, d)

    def _L1_xattn_ref(p, k_v, W_k, b_k, ln_gamma, ln_beta):
        import jax, jax.numpy as jnp
        import numpy as np
        EPS = 1e-06
        IMAGE_DIMS = 512
        kv = k_v @ W_k.T + b_k
        out = jnp.einsum('bij,bjd->bid', p, kv)
        scale = IMAGE_DIMS ** (-0.5)
        sim = jnp.einsum('bid,bjd->bij', out, kv) * scale
        mu = jnp.mean(sim, axis=-1, keepdims=True)
        var = jnp.var(sim, axis=-1, keepdims=True)
        sim = (sim - mu) * jax.lax.rsqrt(var + EPS) * ln_gamma + ln_beta
        attn = jax.nn.softmax(sim, axis=-1)
        return attn

    def _L1_ffn_ref(x, w_gate, w_up, w_down):
        import jax, jax.numpy as jnp
        import numpy as np

        def _sparsify_2to4(h):
            B, S, I = h.shape
            g = h.reshape(B, S, I // 4, 4)
            a = jnp.abs(g)
            _, idx = jax.lax.top_k(a, 2)
            pos = jnp.arange(4)
            mask = (pos == idx[..., 0:1]) | (pos == idx[..., 1:2])
            return (g * mask.astype(g.dtype)).reshape(B, S, I)
        h = jax.nn.silu(jnp.einsum('bsh,hi->bsi', x, w_gate)) * jnp.einsum('bsh,hi->bsi', x, w_up)
        h_sparse = _sparsify_2to4(h)
        return jnp.einsum('bsi,ih->bsh', h_sparse, w_down)
    x = x + _L0_xattn_ref(ctx_512, _layernorm(x, axis=-1), L0_xattn_W0, L0_xattn_a_self0, L0_xattn_a_neigh0, L0_xattn_b0, L0_xattn_W1, L0_xattn_a_self1, L0_xattn_a_neigh1, L0_xattn_b1)
    x = x + _L0_ffn_ref(_layernorm(x, axis=-1), L0_ffn_gate_w, L0_ffn_gate_proj, L0_ffn_up_proj, L0_ffn_down_proj)
    x = x + _L1_xattn_ref(_layernorm(x, axis=-1), ctx_512, L1_xattn_W_k, L1_xattn_b_k, L1_xattn_ln_gamma, L1_xattn_ln_beta)
    x = x + _L1_ffn_ref(_layernorm(x, axis=-1), L1_ffn_w_gate, L1_ffn_w_up, L1_ffn_w_down)
    return x

_drawn_inputs = setup_inputs


def setup_inputs(seed=0):
    import zlib

    import numpy as np

    out = dict(_drawn_inputs(seed))
    spreads = {'L0_xattn_b0': (0.0, 0.1),
     'L0_xattn_b1': (0.0, 0.1),
     'L1_xattn_b_k': (0.0, 2.0),
     'L1_xattn_ln_gamma': (1.0, 0.6),
     'L1_xattn_ln_beta': (0.0, 2.0)}
    factors = {'L1_xattn_W_k': 6.556}
    for name, (base, spread) in spreads.items():
        noise = np.random.default_rng([zlib.crc32(name.encode()), seed]).standard_normal(out[name].shape)
        drawn = base * np.exp(spread * noise) if base else spread * noise
        out[name] = jnp.asarray(drawn.astype(out[name].dtype))
    for name, factor in factors.items():
        out[name] = (out[name] * factor).astype(out[name].dtype)
    return out
```

```python
from contextlib import ExitStack

import concourse.bass as bass
from concourse import mybir

F32 = mybir.dt.float32
F32R = mybir.dt.float32r
BF16 = mybir.dt.bfloat16
I32 = mybir.dt.int32
ALU = mybir.AluOpType
ACT = mybir.ActivationFunctionType
AX = mybir.AxisListType

P = 128
B, N, D = 4, 512, 512
T = B * N // P
TB = N // P
DC = D // P
CTX = 128
H, FO = 8, 64
E, FE = 8, 352
RE = -(-FE // P)
WE = [min(P, FE - P * r) for r in range(RE)]
I = 2048
Q, RQ = I // (4 * P), 4
EPS = 1e-5
EPS_ATT = 1e-6
SCALE = float(D) ** -0.5
SLOPE = 0.2
MASK = 1e10
GAP_MIN = 16384.0
BOUND_MAX = 4000.0


class Chain:

    def __init__(self, eng, sem):
        self.eng, self.sem, self.n = eng, sem, 0

    def link(self, ins):
        self.n += 1
        ins.then_inc(self.sem, 1)
        self.eng.wait_ge(self.sem, self.n)


def product3(eng, out, lhs_hi, lhs_lo, rhs_hi, rhs_lo, start, stop):
    eng.matmul(out, lhs_hi, rhs_lo, start=start, stop=False)
    eng.matmul(out, lhs_lo, rhs_hi, start=False, stop=False)
    return eng.matmul(out, lhs_hi, rhs_hi, start=False, stop=stop)


class Norm:

    def __init__(self, tag, sb, sem, X, ident, negh, xT_hi, xT_lo, banks):
        self.X, self.ident, self.negh, self.hi, self.lo, self.banks = X, ident, negh, xT_hi, xT_lo, banks
        self.stats = sb(tag + "stats", [P, TB, 6], F32)
        self.mv = sb(tag + "mean_var", [P, T, 2], F32)
        self.ve = sb(tag + "var_eps", [P, T], F32)
        self.rstd = sb(tag + "rstd", [P, T], F32)
        self.xn = sb(tag + "xn", [P, 2, D], F32)
        self.var_ready = sem(tag + "var_ready")
        self.rstd_ready = sem(tag + "rstd_ready")
        self.xn_ready = sem(tag + "xn_ready")
        self.turned = sem(tag + "turned")
        self.hi_done = sem(tag + "hi_done")
        self.lo_done = sem(tag + "lo_done")

    def dve_stats(self, chain, c):
        for i in range(TB):
            ins = chain.eng.bn_stats(self.stats[:, i, :], self.X[:, TB * c + i, :])
        chain.link(ins)
        for i in range(TB):
            ins = chain.eng.bn_aggr(self.mv[:, TB * c + i, :], self.stats[:, i, :])
        chain.link(ins)
        chain.eng.tensor_scalar(self.ve[:, TB * c:TB * c + TB], self.mv[:, TB * c:TB * c + TB, 1], EPS, None,
                                ALU.add).then_inc(self.var_ready, 1)

    def pool_rstd(self, eng, c):
        eng.wait_ge(self.var_ready, c + 1)
        s = slice(TB * c, TB * c + TB)
        eng.tensor_tensor(self.rstd[:, s], self.ve[:, s], self.negh[:, 0:TB], ALU.pow).then_inc(self.rstd_ready, 1)

    def dve_norm(self, eng, t):
        if t % TB == 0:
            eng.wait_ge(self.rstd_ready, t // TB + 1)
        if t >= 2:
            eng.wait_ge(self.turned, t - 1)
        eng.tensor_scalar(self.xn[:, t % 2, :], self.X[:, t, :], self.mv[:, t, 0:1], self.rstd[:, t:t + 1],
                          ALU.subtract, ALU.mult).then_inc(self.xn_ready, 1)

    def pe_turn(self, eng, t):
        bank = self.banks[t % 2]
        eng.wait_ge(self.xn_ready, t + 1)
        if t >= 2:
            eng.wait_ge(self.lo_done, t - 1)
        for d in range(DC):
            ins = eng.transpose(bank[:, P * d:P * d + P], self.xn[:, t % 2, P * d:P * d + P], self.ident[:, :])
        ins.then_inc(self.turned, 1)

    def act_hi(self, eng, t):
        eng.wait_ge(self.turned, t + 1)
        eng.copy(self.hi[:, :, P * t:P * t + P],
                 self.banks[t % 2].rearrange("p (d n) -> p d n", d=DC)).then_inc(self.hi_done, 1)

    def dve_lo(self, eng, t):
        eng.wait_ge(self.hi_done, t + 1)
        eng.tensor_tensor(self.lo[:, :, P * t:P * t + P], self.banks[t % 2].rearrange("p (d n) -> p d n", d=DC),
                          self.hi[:, :, P * t:P * t + P].bitcast(F32), ALU.subtract).then_inc(self.lo_done, 1)


def gat_one_hot(nc, outer, dram):
    X, ident, negh, flag = outer["X"], outer["ident"], outer["negh"], outer["flag"]
    with ExitStack() as ctx:
        def sb(name, shape, dt=F32):
            return ctx.enter_context(nc.sbuf_tensor("g_" + name, shape, dt))

        sem = outer["sem"]
        ps = outer["ps"]

        ctx_raw = sb("ctx_raw", [P, T, CTX])
        ctx_hi = sb("ctx_hi", [P, T, CTX], F32R)
        ctx_lo = sb("ctx_lo", [P, T, CTX], F32R)
        w_raw = sb("w_raw", [P, 1 + DC, H * FO])
        w_hi = sb("w_hi", [P, 1 + DC, H * FO], F32R)
        w_lo = sb("w_lo", [P, 1 + DC, H * FO], F32R)
        att = sb("att", [P, 2, H * FO])
        b0_col = sb("b0_col", [P, DC])
        b1_row = sb("b1_row", [P, D])
        stats = sb("stats", [P, TB, 6])
        mv = sb("mean_var", [P, T, 2])
        ve = sb("var_eps", [P, T])
        rstd = sb("rstd", [P, T])
        adj = sb("adj", [P, 2, N])
        top = sb("top", [P, T, 8])
        pick = sb("pick", [P, 2, TB, N], F32R)
        g_hi = sb("g_hi", [P, N], F32R)
        g_lo = sb("g_lo", [P, N], F32R)
        ebuf = sb("ebuf", [P, 2, N])
        rbuf = sb("rbuf", [P, 2, N])
        hbuf = sb("hbuf", [P, 2, N])
        h_hi = sb("h_hi", [P, 2, DC, N], F32R)
        h_lo = sb("h_lo", [P, 2, DC, N], F32R)
        f_hi = sb("f_hi", [P, TB, D], F32R)
        f_lo = sb("f_lo", [P, TB, D], F32R)
        wsum = sb("wsum", [P, 1 + DC, H])
        wmax = sb("wmax", [P, 1 + DC])
        csum = sb("csum", [P, T])
        hmax = sb("hmax", [P, T])
        hcol = sb("hcol", [P, DC])
        hw = sb("hw", [P, DC])
        tops = sb("tops", [P, T, 2])
        gap = sb("gap", [P, T])
        per_part = sb("per_part", [P, 4])
        red = sb("red", [1, 8])
        zbuf = sb("zbuf", [P, 2, N])
        zexp = sb("zexp", [P, 2, N])

        TBANK = [ps[:, 0, :], ps[:, 1, :]]
        GBANK = ps[:, 2, :]
        HBANK = [ps[:, 3, :], ps[:, 4, :]]
        RING = [ps[:, 5, :], ps[:, 6, :], ps[:, 7, :]]

        ld_x = [sem(f"ga_ld_x{b}") for b in range(B)]
        ld_ctx, ld_w, ld_att0, ld_att1, ld_b = (sem("ga_" + n) for n in ("ld_ctx", "ld_w", "ld_att0", "ld_att1", "ld_b"))
        ctx_hi_done, ctx_lo_done = sem("ga_ctx_hi_done"), sem("ga_ctx_lo_done")
        w_hi_done, w_lo_done = sem("ga_w_hi_done"), sem("ga_w_lo_done")
        att_abs, att_free = sem("ga_att_abs"), sem("ga_att_free")
        var_ready, rstd_ready = sem("ga_var_ready"), sem("ga_rstd_ready")
        hot_ready, turned, pick_done = sem("ga_hot_ready"), sem("ga_turned"), sem("ga_pick_done")
        g_done, g_hi_done, g_lo_done = sem("ga_g_done"), sem("ga_g_hi_done"), sem("ga_g_lo_done")
        h_done, h_act, h_exp1, h_sum, h_hi_done, h_lo_done = (
            sem("ga_" + n) for n in ("h_done", "h_act", "h_exp1", "h_sum", "h_hi_done", "h_lo_done"))
        f_done, f_hi_done, ring_free = sem("ga_f_done"), sem("ga_f_hi_done"), sem("ga_ring_free")
        o_done, z_exp, y_ready, x_added = sem("ga_o_done"), sem("ga_z_exp"), sem("ga_y_ready"), sem("ga_x_added")
        dve_chain = sem("ga_dve_chain")
        bounds_ready, bounds_turned = sem("ga_bounds_ready"), sem("ga_bounds_turned")
        pool_const = outer["pool_const"]

        with nc.Block() as block:
            @block.sync
            def _(sp):
                sp.dma_start(X[:, 0:TB, :], dram["x"][0]).then_inc(ld_x[0], 16)
                sp.dma_start(w_raw[:, :, :], dram["gat_w"]).then_inc(ld_w, 16)
                sp.dma_start(ctx_raw[:, :, :], dram["ctx"]).then_inc(ld_ctx, 16)
                sp.dma_start(b0_col[:, :], dram["b0_col"]).then_inc(ld_b, 16)
                sp.dma_start(b1_row[:, :], dram["b1"].broadcast_to([P, D])).then_inc(ld_b, 16)
                for b in range(1, B):
                    sp.dma_start(X[:, TB * b:TB * b + TB, :], dram["x"][b]).then_inc(ld_x[b], 16)
                for j in range(2):
                    sp.dma_start(att[:, j, :], dram["att0"][j:j + 1, :].broadcast_to([P, D])).then_inc(ld_att0, 16)
                sp.wait_ge(att_free, 1)
                for j in range(2):
                    sp.dma_start(att[:, j, :], dram["att1"][j:j + 1, :].broadcast_to([P, D])).then_inc(ld_att1, 16)
                for r in range(RE):
                    sp.dma_start(outer["raw_gu"][:, r, :, :], dram["moe_gu"][r]).then_inc(outer["ld_gu"][r], 16)
                for r in range(RE):
                    sp.dma_start(outer["raw_dn"][:, r, :], dram["moe_dn"][r]).then_inc(outer["ld_dn"][r], 16)

            @block.gpsimd
            def _(pool):
                pool.memset(ident[:, :], 0.0).then_inc(pool_const, 1)
                pool.memset(negh[:, :], -0.5).then_inc(pool_const, 1)
                pool.wait_ge(pool_const, 2)
                pool.affine_select(out=ident[:, :], in_=ident[:, :], compare_op=ALU.not_equal, fill=1.0, base=0,
                                   pattern=[[-1, P]], channel_multiplier=1).then_inc(pool_const, 1)

                def rstd_of(b):
                    pool.wait_ge(var_ready, b + 1)
                    s = slice(TB * b, TB * b + TB)
                    pool.tensor_tensor(rstd[:, s], ve[:, s], negh[:, 0:TB], ALU.pow).then_inc(rstd_ready, 1)

                def layer1_sum(b):
                    for fc in range(DC):
                        j = DC * b + fc
                        pool.wait_ge(h_exp1, j + 1)
                        if j >= 2:
                            pool.wait_ge(h_lo_done, j - 1)
                        pool.tensor_tensor(hbuf[:, j % 2, :], ebuf[:, j % 2, :], rbuf[:, j % 2, :],
                                           ALU.add).then_inc(h_sum, 1)

                def add_x(b):
                    for i in range(TB):
                        t = TB * b + i
                        pool.wait_ge(y_ready, t + 1)
                        pool.tensor_tensor(X[:, t, :], X[:, t, :], zbuf[:, t % 2, :], ALU.add).then_inc(x_added, 1)

                pool.wait_ge(w_hi_done, 1)
                pool.tensor_tensor(w_lo[:, :, :], w_raw[:, :, :], w_hi[:, :, :].bitcast(F32),
                                   ALU.subtract).then_inc(w_lo_done, 1)
                rstd_of(0)
                layer1_sum(0)
                for b in range(B):
                    if b + 1 < B:
                        rstd_of(b + 1)
                        layer1_sum(b + 1)
                    add_x(b)

            @block.tensor
            def _(pe):
                pe.wait_ge(pool_const, 3)
                pe.wait_ge(w_lo_done, 1)
                pe.wait_ge(ctx_lo_done, 1)

                def first_layer(b):
                    for i in range(TB):
                        t = TB * b + i
                        pe.wait_ge(hot_ready, t + 1)
                        if t >= 2:
                            pe.wait_ge(pick_done, t - 1)
                        for m in range(TB):
                            ins = pe.transpose(TBANK[t % 2][:, P * m:P * m + P], adj[:, t % 2, P * m:P * m + P],
                                               ident[:, :])
                        ins.then_inc(turned, 1)
                    pe.wait_ge(pick_done, TB * (b + 1))
                    if b >= 1:
                        pe.wait_ge(g_lo_done, b)
                    for m in range(TB):
                        pe.matmul(GBANK, ctx_lo[:, TB * b + m, :], pick[:, b % 2, m, :], start=(m == 0), stop=False)
                        ins = pe.matmul(GBANK, ctx_hi[:, TB * b + m, :], pick[:, b % 2, m, :], start=False,
                                        stop=(m == TB - 1))
                    ins.then_inc(g_done, 1)
                    pe.wait_ge(g_lo_done, b + 1)
                    for fc in range(DC):
                        j = DC * b + fc
                        if j >= 2:
                            pe.wait_ge(h_act, j - 1)
                        product3(pe, HBANK[j % 2], w_hi[:, 0, P * fc:P * fc + P], w_lo[:, 0, P * fc:P * fc + P],
                                 g_hi[:, :], g_lo[:, :], True, True).then_inc(h_done, 1)

                def second_layer(b):
                    pe.wait_ge(h_lo_done, DC * (b + 1))
                    for m in range(TB):
                        u = 2 * TB * b + m
                        if u >= 3:
                            pe.wait_ge(ring_free, u - 2)
                        for d in range(DC):
                            ins = product3(pe, RING[u % 3], h_hi[:, b % 2, d, P * m:P * m + P],
                                           h_lo[:, b % 2, d, P * m:P * m + P], w_hi[:, 1 + d, :], w_lo[:, 1 + d, :],
                                           d == 0, d == DC - 1)
                        ins.then_inc(f_done, 1)
                    for n in range(TB):
                        u = 2 * TB * b + TB + n
                        pe.wait_ge(ring_free, max(u - 2, 2 * TB * b + TB))
                        for m in range(TB):
                            lhs = pick[:, b % 2, m, P * n:P * n + P]
                            pe.matmul(RING[u % 3], lhs, f_lo[:, m, :], start=(m == 0), stop=False)
                            ins = pe.matmul(RING[u % 3], lhs, f_hi[:, m, :], start=False, stop=(m == TB - 1))
                        ins.then_inc(o_done, 1)

                first_layer(0)
                for b in range(B):
                    if b + 1 < B:
                        first_layer(b + 1)
                    second_layer(b)
                pe.wait_ge(bounds_ready, 1)
                for j in range(4):
                    ins = pe.transpose(TBANK[0][0:1, P * j:P * j + P], per_part[:, j:j + 1], ident[:, :])
                ins.then_inc(bounds_turned, 1)

            @block.scalar
            def _(act):
                act.wait_ge(ld_w, 16)
                act.copy(w_hi[:, :, :], w_raw[:, :, :]).then_inc(w_hi_done, 1)
                act.wait_ge(ld_ctx, 16)
                act.copy(ctx_hi[:, :, :], ctx_raw[:, :, :]).then_inc(ctx_hi_done, 1)

                def bound_part(layer):
                    act.wait_ge([ld_att0, ld_att1][layer], 32)
                    act.activation(att[:, :, :], att[:, :, :], ACT.Abs).then_inc(att_abs, 1)

                def first_layer(b):
                    for i in range(TB):
                        t = TB * b + i
                        act.wait_ge(turned, t + 1)
                        if b >= 2 and i == 0:
                            act.wait_ge(o_done, TB * (b - 1))
                        act.copy(pick[:, b % 2, :, P * i:P * i + P],
                                 TBANK[t % 2].rearrange("p (m n) -> p m n", m=TB)).then_inc(pick_done, 1)
                    act.wait_ge(g_done, b + 1)
                    act.copy(g_hi[:, :], GBANK).then_inc(g_hi_done, 1)
                    for fc in range(DC + 1):
                        j = DC * b + fc
                        if fc < DC:
                            act.wait_ge(h_done, j + 1)
                            if j >= 2:
                                act.wait_ge(h_sum, j - 1)
                            act.activation(ebuf[:, j % 2, :], HBANK[j % 2], ACT.Exp, bias=b0_col[:, fc:fc + 1])
                            act.activation(rbuf[:, j % 2, :], HBANK[j % 2], ACT.Relu,
                                           bias=b0_col[:, fc:fc + 1]).then_inc(h_act, 1)
                        if fc >= 1:
                            act.wait_ge(h_sum, j)
                            act.copy(h_hi[:, b % 2, fc - 1, :], hbuf[:, (j - 1) % 2, :]).then_inc(h_hi_done, 1)

                def second_layer(b):
                    for m in range(TB):
                        u = 2 * TB * b + m
                        act.wait_ge(f_done, TB * b + m + 1)
                        act.copy(f_hi[:, m, :], RING[u % 3]).then_inc(f_hi_done, 1)
                    for n in range(TB):
                        t = TB * b + n
                        act.wait_ge(ring_free, 2 * TB * b + TB + n + 1)
                        act.activation(zexp[:, t % 2, :], zbuf[:, t % 2, :], ACT.Exp).then_inc(z_exp, 1)

                act.wait_ge(ld_b, 32)
                bound_part(0)
                bound_part(1)
                first_layer(0)
                for b in range(B):
                    if b + 1 < B:
                        first_layer(b + 1)
                    second_layer(b)

            @block.vector
            def _(dve):
                chain = Chain(dve, dve_chain)
                dve.wait_ge(pool_const, 3)

                def norm_stats(b):
                    dve.wait_ge(ld_x[b], 16)
                    for i in range(TB):
                        ins = dve.bn_stats(stats[:, i, :], X[:, TB * b + i, :])
                    chain.link(ins)
                    for i in range(TB):
                        ins = dve.bn_aggr(mv[:, TB * b + i, :], stats[:, i, :])
                    chain.link(ins)
                    dve.tensor_scalar(ve[:, TB * b:TB * b + TB], mv[:, TB * b:TB * b + TB, 1], EPS, None,
                                      ALU.add).then_inc(var_ready, 1)

                def one_hot(t):
                    if t % TB == 0:
                        dve.wait_ge(rstd_ready, t // TB + 1)
                    if t >= 2:
                        dve.wait_ge(turned, t - 1)
                    a = adj[:, t % 2, :]
                    chain.link(dve.tensor_scalar(a, X[:, t, :], mv[:, t, 0:1], rstd[:, t:t + 1], ALU.subtract,
                                                 ALU.mult))
                    chain.link(dve.tensor_scalar(a, a, -1.0, None, ALU.add))
                    chain.link(dve.max(top[:, t, :], a))
                    dve.tensor_scalar(a, a, top[:, t, 0:1], None, ALU.is_ge).then_inc(hot_ready, 1)

                def split_ctx():
                    dve.wait_ge(ctx_hi_done, 1)
                    dve.tensor_tensor(ctx_lo[:, :, :], ctx_raw[:, :, :], ctx_hi[:, :, :].bitcast(F32),
                                      ALU.subtract).then_inc(ctx_lo_done, 1)
                    chain.link(dve.tensor_reduce(csum[:, :], ctx_raw[:, :, :], AX.X, ALU.add,
                                                 apply_absolute_value=True))

                def bound_part(layer):
                    dve.wait_ge(att_abs, layer + 1)
                    chain.link(dve.tensor_tensor(att[:, 0, :], att[:, 0, :], att[:, 1, :], ALU.add))
                    if layer == 0:
                        dve.wait_ge(w_lo_done, 1)
                    for k in ([0] if layer == 0 else range(1, 1 + DC)):
                        ins = dve.tensor_tensor(w_raw[:, k, :], w_raw[:, k, :], att[:, 0, :], ALU.mult)
                    chain.link(ins)
                    s = slice(0, 1) if layer == 0 else slice(1, 1 + DC)
                    chain.link(dve.tensor_reduce(wsum[:, s, :],
                                                 w_raw[:, s, :].rearrange("p k (h o) -> p k h o", h=H), AX.X, ALU.add,
                                                 apply_absolute_value=True))
                    if layer == 0:
                        dve.tensor_reduce(wmax[:, s], wsum[:, s, :], AX.X, ALU.max).then_inc(att_free, 1)
                    else:
                        dve.tensor_reduce(wmax[:, s], wsum[:, s, :], AX.X, ALU.max)

                def first_layer(b):
                    for i in range(TB):
                        one_hot(TB * b + i)
                    if b + 1 < B:
                        norm_stats(b + 1)
                    dve.wait_ge(g_hi_done, b + 1)
                    dve.tensor_tensor(g_lo[:, :], GBANK, g_hi[:, :].bitcast(F32), ALU.subtract).then_inc(g_lo_done, 1)
                    for fc in range(DC + 1):
                        j = DC * b + fc
                        if fc < DC:
                            dve.wait_ge(h_act, j + 1)
                            dve.tensor_reduce(hmax[:, j:j + 1], rbuf[:, j % 2, :], AX.X, ALU.max)
                            dve.tensor_scalar(ebuf[:, j % 2, :], ebuf[:, j % 2, :], 1.0, -1.0, ALU.min,
                                              ALU.add).then_inc(h_exp1, 1)
                        if fc >= 1:
                            dve.wait_ge(h_hi_done, j)
                            dve.tensor_tensor(h_lo[:, b % 2, fc - 1, :], hbuf[:, (j - 1) % 2, :],
                                              h_hi[:, b % 2, fc - 1, :].bitcast(F32), ALU.subtract).then_inc(h_lo_done, 1)

                def second_layer(b):
                    for m in range(TB):
                        u = 2 * TB * b + m
                        dve.wait_ge(f_hi_done, TB * b + m + 1)
                        dve.tensor_tensor(f_lo[:, m, :], RING[u % 3], f_hi[:, m, :].bitcast(F32),
                                          ALU.subtract).then_inc(ring_free, 1)
                    for n in range(TB + 1):
                        t = TB * b + n
                        if n < TB:
                            u = 2 * TB * b + TB + n
                            dve.wait_ge(o_done, t + 1)
                            if t >= 2:
                                dve.wait_ge(x_added, t - 1)
                            dve.tensor_tensor(zbuf[:, t % 2, :], RING[u % 3], b1_row[:, :], ALU.add).then_inc(ring_free, 1)
                        if n >= 1:
                            k = (t - 1) % 2
                            dve.wait_ge(z_exp, t)
                            chain.link(dve.tensor_scalar(zexp[:, k, :], zexp[:, k, :], 1.0, -1.0, ALU.min, ALU.add))
                            dve.scalar_tensor_tensor(out=zbuf[:, k, :], in0=zbuf[:, k, :], scalar=0.0,
                                                     in1=zexp[:, k, :], op0=ALU.max, op1=ALU.add).then_inc(y_ready, 1)

                norm_stats(0)
                split_ctx()
                bound_part(0)
                bound_part(1)
                first_layer(0)
                for b in range(B):
                    if b + 1 < B:
                        first_layer(b + 1)
                    second_layer(b)

                chain.link(dve.tensor_scalar(tops[:, :, :], top[:, :, 0:2], MASK, None, ALU.mult))
                chain.link(dve.tensor_tensor(gap[:, :], tops[:, :, 0], tops[:, :, 1], ALU.subtract))
                chain.link(dve.tensor_scalar(gap[:, :], gap[:, :], GAP_MIN, None, ALU.is_ge))
                chain.link(dve.tensor_reduce(per_part[:, 0:1], gap[:, :], AX.X, ALU.min))
                chain.link(dve.tensor_reduce(per_part[:, 1:2], csum[:, :], AX.X, ALU.max))
                chain.link(dve.tensor_copy(per_part[:, 2:3], wmax[:, 0:1]))
                chain.link(dve.tensor_reduce(hcol[:, :], hmax[:, :].rearrange("p (b f) -> p f b", b=B), AX.X, ALU.max))
                chain.link(dve.tensor_scalar(hcol[:, :], hcol[:, :], 1.0, None, ALU.max))
                chain.link(dve.tensor_tensor(hw[:, :], hcol[:, :], wmax[:, 1:1 + DC], ALU.mult))
                dve.tensor_reduce(per_part[:, 3:4], hw[:, :], AX.X, ALU.add).then_inc(bounds_ready, 1)
                dve.wait_ge(bounds_turned, 1)
                row = TBANK[0]
                dve.tensor_reduce(red[:, 0:1], row[0:1, 0:P], AX.X, ALU.min)
                dve.tensor_reduce(red[:, 1:2], row[0:1, P:2 * P], AX.X, ALU.max)
                dve.tensor_reduce(red[:, 2:3], row[0:1, 2 * P:3 * P], AX.X, ALU.max)
                chain.link(dve.tensor_reduce(red[:, 3:4], row[0:1, 3 * P:4 * P], AX.X, ALU.add))
                chain.link(dve.tensor_tensor(red[:, 4:5], red[:, 1:2], red[:, 2:3], ALU.mult))
                chain.link(dve.tensor_scalar(red[:, 5:7], red[:, 3:5], BOUND_MAX, None, ALU.is_le))
                chain.link(dve.tensor_tensor(red[:, 5:6], red[:, 5:6], red[:, 6:7], ALU.mult))
                chain.link(dve.tensor_tensor(red[:, 5:6], red[:, 5:6], red[:, 0:1], ALU.mult))
                dve.tensor_copy(flag[:, :], red[:, 5:6])



class LoopChain:

    def __init__(self, eng, sem, per, turn):
        self.eng, self.sem, self.per, self.turn, self.n = eng, sem, per, turn, 0

    def link(self, ins):
        self.n += 1
        ins.then_inc(self.sem, 1)
        self.eng.wait_ge(self.sem, self.per * self.turn + self.n)

    def end(self):
        assert self.n == self.per, self.n


def gat_general(nc, outer, dram):
    X, ident, negh, ps = (outer[k] for k in ("X", "ident", "negh", "ps"))
    with ExitStack() as ctx:
        def sb(name, shape, dt=F32):
            return ctx.enter_context(nc.sbuf_tensor("gg_" + name, shape, dt))

        sems = []

        def sem(name):
            sems.append(nc.alloc_semaphore(name="gg_" + name))
            return sems[-1]

        cT = sb("ctxT", [P, 1, B * N])
        hT = sb("hT", [P, DC, B * N])
        w = sb("w", [P, 1 + DC, D])
        att = sb("att", [P, 2, 2, D])
        bias = sb("bias", [P, 2, D])
        pick_head = sb("pick_head", [H, H, P])
        lhs = sb("lhs", [P, DC, P])
        feat = sb("feat", [P, T, D])
        tmp = sb("tmp", [P, D])
        s_self = sb("s_self", [P, T, H])
        s_neigh = sb("s_neigh", [P, H])
        nT = sb("nT", [H, B * N])
        nTb = sb("nTb", [H, N])
        neigh = sb("neigh", [P, H, N])
        mv = sb("mv", [P, T, 2])
        st = sb("st", [P, 6])
        rstd = sb("rstd", [P, T])
        mask = sb("mask", [P, N])
        sc = sb("sc", [P, N])
        al = sb("al", [P, N])
        alT = sb("alT", [P, TB, P])
        nmax = sb("nmax", [P, 1])
        den = sb("den", [P, 1])
        z = sb("z", [P, D])
        ez = sb("ez", [P, D])

        ld, ld_x = sem("ld"), sem("ld_x")
        head_const, var_ready, rstd_ready, chain0 = sem("head_const"), sem("var_ready"), sem("rstd_ready"), sem("chain0")
        L = [{k: sem(f"{k}{layer}") for k in
              ("lhs_ready", "feat_done", "neigh_ready", "neigh_turned", "nT_ready", "spread", "spread_read",
               "sc_ready", "al_ready", "al_turned", "alT_ready", "mixed", "z_ready", "ez_ready", "y_ready", "y_turned",
               "chain_f", "chain_h", "chain_m", "chain_z", "mask_ready")} for layer in range(2)]

        with nc.Block() as block:
            @block.sync
            def _(sp):
                sp.dma_start(X[:, :, :].rearrange("p (b i) n -> p b i n", b=B),
                             dram["x"].rearrange("b p i n -> p b i n")).then_inc(ld_x, 16)
                sp.dma_start(cT[:, 0, :], dram["ctxT"]).then_inc(ld, 16)
                sp.dma_start(w[:, :, :], dram["gat_w"]).then_inc(ld, 16)
                for layer in range(2):
                    for j in range(2):
                        sp.dma_start(att[:, layer, j, :], dram[f"att{layer}"][j:j + 1, :].broadcast_to([P, D])
                                     ).then_inc(ld, 16)
                    sp.dma_start(bias[:, layer, :], dram[f"b{layer}"].broadcast_to([P, D])).then_inc(ld, 16)

            @block.gpsimd
            def _(pool):
                pool.memset(pick_head[:, :, :], 0.0).then_inc(head_const, 1)
                pool.wait_ge(head_const, 1)
                pool.affine_select(out=pick_head[:, :, :], in_=pick_head[:, :, :], compare_op=ALU.not_equal, fill=1.0,
                                   base=0, pattern=[[-1, H], [0, P]], channel_multiplier=1).then_inc(head_const, 1)
                pool.wait_ge(var_ready, 1)
                for c in range(B):
                    s = slice(TB * c, TB * c + TB)
                    pool.tensor_tensor(rstd[:, s], rstd[:, s], negh[:, 0:TB], ALU.pow).then_inc(rstd_ready, 1)

            @block.tensor
            def _(pe):
                pe.wait_ge(ld, 16 * 8)
                pe.wait_ge(head_const, 2)
                for layer in range(2):
                    q = L[layer]
                    first, chunks = (0, 1) if layer == 0 else (1, DC)
                    with pe.Fori(0, T) as t:
                        pe.wait_ge(q["lhs_ready"], t + 1)
                        for k in range(chunks):
                            ins = pe.matmul(ps[:, 0, :], lhs[:, k, :], w[:, first + k, :], start=(k == 0),
                                            stop=(k == chunks - 1))
                        ins.then_inc(q["feat_done"], 1)
                        pe.wait_ge(q["neigh_ready"], t + 1)
                        pe.transpose(ps[0:H, 1, 0:P], s_neigh[:, :], ident[:, :]).then_inc(q["neigh_turned"], 1)
                    with pe.Fori(0, B) as b:
                        for h in range(H):
                            pe.wait_ge(q["nT_ready"], H * b + (h + 1))
                            pe.matmul(ps[:, 2, :], pick_head[:, h, :], nTb[:, :], start=True, stop=True).then_inc(q["spread"], 1)
                        with pe.Fori(0, TB) as i:
                            with pe.Fori(0, H) as h:
                                n = (b * TB + i) * H + h
                                pe.wait_ge(q["al_ready"], n + 1)
                                for m in range(TB):
                                    ins = pe.transpose(ps[:, 3, P * m:P * m + P], al[:, P * m:P * m + P], ident[:, :])
                                ins.then_inc(q["al_turned"], 1)
                                pe.wait_ge(q["alT_ready"], n + 1)
                                for m in range(TB):
                                    ins = pe.matmul(ps[:, 4, 0:FO], alT[:, m, :],
                                                    feat[:, bass.ds(b * TB + m, 1), bass.ds(h * FO, FO)],
                                                    start=(m == 0), stop=(m == TB - 1))
                                ins.then_inc(q["mixed"], 1)
                            if layer == 0:
                                pe.wait_ge(q["y_ready"], b * TB + i + 1)
                                for m in range(DC):
                                    ins = pe.transpose(ps[:, 5, P * m:P * m + P], z[:, P * m:P * m + P], ident[:, :])
                                ins.then_inc(q["y_turned"], 1)

            @block.scalar
            def _(act):
                for layer in range(2):
                    q = L[layer]
                    with act.Fori(0, T) as t:
                        with act.Fori(0, H) as h:
                            n = t * H + h
                            act.wait_ge(q["sc_ready"], n + 1)
                            act.activation(al[:, :], sc[:, :], ACT.Exp, bias=nmax[:, 0:1],
                                           accum_out=den[:, 0:1]).then_inc(q["al_ready"], 1)
                        act.wait_ge(q["z_ready"], t + 1)
                        act.activation(ez[:, :], ez[:, :], ACT.Exp).then_inc(q["ez_ready"], 1)

            @block.vector
            def _(dve):
                chain = Chain(dve, chain0)
                dve.wait_ge(ld_x, 16)
                dve.wait_ge(ld, 16 * 8)
                for t in range(T):
                    chain.link(dve.bn_stats(st[:, :], X[:, t, :]))
                    chain.link(dve.bn_aggr(mv[:, t, :], st[:, :]))
                dve.tensor_scalar(rstd[:, :], mv[:, :, 1], EPS, None, ALU.add).then_inc(var_ready, 1)
                dve.wait_ge(rstd_ready, B)
                for layer in range(2):
                    q = L[layer]
                    src, chunks = (cT, 1) if layer == 0 else (hT, DC)
                    with dve.Fori(0, T) as t:
                        lc = LoopChain(dve, q["chain_f"], 6, t)
                        dve.tensor_copy(lhs[:, 0:chunks, :], src[:, :, bass.ds(t * P, P)]).then_inc(q["lhs_ready"], 1)
                        dve.wait_ge(q["feat_done"], t + 1)
                        lc.link(dve.tensor_copy(feat[:, bass.ds(t, 1), :], ps[:, 0:1, :]))
                        lc.link(dve.tensor_tensor(tmp[:, :], ps[:, 0, :], att[:, layer, 0, :], ALU.mult))
                        lc.link(dve.tensor_reduce(s_self[:, bass.ds(t, 1), :], tmp[:, :].rearrange("p (h o) -> p h o", h=H),
                                                  AX.X, ALU.add))
                        lc.link(dve.tensor_tensor(tmp[:, :], ps[:, 0, :], att[:, layer, 1, :], ALU.mult))
                        lc.link(dve.tensor_reduce(s_neigh[:, :], tmp[:, :].rearrange("p (h o) -> p h o", h=H), AX.X,
                                                  ALU.add))
                        dve.sem_inc(q["neigh_ready"], 1)
                        dve.wait_ge(q["neigh_turned"], t + 1)
                        lc.link(dve.tensor_copy(nT[:, bass.ds(t * P, P)], ps[0:H, 1, 0:P]))
                        lc.end()
                    with dve.Fori(0, B) as b:
                        dve.tensor_copy(nTb[:, :], nT[:, bass.ds(b * N, N)]).then_inc(q["nT_ready"], 1)
                        for h in range(H):
                            dve.wait_ge(q["spread"], H * b + (h + 1))
                            ins = dve.tensor_copy(neigh[:, h, :], ps[:, 2, :])
                            ins.then_inc(*((q["nT_ready"], 1) if h + 1 < H else (q["spread_read"], 1)))
                        with dve.Fori(0, TB) as i:
                            t = b * TB + i
                            dve.wait_ge(q["spread_read"], b + 1)
                            lc = LoopChain(dve, q["chain_m"], 2, t)
                            lc.link(dve.tensor_scalar(mask[:, :], X[:, bass.ds(t, 1), :], mv[:, bass.ds(t, 1), 0],
                                                      rstd[:, bass.ds(t, 1)], ALU.subtract, ALU.mult))
                            lc.link(dve.tensor_scalar(mask[:, :], mask[:, :], -1.0, None, ALU.add))
                            dve.tensor_scalar(mask[:, :], mask[:, :], MASK, None, ALU.mult).then_inc(q["mask_ready"], 1)
                            lc.end()
                            with dve.Fori(0, H) as h:
                                n = t * H + h
                                dve.wait_ge(q["mask_ready"], t + 1)
                                lc = LoopChain(dve, q["chain_h"], 6, n)
                                lc.link(dve.tensor_scalar(sc[:, :], neigh[:, bass.ds(h, 1), :],
                                                          s_self[:, bass.ds(t, 1), bass.ds(h, 1)], None, ALU.add))
                                lc.link(dve.scalar_tensor_tensor(out=sc[:, :], in0=sc[:, :], scalar=SLOPE, in1=sc[:, :],
                                                                 op0=ALU.mult, op1=ALU.max))
                                lc.link(dve.tensor_tensor(sc[:, :], sc[:, :], mask[:, :], ALU.add))
                                dve.tensor_reduce(nmax[:, 0:1], sc[:, :], AX.X, ALU.max,
                                                  negate=True).then_inc(q["sc_ready"], 1)
                                dve.wait_ge(q["al_turned"], n + 1)
                                dve.tensor_copy(alT[:, :, :], ps[:, 3, :].rearrange("p (m n) -> p m n", m=TB)
                                                ).then_inc(q["alT_ready"], 1)
                                lc.link(dve.reciprocal(den[:, :], den[:, :]))
                                dve.wait_ge(q["mixed"], n + 1)
                                lc.link(dve.tensor_scalar(z[:, bass.ds(h * FO, FO)], ps[:, 4, 0:FO], den[:, 0:1], None,
                                                          ALU.mult))
                                lc.link(dve.tensor_copy(tmp[:, 0:1], den[:, 0:1]))
                                lc.end()
                            lc = LoopChain(dve, q["chain_z"], 3 if layer == 0 else 4, t)
                            lc.link(dve.tensor_tensor(z[:, :], z[:, :], bias[:, layer, :], ALU.add))
                            dve.tensor_scalar(ez[:, :], z[:, :], 0.0, None, ALU.min).then_inc(q["z_ready"], 1)
                            dve.wait_ge(q["ez_ready"], t + 1)
                            lc.link(dve.tensor_scalar(ez[:, :], ez[:, :], -1.0, None, ALU.add))
                            if layer == 0:
                                dve.scalar_tensor_tensor(out=z[:, :], in0=z[:, :], scalar=0.0, in1=ez[:, :],
                                                         op0=ALU.max, op1=ALU.add).then_inc(q["y_ready"], 1)
                                dve.wait_ge(q["y_turned"], t + 1)
                                lc.link(dve.tensor_copy(hT[:, :, bass.ds(t * P, P)],
                                                        ps[:, 5, :].rearrange("p (m n) -> p m n", m=DC)))
                            else:
                                lc.link(dve.scalar_tensor_tensor(out=z[:, :], in0=z[:, :], scalar=0.0, in1=ez[:, :],
                                                                 op0=ALU.max, op1=ALU.add))
                                lc.link(dve.tensor_tensor(X[:, bass.ds(t, 1), :], X[:, bass.ds(t, 1), :], z[:, :], ALU.add))
                            lc.end()
        nc.clear_and_free_semaphores(sems)
        nc.all_engine_barrier()


class Units:

    def __init__(self, tag, outer, U, R, slots, before, w_hi, w_lo, x_hi, x_lo, hid_hi, hid_lo, los):
        ps = outer["ps"]
        self.U, self.R, self.slots, self.before, self.los = U, R, slots, before, los
        self.w_hi, self.w_lo, self.x_hi, self.x_lo, self.hid_hi, self.hid_lo = w_hi, w_lo, x_hi, x_lo, hid_hi, hid_lo
        self.raw_gu, self.raw_dn, self.ld_gu, self.ld_dn = (outer[k] for k in ("raw_gu", "raw_dn", "ld_gu", "ld_dn"))
        self.GATE = [ps[:, 0, :], ps[:, 1, :]]
        self.UP = [ps[:, 2, :], ps[:, 3, :]]
        self.ACC = [ps[:, 4 + i, :] for i in range(TB)]
        sem = outer["sem"]
        self.gate_up_hi, self.gate_up_lo = sem(tag + "gate_up_hi"), sem(tag + "gate_up_lo")
        self.down_hi, self.down_lo = sem(tag + "down_hi"), sem(tag + "down_lo")
        self.products = sem(tag + "products")
        self.silu, self.hid_made = sem(tag + "silu"), sem(tag + "hid_made")
        self.hid_hi_done, self.hid_lo_done = sem(tag + "hid_hi_done"), sem(tag + "hid_lo_done")
        self.acc_done, self.acc_free = sem(tag + "acc_done"), sem(tag + "acc_free")

    def at(self, u, c, r):
        return self.R * 4 * u + (self.R * c + r)

    def bank(self, c, r):
        return (self.R * c + r) % 2


    def load_gate_up(self, sp, src, u, r):
        sp.wait_ge(self.gate_up_lo, self.R * u + (r - self.slots + 1))
        sp.dma_start(self.raw_gu[:, r % self.slots, :, :],
                     src[bass.ds(self.R * u + r, 1)].rearrange("o p k n -> (o p) k n")
                     ).then_inc(self.ld_gu[r % self.slots], 16)

    def load_down(self, sp, src, u, r):
        sp.wait_ge(self.down_lo, self.R * u + (r - self.R + 1))
        sp.dma_start(self.raw_dn[:, r, :], src[bass.ds(self.R * u + r, 1)].rearrange("o p n -> (o p) n")
                     ).then_inc(self.ld_dn[r], 16)


    def act_gate_up(self, act, u, r, first=False):
        uses = self.R // self.slots
        act.wait_ge(self.ld_gu[r % self.slots], 16 * uses * u + 16 * (self.before + r // self.slots + 1))
        if not first:
            act.wait_ge(self.products, self.at(u - 1, 3, r) + 1)
        act.copy(self.w_hi[:, r, 0:2, :], self.raw_gu[:, r % self.slots, :, :]).then_inc(self.gate_up_hi, 1)

    def act_down(self, act, u, r, first=False):
        act.wait_ge(self.ld_dn[r], 16 * u + 16 * (self.before_dn(r) + 1))
        if not first:
            act.wait_ge(self.acc_done, 16 * u)
        act.copy(self.w_hi[:, r, 2, :], self.raw_dn[:, r, :]).then_inc(self.down_hi, 1)

    def before_dn(self, r):
        return self.before if r < RE else 0

    def pool_gate_up(self, pool, u, r):
        pool.wait_ge(self.gate_up_hi, self.R * u + (r + 1))
        pool.tensor_tensor(self.w_lo[:, r, 0:2, :], self.raw_gu[:, r % self.slots, :, :],
                           self.w_hi[:, r, 0:2, :].bitcast(F32), ALU.subtract).then_inc(self.gate_up_lo, 1)

    def pool_down(self, pool, u, r):
        pool.wait_ge(self.down_hi, self.R * u + (r + 1))
        pool.tensor_tensor(self.w_lo[:, r, 2, :], self.raw_dn[:, r, :], self.w_hi[:, r, 2, :].bitcast(F32),
                           ALU.subtract).then_inc(self.down_lo, 1)


    def pe_gate_up(self, pe, u, c, first=False):
        s = slice(N * c, N * c + N)
        for r in range(self.R):
            if c == 0:
                pe.wait_ge(self.gate_up_lo, self.R * u + (r + 1))
            if not (first and r < 2):
                pe.wait_ge(self.hid_made, self.at(u, c, r) - 1)
            for k, bank in ((0, self.GATE), (1, self.UP)):
                for d in range(DC):
                    w = slice(P * d, P * d + P)
                    ins = product3(pe, bank[self.bank(c, r)], self.w_hi[:, r, k, w], self.w_lo[:, r, k, w],
                                   self.x_hi[:, d, s], self.x_lo[:, d, s], d == 0, d == DC - 1)
            ins.then_inc(self.products, 1)

    def pe_down(self, pe, u, c):
        pe.wait_ge(self.hid_lo_done, 4 * self.los * u + self.los * (c + 1))
        if c == 0:
            pe.wait_ge(self.down_lo, self.R * u + self.R)
        h = c % self.hid_hi.shape[1]
        for i in range(TB):
            pe.wait_ge(self.acc_free, 16 * u + (4 * c + i + 1))
            s = slice(P * i, P * i + P)
            for r in range(self.R):
                ins = product3(pe, self.ACC[i], self.hid_hi[:, h, r, s], self.hid_lo[:, h, r, s],
                               self.w_hi[:, r, 2, :], self.w_lo[:, r, 2, :], r == 0, r == self.R - 1)
            ins.then_inc(self.acc_done, 1)

    def pe_all(self, pe):
        self.pe_gate_up(pe, 0, 0, first=True)
        with pe.Fori(0, self.U - 1) as u:
            for c in range(4):
                self.pe_gate_up(pe, *((u, c + 1) if c < 3 else (u + 1, 0)))
                self.pe_down(pe, u, c)
        for c in range(4):
            if c < 3:
                self.pe_gate_up(pe, self.U - 1, c + 1)
            self.pe_down(pe, self.U - 1, c)


    def act_silu(self, act, u, c, r, sg, first=False):
        act.wait_ge(self.products, self.at(u, c, r) + 1)
        if not (first and r < 2):
            act.wait_ge(self.hid_made, self.at(u, c, r) - 1)
        k = self.bank(c, r)
        act.activation(sg[:, k, :], self.GATE[k], ACT.Silu).then_inc(self.silu, 1)

    def dve_hid(self, dve, u, c, r, sg, out):
        dve.wait_ge(self.silu, self.at(u, c, r) + 1)
        k = self.bank(c, r)
        dve.tensor_tensor(out, sg[:, k, :], self.UP[k], ALU.mult).then_inc(self.hid_made, 1)

    def dve_wait_acc(self, dve, u, c, i):
        dve.wait_ge(self.acc_done, 16 * u + (4 * c + i + 1))


def moe(nc, outer, dram):
    X, ident, negh, ps, sem = (outer[k] for k in ("X", "ident", "negh", "ps", "sem"))
    with ExitStack() as ctx:
        def sb(name, shape, dt=F32):
            return ctx.enter_context(nc.sbuf_tensor("m_" + name, shape, dt))

        x_hi = sb("x_hi", [P, DC, B * N], F32R)
        x_lo = sb("x_lo", [P, DC, B * N], F32R)
        w_hi = sb("w_hi", [P, RE, 3, D], F32R)
        w_lo = sb("w_lo", [P, RE, 3, D], F32R)
        hid_hi = sb("hid_hi", [P, 2, RE, N], F32R)
        hid_lo = sb("hid_lo", [P, 2, RE, N], F32R)
        sg = sb("sg", [P, 2, N])
        hid = sb("hid", [P, 2, N])
        gw_raw = sb("gw_raw", [P, DC, E])
        gw_hi = sb("gw_hi", [P, DC, E], F32R)
        gw_lo = sb("gw_lo", [P, DC, E], F32R)
        lgT = sb("lgT", [E, B * N])
        lg = sb("lg", [P, T, E])
        lmax = sb("lmax", [P, T])
        ex = sb("ex", [P, T, E])
        gt = sb("gt", [P, T, E, E])
        eq = sb("eq", [P, T, E, E])
        tri = sb("tri", [P, E, E])
        rank = sb("rank", [P, T, E])
        den = sb("den", [P, T])
        tw = sb("tw", [P, T, E])
        norm = Norm("m_", sb, sem, X, ident, negh, x_hi, x_lo, [ps[:, 0, :], ps[:, 1, :]])
        LG, LT = ps[:, 2, :], ps[:, 7, :]

        ld_gw, gw_hi_done, gw_lo_done, tri_done = sem("m_ld_gw"), sem("m_gw_hi_done"), sem("m_gw_lo_done"), sem("m_tri_done")
        lg_done, lgT_done, lt_done, shifted, exped = (
            sem("m_" + n) for n in ("lg_done", "lgT_done", "lt_done", "shifted", "exped"))
        dve_chain = sem("m_dve_chain")
        u = Units("m_", outer, E, RE, RE, 0, w_hi, w_lo, x_hi, x_lo, hid_hi, hid_lo, los=RE)

        with nc.Block() as block:
            @block.sync
            def _(sp):
                sp.dma_start(gw_raw[:, :, :], dram["gate_w"]).then_inc(ld_gw, 16)
                with sp.Fori(1, E) as e:
                    for r in range(RE):
                        u.load_gate_up(sp, dram["moe_gu"], e, r)
                    for r in range(RE):
                        u.load_down(sp, dram["moe_dn"], e, r)
                for r in range(RQ):
                    if r < RE:
                        sp.wait_ge(u.down_lo, RE * (E - 1) + r + 1)
                    sp.dma_start(outer["raw_dn"][:, r, :], dram["ffn_dn"][r]).then_inc(outer["ld_dn"][r], 16)
                for r in range(2):
                    sp.wait_ge(u.gate_up_lo, RE * (E - 1) + r + 1)
                    sp.dma_start(outer["raw_gu"][:, r, :, :], dram["ffn_gu"][r]).then_inc(outer["ld_gu"][r], 16)

            @block.gpsimd
            def _(pool):
                pool.memset(tri[:, :, :], 1.0).then_inc(tri_done, 1)
                pool.wait_ge(tri_done, 1)
                pool.affine_select(out=tri[:, :, :], in_=tri[:, :, :], compare_op=ALU.is_gt, fill=0.0, base=0,
                                   pattern=[[1, E], [-1, E]], channel_multiplier=0).then_inc(tri_done, 1)
                for c in range(B):
                    norm.pool_rstd(pool, c)
                with pool.Fori(0, E) as e:
                    for r in range(RE):
                        u.pool_gate_up(pool, e, r)
                    for r in range(RE):
                        u.pool_down(pool, e, r)

            @block.tensor
            def _(pe):
                for c in range(B):
                    for i in range(TB):
                        norm.pe_turn(pe, TB * c + i)
                    pe.wait_ge(norm.lo_done, TB * (c + 1))
                    if c == 0:
                        pe.wait_ge(gw_lo_done, 1)
                    if c >= 1:
                        pe.wait_ge(lgT_done, c)
                    s = slice(N * c, N * c + N)
                    for d in range(DC):
                        ins = product3(pe, LG[0:E, :], gw_hi[:, d, :], gw_lo[:, d, :], x_hi[:, d, s], x_lo[:, d, s],
                                       d == 0, d == DC - 1)
                    ins.then_inc(lg_done, 1)
                pe.wait_ge(lgT_done, B)
                for t in range(T):
                    ins = pe.transpose(LT[:, E * t:E * t + E], lgT[:, P * t:P * t + P], ident[0:E, 0:E])
                ins.then_inc(lt_done, 1)
                u.pe_all(pe)

            @block.scalar
            def _(act):
                act.wait_ge(ld_gw, 16)
                act.copy(gw_hi[:, :, :], gw_raw[:, :, :]).then_inc(gw_hi_done, 1)
                for r in range(RE):
                    u.act_gate_up(act, 0, r, first=True)
                for r in range(RE):
                    u.act_down(act, 0, r, first=True)
                for c in range(B):
                    for i in range(TB):
                        norm.act_hi(act, TB * c + i)
                    act.wait_ge(lg_done, c + 1)
                    act.copy(lgT[:, N * c:N * c + N], LG[0:E, :]).then_inc(lgT_done, 1)
                act.wait_ge(shifted, 1)
                act.activation(ex[:, :, :], lg[:, :, :], ACT.Exp).then_inc(exped, 1)

                def step(e, c, r, first=False):
                    u.act_silu(act, e, c, r, sg, first)
                    act.wait_ge(u.hid_made, u.at(e, c, r) + 1)
                    act.copy(hid_hi[:, c % 2, r, :], hid[:, u.bank(c, r), :]).then_inc(u.hid_hi_done, 1)

                for r in range(RE):
                    step(0, 0, r, first=True)
                with act.Fori(0, E - 1) as e:
                    for c in (1, 2, 3):
                        for r in range(RE):
                            step(e, c, r)
                            if c == 3:
                                u.act_gate_up(act, e + 1, r)
                    for r in range(RE):
                        step(e + 1, 0, r)
                    for r in range(RE):
                        u.act_down(act, e + 1, r)
                for c in (1, 2, 3):
                    for r in range(RE):
                        step(E - 1, c, r)

            @block.vector
            def _(dve):
                chain = Chain(dve, dve_chain)
                dve.wait_ge(gw_hi_done, 1)
                dve.tensor_tensor(gw_lo[:, :, :], gw_raw[:, :, :], gw_hi[:, :, :].bitcast(F32),
                                  ALU.subtract).then_inc(gw_lo_done, 1)
                norm.dve_stats(chain, 0)
                for c in range(B):
                    if c + 1 < B:
                        norm.dve_stats(chain, c + 1)
                    for i in range(TB + 1):
                        if i < TB:
                            norm.dve_norm(dve, TB * c + i)
                        if i >= 1:
                            norm.dve_lo(dve, TB * c + i - 1)
                dve.wait_ge(lt_done, 1)
                chain.link(dve.tensor_copy(lg[:, :, :], LT[:, 0:T * E].rearrange("p (t e) -> p t e", e=E)))
                chain.link(dve.tensor_reduce(lmax[:, :], lg[:, :, :], AX.X, ALU.max))
                of_e = lg[:, :, :].unsqueeze(3).broadcast_to([P, T, E, E])
                of_j = lg[:, :, :].unsqueeze(2).broadcast_to([P, T, E, E])
                dve.tensor_tensor(gt[:, :, :, :], of_j, of_e, ALU.is_gt)
                chain.link(dve.tensor_tensor(eq[:, :, :, :], of_j, of_e, ALU.is_equal))
                dve.wait_ge(tri_done, 2)
                chain.link(dve.tensor_tensor(eq[:, :, :, :], eq[:, :, :, :],
                                             tri[:, :, :].unsqueeze(1).broadcast_to([P, T, E, E]), ALU.mult))
                chain.link(dve.tensor_tensor(gt[:, :, :, :], gt[:, :, :, :], eq[:, :, :, :], ALU.add))
                chain.link(dve.tensor_reduce(rank[:, :, :], gt[:, :, :, :], AX.X, ALU.add))
                dve.tensor_tensor(lg[:, :, :], lg[:, :, :], lmax[:, :].unsqueeze(2).broadcast_to([P, T, E]),
                                  ALU.subtract).then_inc(shifted, 1)
                dve.wait_ge(exped, 1)
                chain.link(dve.scalar_tensor_tensor(out=ex[:, :, :], in0=rank[:, :, :], scalar=1.5, in1=ex[:, :, :],
                                                    op0=ALU.is_le, op1=ALU.mult))
                chain.link(dve.tensor_reduce(den[:, :], ex[:, :, :], AX.X, ALU.add))
                chain.link(dve.reciprocal(den[:, :], den[:, :]))
                chain.link(dve.tensor_tensor(tw[:, :, :], ex[:, :, :],
                                             den[:, :].unsqueeze(2).broadcast_to([P, T, E]), ALU.mult))
                dve.sem_inc(u.acc_free, TB)

                def hidden(e, c, first=False):
                    for r in range(RE + 1):
                        if r < RE:
                            if not (first and r < 2):
                                dve.wait_ge(u.hid_lo_done, u.at(e, c, r) - 1)
                            u.dve_hid(dve, e, c, r, sg, hid[:, u.bank(c, r), :])
                        if r >= 1:
                            dve.wait_ge(u.hid_hi_done, u.at(e, c, r))
                            dve.tensor_tensor(hid_lo[:, c % 2, r - 1, :], hid[:, u.bank(c, r - 1), :],
                                              hid_hi[:, c % 2, r - 1, :].bitcast(F32),
                                              ALU.subtract).then_inc(u.hid_lo_done, 1)

                def evac(e, c):
                    for i in range(TB):
                        t = TB * c + i
                        u.dve_wait_acc(dve, e, c, i)
                        w = tw[:, t, e:e + 1] if isinstance(e, int) else tw[:, t, bass.ds(e, 1)]
                        dve.scalar_tensor_tensor(out=X[:, t, :], in0=u.ACC[i], scalar=w, in1=X[:, t, :], op0=ALU.mult,
                                                 op1=ALU.add).then_inc(u.acc_free, 1)

                hidden(0, 0, first=True)
                with dve.Fori(0, E - 1) as e:
                    for c in range(B):
                        hidden(*((e, c + 1) if c + 1 < B else (e + 1, 0)))
                        evac(e, c)
                for c in range(B):
                    if c + 1 < B:
                        hidden(E - 1, c + 1)
                    evac(E - 1, c)




def image_attention(nc, outer, dram):
    X, ident, negh, ps, sem = (outer[k] for k in ("X", "ident", "negh", "ps", "sem"))
    with ExitStack() as ctx:
        def sb(name, shape, dt=F32):
            return ctx.enter_context(nc.sbuf_tensor("a_" + name, shape, dt))

        x_hi = sb("x_hi", [P, DC, B * N], F32R)
        x_lo = sb("x_lo", [P, DC, B * N], F32R)
        c_raw = sb("c_raw", [P, B * N])
        c_hi = sb("c_hi", [P, B * N], F32R)
        c_lo = sb("c_lo", [P, B * N], F32R)
        wk_raw = sb("wk_raw", [P, CTX])
        wk_hi = sb("wk_hi", [P, CTX], F32R)
        wk_lo = sb("wk_lo", [P, CTX], F32R)
        bk = sb("bk", [P, 1])
        gamma = sb("gamma", [P, N])
        beta = sb("beta", [P, N])
        kvT = sb("kvT", [P, N])
        kvT_hi = sb("kvT_hi", [P, B, N], F32R)
        kvT_lo = sb("kvT_lo", [P, B, N], F32R)
        kv_hi = sb("kv_hi", [P, B, TB, CTX], F32R)
        kv_lo = sb("kv_lo", [P, B, TB, CTX], F32R)
        o_hi = sb("o_hi", [P, N], F32R)
        o_lo = sb("o_lo", [P, N], F32R)
        st = sb("st", [P, 2, 6])
        mv = sb("mv", [P, T, 2])
        ve = sb("ve", [P, T])
        rs = sb("rs", [P, T])
        y = sb("y", [P, 2, N])
        nmax = sb("nmax", [P, T])
        prob = sb("prob", [P, 2, N])
        den = sb("den", [P, T])
        rden = sb("rden", [P, T])
        norm = Norm("a_", sb, sem, X, ident, negh, x_hi, x_lo, [ps[:, 0, :], ps[:, 1, :]])
        KVB, KTB, OB = ps[:, 2, :], ps[:, 3, :], ps[:, 4, :]
        SIM = [ps[:, 5, :], ps[:, 6, :], ps[:, 7, :]]

        ld_c, ld_wk, ld_row = sem("a_ld_c"), sem("a_ld_wk"), sem("a_ld_row")
        in_hi, in_lo = sem("a_in_hi"), sem("a_in_lo")
        kvT_done, kvT_made, kvT_hi_done, kvT_lo_done = (
            sem("a_" + n) for n in ("kvT_done", "kvT_made", "kvT_hi_done", "kvT_lo_done"))
        kv_turned, kv_hi_done, kv_lo_done = sem("a_kv_turned"), sem("a_kv_hi_done"), sem("a_kv_lo_done")
        o_done, o_hi_done, o_lo_done = sem("a_o_done"), sem("a_o_hi_done"), sem("a_o_lo_done")
        sim_done, sim_free = sem("a_sim_done"), sem("a_sim_free")
        var_ready, rs_ready, y_ready, prob_ready, x_added = (
            sem("a_" + n) for n in ("svar_ready", "srs_ready", "y_ready", "prob_ready", "x_added"))
        dve_chain = sem("a_dve_chain")

        with nc.Block() as block:
            @block.sync
            def _(sp):
                sp.dma_start(wk_raw[:, :], dram["wkT"]).then_inc(ld_wk, 16)
                sp.dma_start(bk[:, :], dram["bk"]).then_inc(ld_wk, 16)
                sp.dma_start(c_raw[:, :], dram["ctxT"]).then_inc(ld_c, 16)
                sp.dma_start(gamma[:, :], dram["gamma"].broadcast_to([P, N])).then_inc(ld_row, 16)
                sp.dma_start(beta[:, :], dram["beta"].broadcast_to([P, N])).then_inc(ld_row, 16)

            @block.gpsimd
            def _(pool):
                for c in range(B):
                    norm.pool_rstd(pool, c)
                for t in range(T):
                    pool.wait_ge(var_ready, t + 1)
                    pool.tensor_tensor(rs[:, t:t + 1], ve[:, t:t + 1], negh[:, 0:1], ALU.pow).then_inc(rs_ready, 1)

            @block.tensor
            def _(pe):
                pe.wait_ge(in_lo, 2)
                for b in range(B):
                    if b >= 1:
                        pe.wait_ge(kvT_made, b)
                    product3(pe, KVB, wk_hi[:, :], wk_lo[:, :], c_hi[:, N * b:N * b + N], c_lo[:, N * b:N * b + N],
                             True, True).then_inc(kvT_done, 1)
                    pe.wait_ge(kvT_made, b + 1)
                    if b >= 1:
                        pe.wait_ge(kv_lo_done, b)
                    for i in range(TB):
                        ins = pe.transpose(KTB[:, P * i:P * i + P], kvT[:, P * i:P * i + P], ident[:, :])
                    ins.then_inc(kv_turned, 1)
                for t in range(T):
                    norm.pe_turn(pe, t)
                pe.wait_ge(kv_lo_done, B)
                for b in range(B):
                    s = slice(N * b, N * b + N)
                    pe.wait_ge(norm.lo_done, TB * (b + 1))
                    if b >= 1:
                        pe.wait_ge(o_lo_done, b)
                    for j in range(TB):
                        ins = product3(pe, OB, kv_hi[:, b, j, :], kv_lo[:, b, j, :], x_hi[:, j, s], x_lo[:, j, s],
                                       j == 0, j == TB - 1)
                    ins.then_inc(o_done, 1)
                    pe.wait_ge(o_lo_done, b + 1)
                    for i in range(TB):
                        t = TB * b + i
                        if t >= 3:
                            pe.wait_ge(sim_free, t - 2)
                        product3(pe, SIM[t % 3], o_hi[:, P * i:P * i + P], o_lo[:, P * i:P * i + P], kvT_hi[:, b, :],
                                 kvT_lo[:, b, :], True, True).then_inc(sim_done, 1)

            @block.scalar
            def _(act):
                act.wait_ge(ld_wk, 32)
                act.copy(wk_hi[:, :], wk_raw[:, :]).then_inc(in_hi, 1)
                act.wait_ge(ld_c, 16)
                act.copy(c_hi[:, :], c_raw[:, :]).then_inc(in_hi, 1)
                for b in range(B):
                    act.wait_ge(kvT_made, b + 1)
                    act.copy(kvT_hi[:, b, :], kvT[:, :]).then_inc(kvT_hi_done, 1)
                    act.wait_ge(kv_turned, b + 1)
                    act.copy(kv_hi[:, b, :, :], KTB.rearrange("p (j d) -> p j d", j=TB)).then_inc(kv_hi_done, 1)
                for t in range(T):
                    norm.act_hi(act, t)
                for b in range(B):
                    act.wait_ge(o_done, b + 1)
                    if b >= 1:
                        act.wait_ge(sim_done, TB * b)
                    act.copy(o_hi[:, :], OB).then_inc(o_hi_done, 1)
                    for i in range(TB):
                        t = TB * b + i
                        act.wait_ge(y_ready, t + 1)
                        if t >= 2:
                            act.wait_ge(x_added, t - 1)
                        act.activation(prob[:, t % 2, :], y[:, t % 2, :], ACT.Exp, bias=nmax[:, t:t + 1],
                                       accum_out=den[:, t:t + 1]).then_inc(prob_ready, 1)

            @block.vector
            def _(dve):
                chain = Chain(dve, dve_chain)
                dve.wait_ge(in_hi, 2)
                dve.tensor_tensor(wk_lo[:, :], wk_raw[:, :], wk_hi[:, :].bitcast(F32), ALU.subtract).then_inc(in_lo, 1)
                dve.tensor_tensor(c_lo[:, :], c_raw[:, :], c_hi[:, :].bitcast(F32), ALU.subtract).then_inc(in_lo, 1)
                for b in range(B):
                    dve.wait_ge(kvT_done, b + 1)
                    if b >= 1:
                        dve.wait_ge(kv_turned, b)
                        dve.wait_ge(kvT_lo_done, b)
                    dve.tensor_scalar(kvT[:, :], KVB, bk[:, 0:1], None, ALU.add).then_inc(kvT_made, 1)
                    dve.wait_ge(kvT_hi_done, b + 1)
                    dve.tensor_tensor(kvT_lo[:, b, :], kvT[:, :], kvT_hi[:, b, :].bitcast(F32),
                                      ALU.subtract).then_inc(kvT_lo_done, 1)
                    dve.wait_ge(kv_hi_done, b + 1)
                    dve.tensor_tensor(kv_lo[:, b, :, :], KTB.rearrange("p (j d) -> p j d", j=TB),
                                      kv_hi[:, b, :, :].bitcast(F32), ALU.subtract).then_inc(kv_lo_done, 1)
                norm.dve_stats(chain, 0)
                for c in range(B):
                    if c + 1 < B:
                        norm.dve_stats(chain, c + 1)
                    for i in range(TB + 1):
                        if i < TB:
                            norm.dve_norm(dve, TB * c + i)
                        if i >= 1:
                            norm.dve_lo(dve, TB * c + i - 1)

                def scores_norm(t):
                    sim, yt = SIM[t % 3], y[:, t % 2, :]
                    dve.wait_ge(sim_done, t + 1)
                    chain.link(dve.bn_stats(st[:, t % 2, :], sim))
                    chain.link(dve.bn_aggr(mv[:, t, :], st[:, t % 2, :]))
                    dve.tensor_scalar(ve[:, t:t + 1], mv[:, t, 1:2], SCALE * SCALE, EPS_ATT, ALU.mult,
                                      ALU.add).then_inc(var_ready, 1)
                    if t >= 2:
                        dve.wait_ge(prob_ready, t - 1)
                    chain.n += 1
                    dve.scalar_tensor_tensor(out=yt, in0=sim, scalar=mv[:, t, 0:1], in1=gamma[:, :], op0=ALU.subtract,
                                             op1=ALU.mult).then_inc(chain.sem, 1)
                    dve.wait_ge(rs_ready, t + 1)
                    chain.link(dve.tensor_scalar(rs[:, t:t + 1], rs[:, t:t + 1], SCALE, None, ALU.mult))
                    chain.n += 1
                    dve.scalar_tensor_tensor(out=yt, in0=yt, scalar=rs[:, t:t + 1], in1=beta[:, :], op0=ALU.mult,
                                             op1=ALU.add).then_inc(chain.sem, 1)
                    dve.wait_ge(chain.sem, chain.n)
                    dve.tensor_reduce(nmax[:, t:t + 1], yt, AX.X, ALU.max, negate=True).then_inc(y_ready, 1)

                def add_prob(t):
                    dve.wait_ge(prob_ready, t + 1)
                    chain.link(dve.reciprocal(rden[:, t:t + 1], den[:, t:t + 1]))
                    dve.scalar_tensor_tensor(out=X[:, t, :], in0=prob[:, t % 2, :], scalar=rden[:, t:t + 1],
                                             in1=X[:, t, :], op0=ALU.mult, op1=ALU.add).then_inc(x_added, 1)

                dve.wait_ge(ld_row, 32)
                for b in range(B):
                    dve.wait_ge(o_hi_done, b + 1)
                    dve.tensor_tensor(o_lo[:, :], OB, o_hi[:, :].bitcast(F32), ALU.subtract).then_inc(o_lo_done, 1)
                    for i in range(TB):
                        t = TB * b + i
                        scores_norm(t)
                        dve.sem_inc(sim_free, 1)
                        if t >= 1:
                            add_prob(t - 1)
                add_prob(T - 1)


def ffn(nc, outer, dram, out):
    X, ident, negh, ps, sem = (outer[k] for k in ("X", "ident", "negh", "ps", "sem"))
    HN = N // 2
    with ExitStack() as ctx:
        def sb(name, shape, dt=F32):
            return ctx.enter_context(nc.sbuf_tensor("f_" + name, shape, dt))

        x_hi = sb("x_hi", [P, DC, B * N], F32R)
        x_lo = sb("x_lo", [P, DC, B * N], F32R)
        w_hi = sb("w_hi", [P, RQ, 3, D], F32R)
        w_lo = sb("w_lo", [P, RQ, 3, D], F32R)
        hid_hi = sb("hid_hi", [P, 1, RQ, N], F32R)
        hid_lo = sb("hid_lo", [P, 1, RQ, N], F32R)
        sg = sb("sg", [P, 2, N])
        hid = sb("hid", [P, RQ, N])
        mag = sb("mag", [P, RQ, HN])
        beats = sb("beats", [P, 6, HN], BF16)
        tally = sb("tally", [P, RQ, HN], BF16)
        norm = Norm("f_", sb, sem, X, ident, negh, x_hi, x_lo, [ps[:, 0, :], ps[:, 1, :]])
        mag_ready, mag_free, masked, dve_chain = sem("f_mag_ready"), sem("f_mag_free"), sem("f_masked"), sem("f_dve_chain")
        step_chain, stored = sem("f_step_chain"), sem("f_stored")
        u = Units("f_", outer, Q, RQ, 2, E, w_hi, w_lo, x_hi, x_lo, hid_hi, hid_lo, los=2)
        LINKS = 2 * 4

        with nc.Block() as block:
            @block.sync
            def _(sp):
                for r in range(2, RQ):
                    u.load_gate_up(sp, dram["ffn_gu"], 0, r)
                with sp.Fori(1, Q) as q:
                    for r in range(2):
                        u.load_gate_up(sp, dram["ffn_gu"], q, r)
                    for r in range(RQ):
                        u.load_down(sp, dram["ffn_dn"], q, r)
                    for r in range(2, RQ):
                        u.load_gate_up(sp, dram["ffn_gu"], q, r)
                for c in range(B):
                    sp.wait_ge(u.acc_free, TB + 16 * (Q - 1) + 4 * (c + 1))
                    sp.dma_start(out[c], X[:, TB * c:TB * c + TB, :]).then_inc(stored, 16)
                sp.wait_ge(stored, 16 * B)

            @block.gpsimd
            def _(pool):
                for r in range(RQ):
                    u.pool_gate_up(pool, 0, r)
                for r in range(RQ):
                    u.pool_down(pool, 0, r)
                for c in range(B):
                    norm.pool_rstd(pool, c)
                with pool.Fori(1, Q) as q:
                    for r in range(RQ):
                        u.pool_gate_up(pool, q, r)
                    for r in range(RQ):
                        u.pool_down(pool, q, r)

            @block.tensor
            def _(pe):
                for t in range(T):
                    norm.pe_turn(pe, t)
                pe.wait_ge(norm.lo_done, T)
                u.pe_all(pe)

            @block.scalar
            def _(act):
                for r in range(RQ):
                    u.act_gate_up(act, 0, r, first=True)
                for r in range(RQ):
                    u.act_down(act, 0, r, first=True)
                for t in range(T):
                    norm.act_hi(act, t)

                def sparsify(q, c, first=False):
                    s = 8 * q + 2 * c
                    for h in range(2):
                        half = slice(HN * h, HN * h + HN)
                        act.wait_ge(u.hid_made, u.at(q, c, RQ))
                        if not (first and h == 0):
                            act.wait_ge(mag_free, s + h)
                        act.activation(mag[:, :, :], hid[:, :, half], ACT.Abs).then_inc(mag_ready, 1)
                        if not first and h == 0:
                            act.wait_ge(u.acc_done, 16 * q + 4 * c)
                        act.wait_ge(masked, s + (h + 1))
                        act.copy(hid_hi[:, 0, :, half], hid[:, :, half]).then_inc(u.hid_hi_done, 1)

                for r in range(RQ):
                    u.act_silu(act, 0, 0, r, sg, first=True)
                sparsify(0, 0, first=True)
                with act.Fori(0, Q - 1) as q:
                    for c in (1, 2, 3):
                        for r in range(RQ):
                            u.act_silu(act, q, c, r, sg)
                            if c == 3:
                                u.act_gate_up(act, q + 1, r)
                        sparsify(q, c)
                    for r in range(RQ):
                        u.act_silu(act, q + 1, 0, r, sg)
                    sparsify(q + 1, 0)
                    for r in range(RQ):
                        u.act_down(act, q + 1, r)
                for c in (1, 2, 3):
                    for r in range(RQ):
                        u.act_silu(act, Q - 1, c, r, sg)
                    sparsify(Q - 1, c)

            @block.vector
            def _(dve):
                chain = Chain(dve, dve_chain)
                norm.dve_stats(chain, 0)
                for c in range(B):
                    if c + 1 < B:
                        norm.dve_stats(chain, c + 1)
                    for i in range(TB + 1):
                        if i < TB:
                            norm.dve_norm(dve, TB * c + i)
                        if i >= 1:
                            norm.dve_lo(dve, TB * c + i - 1)
                dve.sem_inc(u.acc_free, TB)

                def hidden(q, c, first=False):
                    if not first:
                        dve.wait_ge(u.hid_lo_done, 8 * q + 2 * c)
                    for r in range(RQ):
                        u.dve_hid(dve, q, c, r, sg, hid[:, r, :])
                    for h in range(2):
                        keep_two(q, c, h)
                        if h == 1:
                            split(q, c, 0)
                    split(q, c, 1)

                def keep_two(q, c, h):
                    links = LINKS * 4 * q + LINKS * c + 4 * h
                    half = slice(HN * h, HN * h + HN)
                    dve.wait_ge(mag_ready, 8 * q + (2 * c + h + 1))
                    for i, j0, j1, at in ((0, 1, 4, 0), (1, 2, 4, 3), (2, 3, 4, 5)):
                        n = j1 - j0
                        ins = dve.tensor_tensor(beats[:, at:at + n, :],
                                                mag[:, i, :].unsqueeze(1).broadcast_to([P, n, HN]),
                                                mag[:, j0:j1, :], ALU.is_ge)
                    ins.then_inc(step_chain, 1)
                    dve.wait_ge(step_chain, links + 1)
                    dve.sem_inc(mag_free, 1)
                    b = [beats[:, k, :] for k in range(6)]
                    dve.tensor_tensor(tally[:, 0, :], b[0], b[1], ALU.add)
                    dve.tensor_tensor(tally[:, 1, :], b[0], b[3], ALU.subtract)
                    dve.tensor_tensor(tally[:, 2, :], b[1], b[3], ALU.add)
                    dve.tensor_tensor(tally[:, 3, :], b[2], b[4], ALU.add).then_inc(step_chain, 1)
                    dve.wait_ge(step_chain, links + 2)
                    dve.tensor_tensor(tally[:, 0, :], tally[:, 0, :], b[2], ALU.add)
                    dve.tensor_tensor(tally[:, 1, :], tally[:, 1, :], b[4], ALU.subtract)
                    dve.tensor_tensor(tally[:, 2, :], tally[:, 2, :], b[5], ALU.subtract)
                    dve.tensor_tensor(tally[:, 3, :], tally[:, 3, :], b[5], ALU.add).then_inc(step_chain, 1)
                    dve.wait_ge(step_chain, links + 3)
                    for r, (bound, op) in enumerate(((1.5, ALU.is_ge), (-0.5, ALU.is_le), (0.5, ALU.is_le),
                                                     (1.5, ALU.is_le))):
                        ins = dve.scalar_tensor_tensor(out=hid[:, r, half], in0=tally[:, r, :], scalar=bound,
                                                       in1=hid[:, r, half], op0=op, op1=ALU.mult)
                    ins.then_inc(step_chain, 1)
                    dve.wait_ge(step_chain, links + 4)
                    dve.sem_inc(masked, 1)

                def split(q, c, h):
                    half = slice(HN * h, HN * h + HN)
                    dve.wait_ge(u.hid_hi_done, 8 * q + (2 * c + h + 1))
                    dve.tensor_tensor(hid_lo[:, 0, :, half], hid[:, :, half], hid_hi[:, 0, :, half].bitcast(F32),
                                      ALU.subtract).then_inc(u.hid_lo_done, 1)

                def evac(q, c):
                    for i in range(TB):
                        u.dve_wait_acc(dve, q, c, i)
                        dve.tensor_tensor(X[:, TB * c + i, :], u.ACC[i], X[:, TB * c + i, :],
                                          ALU.add).then_inc(u.acc_free, 1)

                hidden(0, 0, first=True)
                with dve.Fori(0, Q - 1) as q:
                    for c in range(4):
                        hidden(*((q, c + 1) if c < 3 else (q + 1, 0)))
                        evac(q, c)
                for c in range(4):
                    if c < 3:
                        hidden(Q - 1, c + 1)
                    evac(Q - 1, c)


def build(nc, dram, out):
    with ExitStack() as ctx:
        def sem(name):
            return ctx.enter_context(nc.semaphore(name))

        def sb(name, shape, dt=F32):
            return ctx.enter_context(nc.sbuf_tensor(name, shape, dt))

        outer = {
            "sem": sem,
            "X": sb("x", [P, T, D]),
            "raw_gu": sb("raw_gate_up", [P, RE, 2, D]),
            "raw_dn": sb("raw_down", [P, RQ, D]),
            "ident": sb("ident", [P, P]),
            "negh": sb("minus_half", [P, TB]),
            "flag": sb("flag", [1, 1], I32),
            "ps": ctx.enter_context(nc.psum_tensor("ps", [P, 8, 512], F32)),
            "ld_gu": [sem(f"ld_gate_up{r}") for r in range(RE)],
            "ld_dn": [sem(f"ld_down{r}") for r in range(RQ)],
            "pool_const": sem("pool_const"),
        }
        gat_one_hot(nc, outer, dram)
        holds = nc.values_load(outer["flag"][0:1, 0:1], min_val=0, max_val=1)
        with nc.If(holds == 0):
            gat_general(nc, outer, dram)
        moe(nc, outer, dram)
        image_attention(nc, outer, dram)
        ffn(nc, outer, dram, out)


def kernel(x, ctx_512, L0_xattn_W0, L0_xattn_a_self0, L0_xattn_a_neigh0, L0_xattn_b0, L0_xattn_W1,
           L0_xattn_a_self1, L0_xattn_a_neigh1, L0_xattn_b1, L0_ffn_gate_w, L0_ffn_gate_proj, L0_ffn_up_proj,
           L0_ffn_down_proj, L1_xattn_W_k, L1_xattn_b_k, L1_xattn_ln_gamma, L1_xattn_ln_beta, L1_ffn_w_gate,
           L1_ffn_w_up, L1_ffn_w_down):
    import numpy as np
    from concourse import bacc
    from concourse.bass_utils import run_bass_kernel_spmd

    def tokens(a):
        return a.reshape(-1, P, a.shape[-1]).transpose(1, 0, 2)

    def heads(w):
        return w.transpose(1, 0, 2).reshape(-1, P, H * FO).transpose(1, 0, 2)

    pad = ((0, 0), (0, RE * P - FE), (0, 0))

    def expert_in(w):
        return np.pad(w, pad).reshape(E * RE, P, DC, P).transpose(0, 3, 2, 1).reshape(E * RE, P, D)

    def quartet_in(w):
        return w.reshape(DC, P, Q, P, RQ).transpose(2, 4, 1, 0, 3).reshape(Q * RQ, P, D)

    a = {k: np.asarray(v) for k, v in locals().items() if hasattr(v, "shape")}
    arrays = {
        "x": a["x"].reshape(B, TB, P, D).transpose(0, 2, 1, 3),
        "ctx": tokens(a["ctx_512"]),
        "ctxT": a["ctx_512"].reshape(B * N, CTX).T,
        "gat_w": np.concatenate([heads(a["L0_xattn_W0"]), heads(a["L0_xattn_W1"])], axis=1),
        "att0": np.stack([a["L0_xattn_a_self0"].ravel(), a["L0_xattn_a_neigh0"].ravel()]),
        "att1": np.stack([a["L0_xattn_a_self1"].ravel(), a["L0_xattn_a_neigh1"].ravel()]),
        "b0_col": a["L0_xattn_b0"].reshape(DC, P).T,
        "b0": a["L0_xattn_b0"].reshape(1, D),
        "b1": a["L0_xattn_b1"].reshape(1, D),
        "gate_w": a["L0_ffn_gate_w"].reshape(E, DC, P).transpose(2, 1, 0),
        "moe_gu": np.stack([expert_in(a["L0_ffn_gate_proj"]), expert_in(a["L0_ffn_up_proj"])], axis=2),
        "moe_dn": np.pad(a["L0_ffn_down_proj"].transpose(0, 2, 1), pad).reshape(E * RE, P, D),
        "wkT": a["L1_xattn_W_k"].T,
        "bk": a["L1_xattn_b_k"].reshape(CTX, 1),
        "gamma": a["L1_xattn_ln_gamma"].reshape(1, N),
        "beta": a["L1_xattn_ln_beta"].reshape(1, N),
        "ffn_gu": np.stack([quartet_in(a["L1_ffn_w_gate"]), quartet_in(a["L1_ffn_w_up"])], axis=2),
        "ffn_dn": a["L1_ffn_w_down"].reshape(Q, P, RQ, D).transpose(0, 2, 1, 3).reshape(Q * RQ, P, D),
    }
    nc = bacc.Bacc("TRN2", target_bir_lowering=False, num_devices=1)
    in_map, dram = {}, {}
    for name, v in arrays.items():
        in_map["in_" + name] = np.ascontiguousarray(v)
        dram[name] = nc.dram_tensor("in_" + name, v.shape, mybir.dt.from_np(v.dtype), kind="ExternalInput").ap()
    out = nc.dram_tensor("out", (B, P, TB, D), F32, kind="ExternalOutput").ap()
    build(nc, dram, out)
    r = run_bass_kernel_spmd(nc, [in_map], core_ids=[0])
    return r.results[0]["out"].reshape(B, P, TB, D).transpose(0, 2, 1, 3).reshape(B, N, D)
```

```python
from contextlib import ExitStack
from itertools import islice

import concourse.bass as bass
from concourse import mybir

F32 = mybir.dt.float32
F32R = mybir.dt.float32r
BF16 = mybir.dt.bfloat16
I32 = mybir.dt.int32
ALU = mybir.AluOpType
ACT = mybir.ActivationFunctionType
AX = mybir.AxisListType

P = 128
B, N, D = 4, 512, 512
T = B * N // P
TB = N // P
DC = D // P
CTX = 128
H, FO = 8, 64
E, FE = 8, 352
RE = -(-FE // P)
I = 2048
Q, RQ = I // (4 * P), 4
EPS = 1e-5
EPS_ATT = 1e-6
SCALE = float(D) ** -0.5
SLOPE = 0.2
MASK = 1e10
GAP_MIN = 16384.0
BOUND_MAX = 4000.0
REAL = 2 * B * N // P + E - 1
NEXT, MORE = 16, 32
BIG = 65536.0


def load_expert(sp, rt, dram, e, gate_up=True, down=True):
    at = slice(e, e + 1) if isinstance(e, int) else bass.ds(e, 1)
    for d in range(DC if gate_up else 0):
        sp.dma_start(rt["raw_gu"][:, d], dram["moe_gu"][at, :, d].rearrange("o p k f -> (o p) k f")
                     ).then_inc(rt["ld_gu"], 16)
    for r in range(RE if down else 0):
        sp.dma_start(rt["raw_dn"][:, r], dram["moe_dn"][at, :, r].rearrange("o p n -> (o p) n")
                     ).then_inc(rt["ld_dn"], 16)


class Chain:

    def __init__(self, eng, sem):
        self.eng, self.sem, self.n = eng, sem, 0

    def link(self, ins):
        self.n += 1
        ins.then_inc(self.sem, 1)
        self.eng.wait_ge(self.sem, self.n)


def product3(eng, out, lhs_hi, lhs_lo, rhs_hi, rhs_lo, start, stop):
    eng.matmul(out, lhs_hi, rhs_lo, start=start, stop=False)
    eng.matmul(out, lhs_lo, rhs_hi, start=False, stop=False)
    return eng.matmul(out, lhs_hi, rhs_hi, start=False, stop=stop)


class Norm:

    def __init__(self, tag, sb, sem, X, ident, negh, banks, buffers=2):
        self.X, self.ident, self.negh, self.banks, self.nb = X, ident, negh, banks, buffers
        self.stats = sb(tag + "stats", [P, TB, 6], F32)
        self.mv = sb(tag + "mean_var", [P, T, 2], F32)
        self.ve = sb(tag + "var_eps", [P, T], F32)
        self.rstd = sb(tag + "rstd", [P, T], F32)
        self.xn = sb(tag + "xn", [P, buffers, D], F32)
        self.var_ready = sem(tag + "var_ready")
        self.rstd_ready = sem(tag + "rstd_ready")
        self.xn_ready = sem(tag + "xn_ready")
        self.turned = sem(tag + "turned")
        self.hi_done = sem(tag + "hi_done")
        self.lo_done = sem(tag + "lo_done")

    def dve_stats(self, chain, c):
        for i in range(TB):
            ins = chain.eng.bn_stats(self.stats[:, i, :], self.X[:, TB * c + i, :])
        chain.link(ins)
        for i in range(TB):
            ins = chain.eng.bn_aggr(self.mv[:, TB * c + i, :], self.stats[:, i, :])
        chain.link(ins)
        chain.eng.tensor_scalar(self.ve[:, TB * c:TB * c + TB], self.mv[:, TB * c:TB * c + TB, 1], EPS, None,
                                ALU.add).then_inc(self.var_ready, 1)

    def pool_rstd(self, eng, c):
        eng.wait_ge(self.var_ready, c + 1)
        s = slice(TB * c, TB * c + TB)
        eng.tensor_tensor(self.rstd[:, s], self.ve[:, s], self.negh[:, 0:TB], ALU.pow).then_inc(self.rstd_ready, 1)

    def dve_norm(self, eng, t):
        if t % TB == 0:
            eng.wait_ge(self.rstd_ready, t // TB + 1)
        if t >= self.nb:
            eng.wait_ge(self.turned, t - self.nb + 1)
        eng.tensor_scalar(self.xn[:, t % self.nb, :], self.X[:, t, :], self.mv[:, t, 0:1], self.rstd[:, t:t + 1],
                          ALU.subtract, ALU.mult).then_inc(self.xn_ready, 1)

    def pe_turn(self, eng, t):
        k = len(self.banks)
        bank = self.banks[t % k]
        eng.wait_ge(self.xn_ready, t + 1)
        if t >= k:
            eng.wait_ge(self.lo_done, t - k + 1)
        for d in range(DC):
            ins = eng.transpose(bank[:, P * d:P * d + P], self.xn[:, t % self.nb, P * d:P * d + P], self.ident[:, :])
        ins.then_inc(self.turned, 1)

    def act_hi(self, eng, t, hi):
        eng.wait_ge(self.turned, t + 1)
        eng.copy(hi, self.banks[t % len(self.banks)].rearrange("p (d n) -> p d n", d=DC)).then_inc(self.hi_done, 1)

    def dve_lo(self, eng, t, hi, lo):
        eng.wait_ge(self.hi_done, t + 1)
        eng.tensor_tensor(lo, self.banks[t % len(self.banks)].rearrange("p (d n) -> p d n", d=DC), hi.bitcast(F32),
                          ALU.subtract).then_inc(self.lo_done, 1)


def gat_one_hot(nc, outer, dram):
    X, ident, negh, flag = outer["X"], outer["ident"], outer["negh"], outer["flag"]
    with ExitStack() as ctx:
        def sb(name, shape, dt=F32):
            return ctx.enter_context(nc.sbuf_tensor("g_" + name, shape, dt))

        sem = outer["sem"]
        ps = outer["ps"]

        ctx_raw = sb("ctx_raw", [P, T, CTX])
        ctx_hi = sb("ctx_hi", [P, T, CTX], F32R)
        ctx_lo = sb("ctx_lo", [P, T, CTX], F32R)
        w_raw = sb("w_raw", [P, 1 + DC, H * FO])
        w_hi = sb("w_hi", [P, 1 + DC, H * FO], F32R)
        w_lo = sb("w_lo", [P, 1 + DC, H * FO], F32R)
        att = sb("att", [P, 2, H * FO])
        b0_col = sb("b0_col", [P, DC])
        b1_row = sb("b1_row", [P, D])
        stats = sb("stats", [P, TB, 6])
        mv = sb("mean_var", [P, T, 2])
        ve = sb("var_eps", [P, T])
        rstd = sb("rstd", [P, T])
        adj = sb("adj", [P, 2, N])
        top = sb("top", [P, T, 8])
        pick = sb("pick", [P, 2, TB, N], F32R)
        g_hi = sb("g_hi", [P, N], F32R)
        g_lo = sb("g_lo", [P, N], F32R)
        ebuf = sb("ebuf", [P, 2, N])
        rbuf = sb("rbuf", [P, 2, N])
        hbuf = sb("hbuf", [P, 2, N])
        h_hi = sb("h_hi", [P, 2, DC, N], F32R)
        h_lo = sb("h_lo", [P, 2, DC, N], F32R)
        f_hi = sb("f_hi", [P, TB, D], F32R)
        f_lo = sb("f_lo", [P, TB, D], F32R)
        wsum = sb("wsum", [P, 1 + DC, H])
        wmax = sb("wmax", [P, 1 + DC])
        csum = sb("csum", [P, T])
        hmax = sb("hmax", [P, T])
        hcol = sb("hcol", [P, DC])
        hw = sb("hw", [P, DC])
        tops = sb("tops", [P, T, 2])
        gap = sb("gap", [P, T])
        per_part = sb("per_part", [P, 4])
        red = sb("red", [1, 8])
        zbuf = sb("zbuf", [P, 2, N])
        zexp = sb("zexp", [P, 2, N])

        TBANK = [ps[:, 0, :], ps[:, 1, :]]
        GBANK = ps[:, 2, :]
        HBANK = [ps[:, 3, :], ps[:, 4, :]]
        RING = [ps[:, 5, :], ps[:, 6, :], ps[:, 7, :]]

        ld_x = [sem(f"ga_ld_x{b}") for b in range(B)]
        ld_ctx, ld_w, ld_att0, ld_att1, ld_b = (sem("ga_" + n) for n in ("ld_ctx", "ld_w", "ld_att0", "ld_att1", "ld_b"))
        ctx_hi_done, ctx_lo_done = sem("ga_ctx_hi_done"), sem("ga_ctx_lo_done")
        w_hi_done, w_lo_done = sem("ga_w_hi_done"), sem("ga_w_lo_done")
        att_abs, att_free = sem("ga_att_abs"), sem("ga_att_free")
        var_ready, rstd_ready = sem("ga_var_ready"), sem("ga_rstd_ready")
        hot_ready, turned, pick_done = sem("ga_hot_ready"), sem("ga_turned"), sem("ga_pick_done")
        g_done, g_hi_done, g_lo_done = sem("ga_g_done"), sem("ga_g_hi_done"), sem("ga_g_lo_done")
        h_done, h_act, h_exp1, h_sum, h_hi_done, h_lo_done = (
            sem("ga_" + n) for n in ("h_done", "h_act", "h_exp1", "h_sum", "h_hi_done", "h_lo_done"))
        f_done, f_hi_done, ring_free = sem("ga_f_done"), sem("ga_f_hi_done"), sem("ga_ring_free")
        o_done, z_exp, y_ready, x_added = sem("ga_o_done"), sem("ga_z_exp"), sem("ga_y_ready"), sem("ga_x_added")
        dve_chain = sem("ga_dve_chain")
        bounds_ready, bounds_turned = sem("ga_bounds_ready"), sem("ga_bounds_turned")
        pool_const = outer["pool_const"]

        steps = [(b if b < B else None, b - 1 if b >= 1 else None) for b in range(B + 1)]

        with nc.Block() as block:
            @block.sync
            def _(sp):
                sp.dma_start(X[:, 0:TB, :], dram["x"][0]).then_inc(ld_x[0], 16)
                sp.dma_start(w_raw[:, :, :], dram["gat_w"]).then_inc(ld_w, 16)
                sp.dma_start(ctx_raw[:, :, :], dram["ctx"]).then_inc(ld_ctx, 16)
                sp.dma_start(b0_col[:, :], dram["b0_col"]).then_inc(ld_b, 16)
                sp.dma_start(b1_row[:, :], dram["b1"].broadcast_to([P, D])).then_inc(ld_b, 16)
                for b in range(1, B):
                    sp.dma_start(X[:, TB * b:TB * b + TB, :], dram["x"][b]).then_inc(ld_x[b], 16)
                for j in range(2):
                    sp.dma_start(att[:, j, :], dram["att0"][j:j + 1, :].broadcast_to([P, D])).then_inc(ld_att0, 16)
                load_expert(sp, outer["route"], dram, 0)
                sp.wait_ge(att_free, 1)
                for j in range(2):
                    sp.dma_start(att[:, j, :], dram["att1"][j:j + 1, :].broadcast_to([P, D])).then_inc(ld_att1, 16)

            @block.gpsimd
            def _(pool):
                pool.memset(ident[:, :], 0.0).then_inc(pool_const, 1)
                pool.memset(negh[:, :], -0.5).then_inc(pool_const, 1)
                pool.wait_ge(pool_const, 2)
                pool.affine_select(out=ident[:, :], in_=ident[:, :], compare_op=ALU.not_equal, fill=1.0, base=0,
                                   pattern=[[-1, P]], channel_multiplier=1).then_inc(pool_const, 1)

                def rstd_of(b):
                    pool.wait_ge(var_ready, b + 1)
                    s = slice(TB * b, TB * b + TB)
                    pool.tensor_tensor(rstd[:, s], ve[:, s], negh[:, 0:TB], ALU.pow).then_inc(rstd_ready, 1)

                def layer1_sum(b, fc):
                    j = DC * b + fc
                    pool.wait_ge(h_exp1, j + 1)
                    if j >= 2:
                        pool.wait_ge(h_lo_done, j - 1)
                    pool.tensor_tensor(hbuf[:, j % 2, :], ebuf[:, j % 2, :], rbuf[:, j % 2, :],
                                       ALU.add).then_inc(h_sum, 1)

                def add_x(b, i):
                    t = TB * b + i
                    pool.wait_ge(y_ready, t + 1)
                    pool.tensor_tensor(X[:, t, :], X[:, t, :], zbuf[:, t % 2, :], ALU.add).then_inc(x_added, 1)

                rstd_of(0)
                pool.wait_ge(w_hi_done, 1)
                pool.tensor_tensor(w_lo[:, :, :], w_raw[:, :, :], w_hi[:, :, :].bitcast(F32),
                                   ALU.subtract).then_inc(w_lo_done, 1)
                for new, old in steps:
                    if new is not None and new + 1 < B:
                        rstd_of(new + 1)
                    for k in range(TB + 1):
                        if new is not None and k < TB:
                            layer1_sum(new, k)
                        if old is not None and k >= 1:
                            add_x(old, k - 1)

            @block.tensor
            def _(pe):
                pe.wait_ge(pool_const, 3)

                def turn_hot(b, i):
                    t = TB * b + i
                    pe.wait_ge(hot_ready, t + 1)
                    if t >= 2:
                        pe.wait_ge(pick_done, t - 1)
                    for m in range(TB):
                        ins = pe.transpose(TBANK[t % 2][:, P * m:P * m + P], adj[:, t % 2, P * m:P * m + P],
                                           ident[:, :])
                    ins.then_inc(turned, 1)

                def context_rows(b):
                    if b == 0:
                        pe.wait_ge(ctx_lo_done, 1)
                    pe.wait_ge(pick_done, TB * (b + 1))
                    if b >= 1:
                        pe.wait_ge(g_lo_done, b)
                    for m in range(TB):
                        pe.matmul(GBANK, ctx_lo[:, TB * b + m, :], pick[:, b % 2, m, :], start=(m == 0), stop=False)
                        ins = pe.matmul(GBANK, ctx_hi[:, TB * b + m, :], pick[:, b % 2, m, :], start=False,
                                        stop=(m == TB - 1))
                    ins.then_inc(g_done, 1)

                def hidden(b, fc):
                    if fc == 0:
                        pe.wait_ge(g_lo_done, b + 1)
                    if b == 0:
                        pe.wait_ge(w_lo_done, 1)
                    j = DC * b + fc
                    if j >= 2:
                        pe.wait_ge(h_act, j - 1)
                    product3(pe, HBANK[j % 2], w_hi[:, 0, P * fc:P * fc + P], w_lo[:, 0, P * fc:P * fc + P],
                             g_hi[:, :], g_lo[:, :], True, True).then_inc(h_done, 1)

                def features(b, m):
                    if m == 0:
                        pe.wait_ge(h_lo_done, DC * (b + 1))
                    u = 2 * TB * b + m
                    if u >= 3:
                        pe.wait_ge(ring_free, u - 2)
                    for d in range(DC):
                        ins = product3(pe, RING[u % 3], h_hi[:, b % 2, d, P * m:P * m + P],
                                       h_lo[:, b % 2, d, P * m:P * m + P], w_hi[:, 1 + d, :], w_lo[:, 1 + d, :],
                                       d == 0, d == DC - 1)
                    ins.then_inc(f_done, 1)

                def picked(b, n):
                    u = 2 * TB * b + TB + n
                    pe.wait_ge(ring_free, max(u - 2, 2 * TB * b + TB))
                    for m in range(TB):
                        lhs = pick[:, b % 2, m, P * n:P * n + P]
                        pe.matmul(RING[u % 3], lhs, f_lo[:, m, :], start=(m == 0), stop=False)
                        ins = pe.matmul(RING[u % 3], lhs, f_hi[:, m, :], start=False, stop=(m == TB - 1))
                    ins.then_inc(o_done, 1)

                for new, old in steps:
                    for k in range(TB + 1):
                        if new is not None:
                            if k == 0:
                                turn_hot(new, 0)
                            if k < TB - 1:
                                turn_hot(new, k + 1)
                            if k == TB - 1:
                                context_rows(new)
                        if old is not None and k < TB:
                            features(old, k)
                    for k in range(TB):
                        if old is not None:
                            picked(old, k)
                        if new is not None:
                            hidden(new, k)
                pe.wait_ge(bounds_ready, 1)
                for j in range(4):
                    ins = pe.transpose(TBANK[0][0:1, P * j:P * j + P], per_part[:, j:j + 1], ident[:, :])
                ins.then_inc(bounds_turned, 1)

            @block.scalar
            def _(act):
                act.wait_ge(ld_w, 16)
                act.copy(w_hi[:, :, :], w_raw[:, :, :]).then_inc(w_hi_done, 1)
                act.wait_ge(ld_ctx, 16)
                act.copy(ctx_hi[:, :, :], ctx_raw[:, :, :]).then_inc(ctx_hi_done, 1)

                def bound_part(layer):
                    act.wait_ge([ld_att0, ld_att1][layer], 32)
                    act.activation(att[:, :, :], att[:, :, :], ACT.Abs).then_inc(att_abs, 1)

                def pick_of(b, i):
                    t = TB * b + i
                    act.wait_ge(turned, t + 1)
                    if b >= 2 and i == 0:
                        act.wait_ge(o_done, TB * (b - 1))
                    act.copy(pick[:, b % 2, :, P * i:P * i + P],
                             TBANK[t % 2].rearrange("p (m n) -> p m n", m=TB)).then_inc(pick_done, 1)

                def g_hi_of(b):
                    act.wait_ge(g_done, b + 1)
                    act.copy(g_hi[:, :], GBANK).then_inc(g_hi_done, 1)

                def elu_parts(b, fc):
                    j = DC * b + fc
                    act.wait_ge(h_done, j + 1)
                    if j >= 2:
                        act.wait_ge(h_sum, j - 1)
                    act.activation(ebuf[:, j % 2, :], HBANK[j % 2], ACT.Exp, bias=b0_col[:, fc:fc + 1])
                    act.activation(rbuf[:, j % 2, :], HBANK[j % 2], ACT.Relu, bias=b0_col[:, fc:fc + 1]).then_inc(h_act, 1)

                def h_hi_of(b, fc):
                    j = DC * b + fc
                    act.wait_ge(h_sum, j + 1)
                    act.copy(h_hi[:, b % 2, fc, :], hbuf[:, j % 2, :]).then_inc(h_hi_done, 1)

                def f_hi_of(b, m):
                    act.wait_ge(f_done, TB * b + m + 1)
                    act.copy(f_hi[:, m, :], RING[(2 * TB * b + m) % 3]).then_inc(f_hi_done, 1)

                def z_exp_of(b, n):
                    t = TB * b + n
                    act.wait_ge(ring_free, 2 * TB * b + TB + n + 1)
                    act.activation(zexp[:, t % 2, :], zbuf[:, t % 2, :], ACT.Exp).then_inc(z_exp, 1)

                act.wait_ge(ld_b, 32)
                for new, old in steps:
                    for k in range(TB):
                        if new is not None:
                            if k == 0:
                                pick_of(new, 0)
                            if k < TB - 1:
                                pick_of(new, k + 1)
                            if k == TB - 1:
                                g_hi_of(new)
                        if old is not None:
                            f_hi_of(old, k)
                    for k in range(TB + 1):
                        if new is not None and k < TB:
                            elu_parts(new, k)
                        if old is not None and k < TB:
                            z_exp_of(old, k)
                        if new is not None and k >= 1:
                            h_hi_of(new, k - 1)
                    if new in (0, 1):
                        bound_part(new)

            @block.vector
            def _(dve):
                chain = Chain(dve, dve_chain)
                dve.wait_ge(pool_const, 3)

                def norm_stats(b):
                    dve.wait_ge(ld_x[b], 16)
                    for i in range(TB):
                        ins = dve.bn_stats(stats[:, i, :], X[:, TB * b + i, :])
                    chain.link(ins)
                    for i in range(TB):
                        ins = dve.bn_aggr(mv[:, TB * b + i, :], stats[:, i, :])
                    chain.link(ins)
                    dve.tensor_scalar(ve[:, TB * b:TB * b + TB], mv[:, TB * b:TB * b + TB, 1], EPS, None,
                                      ALU.add).then_inc(var_ready, 1)

                def one_hot(t):
                    if t % TB == 0:
                        dve.wait_ge(rstd_ready, t // TB + 1)
                    if t >= 2:
                        dve.wait_ge(turned, t - 1)
                    a = adj[:, t % 2, :]
                    chain.link(dve.tensor_scalar(a, X[:, t, :], mv[:, t, 0:1], rstd[:, t:t + 1], ALU.subtract,
                                                 ALU.mult))
                    chain.link(dve.tensor_scalar(a, a, -1.0, None, ALU.add))
                    chain.link(dve.max(top[:, t, :], a))
                    dve.tensor_scalar(a, a, top[:, t, 0:1], None, ALU.is_ge).then_inc(hot_ready, 1)

                def split_ctx():
                    dve.wait_ge(ctx_hi_done, 1)
                    dve.tensor_tensor(ctx_lo[:, :, :], ctx_raw[:, :, :], ctx_hi[:, :, :].bitcast(F32),
                                      ALU.subtract).then_inc(ctx_lo_done, 1)
                    chain.link(dve.tensor_reduce(csum[:, :], ctx_raw[:, :, :], AX.X, ALU.add,
                                                 apply_absolute_value=True))

                def bound_part(layer):
                    dve.wait_ge(att_abs, layer + 1)
                    chain.link(dve.tensor_tensor(att[:, 0, :], att[:, 0, :], att[:, 1, :], ALU.add))
                    if layer == 0:
                        dve.wait_ge(w_lo_done, 1)
                    for k in ([0] if layer == 0 else range(1, 1 + DC)):
                        ins = dve.tensor_tensor(w_raw[:, k, :], w_raw[:, k, :], att[:, 0, :], ALU.mult)
                    chain.link(ins)
                    s = slice(0, 1) if layer == 0 else slice(1, 1 + DC)
                    chain.link(dve.tensor_reduce(wsum[:, s, :],
                                                 w_raw[:, s, :].rearrange("p k (h o) -> p k h o", h=H), AX.X, ALU.add,
                                                 apply_absolute_value=True))
                    if layer == 0:
                        dve.tensor_reduce(wmax[:, s], wsum[:, s, :], AX.X, ALU.max).then_inc(att_free, 1)
                    else:
                        dve.tensor_reduce(wmax[:, s], wsum[:, s, :], AX.X, ALU.max)

                def g_lo_of(b):
                    dve.wait_ge(g_hi_done, b + 1)
                    dve.tensor_tensor(g_lo[:, :], GBANK, g_hi[:, :].bitcast(F32), ALU.subtract).then_inc(g_lo_done, 1)

                def exp_less_1(b, fc):
                    j = DC * b + fc
                    dve.wait_ge(h_act, j + 1)
                    dve.tensor_reduce(hmax[:, j:j + 1], rbuf[:, j % 2, :], AX.X, ALU.max)
                    dve.tensor_scalar(ebuf[:, j % 2, :], ebuf[:, j % 2, :], 1.0, -1.0, ALU.min,
                                      ALU.add).then_inc(h_exp1, 1)

                def h_lo_of(b, fc):
                    j = DC * b + fc
                    dve.wait_ge(h_hi_done, j + 1)
                    dve.tensor_tensor(h_lo[:, b % 2, fc, :], hbuf[:, j % 2, :], h_hi[:, b % 2, fc, :].bitcast(F32),
                                      ALU.subtract).then_inc(h_lo_done, 1)

                def f_lo_of(b, m):
                    dve.wait_ge(f_hi_done, TB * b + m + 1)
                    dve.tensor_tensor(f_lo[:, m, :], RING[(2 * TB * b + m) % 3], f_hi[:, m, :].bitcast(F32),
                                      ALU.subtract).then_inc(ring_free, 1)

                def z_of(b, n):
                    t = TB * b + n
                    dve.wait_ge(o_done, t + 1)
                    if t >= 2:
                        dve.wait_ge(x_added, t - 1)
                    dve.tensor_tensor(zbuf[:, t % 2, :], RING[(2 * TB * b + TB + n) % 3], b1_row[:, :],
                                      ALU.add).then_inc(ring_free, 1)

                def elu_z(b, n):
                    k = (TB * b + n) % 2
                    dve.wait_ge(z_exp, TB * b + n + 1)
                    chain.link(dve.tensor_scalar(zexp[:, k, :], zexp[:, k, :], 1.0, -1.0, ALU.min, ALU.add))
                    dve.scalar_tensor_tensor(out=zbuf[:, k, :], in0=zbuf[:, k, :], scalar=0.0,
                                             in1=zexp[:, k, :], op0=ALU.max, op1=ALU.add).then_inc(y_ready, 1)

                norm_stats(0)
                one_hot(0)
                one_hot(1)
                for new, old in steps:
                    for k in range(TB):
                        if new is not None:
                            if k < 2:
                                one_hot(TB * new + k + 2)
                            if k == 0 and new == 0:
                                split_ctx()
                            if k == 2 and new + 1 < B:
                                norm_stats(new + 1)
                            if k == TB - 1:
                                g_lo_of(new)
                        if old is not None:
                            f_lo_of(old, k)
                    for k in range(TB + 1):
                        if old is not None and k < TB:
                            z_of(old, k)
                        if new is not None and k < TB:
                            exp_less_1(new, k)
                        if old is not None and k >= 1:
                            elu_z(old, k - 1)
                        if new is not None and k >= 1:
                            h_lo_of(new, k - 1)
                        if new is not None and new + 1 < B and k in (1, 2):
                            one_hot(TB * (new + 1) + k - 1)
                    if new in (0, 1):
                        bound_part(new)

                chain.link(dve.tensor_scalar(tops[:, :, :], top[:, :, 0:2], MASK, None, ALU.mult))
                chain.link(dve.tensor_tensor(gap[:, :], tops[:, :, 0], tops[:, :, 1], ALU.subtract))
                chain.link(dve.tensor_scalar(gap[:, :], gap[:, :], GAP_MIN, None, ALU.is_ge))
                chain.link(dve.tensor_reduce(per_part[:, 0:1], gap[:, :], AX.X, ALU.min))
                chain.link(dve.tensor_reduce(per_part[:, 1:2], csum[:, :], AX.X, ALU.max))
                chain.link(dve.tensor_copy(per_part[:, 2:3], wmax[:, 0:1]))
                chain.link(dve.tensor_reduce(hcol[:, :], hmax[:, :].rearrange("p (b f) -> p f b", b=B), AX.X, ALU.max))
                chain.link(dve.tensor_scalar(hcol[:, :], hcol[:, :], 1.0, None, ALU.max))
                chain.link(dve.tensor_tensor(hw[:, :], hcol[:, :], wmax[:, 1:1 + DC], ALU.mult))
                dve.tensor_reduce(per_part[:, 3:4], hw[:, :], AX.X, ALU.add).then_inc(bounds_ready, 1)
                dve.wait_ge(bounds_turned, 1)
                row = TBANK[0]
                dve.tensor_reduce(red[:, 0:1], row[0:1, 0:P], AX.X, ALU.min)
                dve.tensor_reduce(red[:, 1:2], row[0:1, P:2 * P], AX.X, ALU.max)
                dve.tensor_reduce(red[:, 2:3], row[0:1, 2 * P:3 * P], AX.X, ALU.max)
                chain.link(dve.tensor_reduce(red[:, 3:4], row[0:1, 3 * P:4 * P], AX.X, ALU.add))
                chain.link(dve.tensor_tensor(red[:, 4:5], red[:, 1:2], red[:, 2:3], ALU.mult))
                chain.link(dve.tensor_scalar(red[:, 5:7], red[:, 3:5], BOUND_MAX, None, ALU.is_le))
                chain.link(dve.tensor_tensor(red[:, 5:6], red[:, 5:6], red[:, 6:7], ALU.mult))
                chain.link(dve.tensor_tensor(red[:, 5:6], red[:, 5:6], red[:, 0:1], ALU.mult))
                dve.tensor_copy(flag[:, :], red[:, 5:6])



class LoopChain:

    def __init__(self, eng, sem, per, turn):
        self.eng, self.sem, self.per, self.turn, self.n = eng, sem, per, turn, 0

    def link(self, ins):
        self.n += 1
        ins.then_inc(self.sem, 1)
        self.eng.wait_ge(self.sem, self.per * self.turn + self.n)

    def end(self):
        assert self.n == self.per, self.n


def gat_general(nc, outer, dram):
    X, ident, negh, ps = (outer[k] for k in ("X", "ident", "negh", "ps"))
    with ExitStack() as ctx:
        def sb(name, shape, dt=F32):
            return ctx.enter_context(nc.sbuf_tensor("gg_" + name, shape, dt))

        sems = []

        def sem(name):
            sems.append(nc.alloc_semaphore(name="gg_" + name))
            return sems[-1]

        cT = sb("ctxT", [P, 1, B * N])
        hT = sb("hT", [P, DC, B * N])
        w = sb("w", [P, 1 + DC, D])
        att = sb("att", [P, 2, 2, D])
        bias = sb("bias", [P, 2, D])
        pick_head = sb("pick_head", [H, H, P])
        lhs = sb("lhs", [P, DC, P])
        feat = sb("feat", [P, T, D])
        tmp = sb("tmp", [P, D])
        s_self = sb("s_self", [P, T, H])
        s_neigh = sb("s_neigh", [P, H])
        nT = sb("nT", [H, B * N])
        nTb = sb("nTb", [H, N])
        neigh = sb("neigh", [P, H, N])
        mv = sb("mv", [P, T, 2])
        st = sb("st", [P, 6])
        rstd = sb("rstd", [P, T])
        mask = sb("mask", [P, N])
        sc = sb("sc", [P, N])
        al = sb("al", [P, N])
        alT = sb("alT", [P, TB, P])
        nmax = sb("nmax", [P, 1])
        den = sb("den", [P, 1])
        z = sb("z", [P, D])
        ez = sb("ez", [P, D])

        ld, ld_x = sem("ld"), sem("ld_x")
        head_const, var_ready, rstd_ready, chain0 = sem("head_const"), sem("var_ready"), sem("rstd_ready"), sem("chain0")
        L = [{k: sem(f"{k}{layer}") for k in
              ("lhs_ready", "feat_done", "neigh_ready", "neigh_turned", "nT_ready", "spread", "spread_read",
               "sc_ready", "al_ready", "al_turned", "alT_ready", "mixed", "z_ready", "ez_ready", "y_ready", "y_turned",
               "chain_f", "chain_h", "chain_m", "chain_z", "mask_ready")} for layer in range(2)]

        with nc.Block() as block:
            @block.sync
            def _(sp):
                sp.dma_start(X[:, :, :].rearrange("p (b i) n -> p b i n", b=B),
                             dram["x"].rearrange("b p i n -> p b i n")).then_inc(ld_x, 16)
                sp.dma_start(cT[:, 0, :], dram["ctxT"]).then_inc(ld, 16)
                sp.dma_start(w[:, :, :], dram["gat_w"]).then_inc(ld, 16)
                for layer in range(2):
                    for j in range(2):
                        sp.dma_start(att[:, layer, j, :], dram[f"att{layer}"][j:j + 1, :].broadcast_to([P, D])
                                     ).then_inc(ld, 16)
                    sp.dma_start(bias[:, layer, :], dram[f"b{layer}"].broadcast_to([P, D])).then_inc(ld, 16)

            @block.gpsimd
            def _(pool):
                pool.memset(pick_head[:, :, :], 0.0).then_inc(head_const, 1)
                pool.wait_ge(head_const, 1)
                pool.affine_select(out=pick_head[:, :, :], in_=pick_head[:, :, :], compare_op=ALU.not_equal, fill=1.0,
                                   base=0, pattern=[[-1, H], [0, P]], channel_multiplier=1).then_inc(head_const, 1)
                pool.wait_ge(var_ready, 1)
                for c in range(B):
                    s = slice(TB * c, TB * c + TB)
                    pool.tensor_tensor(rstd[:, s], rstd[:, s], negh[:, 0:TB], ALU.pow).then_inc(rstd_ready, 1)

            @block.tensor
            def _(pe):
                pe.wait_ge(ld, 16 * 8)
                pe.wait_ge(head_const, 2)
                for layer in range(2):
                    q = L[layer]
                    first, chunks = (0, 1) if layer == 0 else (1, DC)
                    with pe.Fori(0, T) as t:
                        pe.wait_ge(q["lhs_ready"], t + 1)
                        for k in range(chunks):
                            ins = pe.matmul(ps[:, 0, :], lhs[:, k, :], w[:, first + k, :], start=(k == 0),
                                            stop=(k == chunks - 1))
                        ins.then_inc(q["feat_done"], 1)
                        pe.wait_ge(q["neigh_ready"], t + 1)
                        pe.transpose(ps[0:H, 1, 0:P], s_neigh[:, :], ident[:, :]).then_inc(q["neigh_turned"], 1)
                    with pe.Fori(0, B) as b:
                        for h in range(H):
                            pe.wait_ge(q["nT_ready"], H * b + (h + 1))
                            pe.matmul(ps[:, 2, :], pick_head[:, h, :], nTb[:, :], start=True, stop=True).then_inc(q["spread"], 1)
                        with pe.Fori(0, TB) as i:
                            with pe.Fori(0, H) as h:
                                n = (b * TB + i) * H + h
                                pe.wait_ge(q["al_ready"], n + 1)
                                for m in range(TB):
                                    ins = pe.transpose(ps[:, 3, P * m:P * m + P], al[:, P * m:P * m + P], ident[:, :])
                                ins.then_inc(q["al_turned"], 1)
                                pe.wait_ge(q["alT_ready"], n + 1)
                                for m in range(TB):
                                    ins = pe.matmul(ps[:, 4, 0:FO], alT[:, m, :],
                                                    feat[:, bass.ds(b * TB + m, 1), bass.ds(h * FO, FO)],
                                                    start=(m == 0), stop=(m == TB - 1))
                                ins.then_inc(q["mixed"], 1)
                            if layer == 0:
                                pe.wait_ge(q["y_ready"], b * TB + i + 1)
                                for m in range(DC):
                                    ins = pe.transpose(ps[:, 5, P * m:P * m + P], z[:, P * m:P * m + P], ident[:, :])
                                ins.then_inc(q["y_turned"], 1)

            @block.scalar
            def _(act):
                for layer in range(2):
                    q = L[layer]
                    with act.Fori(0, T) as t:
                        with act.Fori(0, H) as h:
                            n = t * H + h
                            act.wait_ge(q["sc_ready"], n + 1)
                            act.activation(al[:, :], sc[:, :], ACT.Exp, bias=nmax[:, 0:1],
                                           accum_out=den[:, 0:1]).then_inc(q["al_ready"], 1)
                        act.wait_ge(q["z_ready"], t + 1)
                        act.activation(ez[:, :], ez[:, :], ACT.Exp).then_inc(q["ez_ready"], 1)

            @block.vector
            def _(dve):
                chain = Chain(dve, chain0)
                dve.wait_ge(ld_x, 16)
                dve.wait_ge(ld, 16 * 8)
                for t in range(T):
                    chain.link(dve.bn_stats(st[:, :], X[:, t, :]))
                    chain.link(dve.bn_aggr(mv[:, t, :], st[:, :]))
                dve.tensor_scalar(rstd[:, :], mv[:, :, 1], EPS, None, ALU.add).then_inc(var_ready, 1)
                dve.wait_ge(rstd_ready, B)
                for layer in range(2):
                    q = L[layer]
                    src, chunks = (cT, 1) if layer == 0 else (hT, DC)
                    with dve.Fori(0, T) as t:
                        lc = LoopChain(dve, q["chain_f"], 6, t)
                        dve.tensor_copy(lhs[:, 0:chunks, :], src[:, :, bass.ds(t * P, P)]).then_inc(q["lhs_ready"], 1)
                        dve.wait_ge(q["feat_done"], t + 1)
                        lc.link(dve.tensor_copy(feat[:, bass.ds(t, 1), :], ps[:, 0:1, :]))
                        lc.link(dve.tensor_tensor(tmp[:, :], ps[:, 0, :], att[:, layer, 0, :], ALU.mult))
                        lc.link(dve.tensor_reduce(s_self[:, bass.ds(t, 1), :], tmp[:, :].rearrange("p (h o) -> p h o", h=H),
                                                  AX.X, ALU.add))
                        lc.link(dve.tensor_tensor(tmp[:, :], ps[:, 0, :], att[:, layer, 1, :], ALU.mult))
                        lc.link(dve.tensor_reduce(s_neigh[:, :], tmp[:, :].rearrange("p (h o) -> p h o", h=H), AX.X,
                                                  ALU.add))
                        dve.sem_inc(q["neigh_ready"], 1)
                        dve.wait_ge(q["neigh_turned"], t + 1)
                        lc.link(dve.tensor_copy(nT[:, bass.ds(t * P, P)], ps[0:H, 1, 0:P]))
                        lc.end()
                    with dve.Fori(0, B) as b:
                        dve.tensor_copy(nTb[:, :], nT[:, bass.ds(b * N, N)]).then_inc(q["nT_ready"], 1)
                        for h in range(H):
                            dve.wait_ge(q["spread"], H * b + (h + 1))
                            ins = dve.tensor_copy(neigh[:, h, :], ps[:, 2, :])
                            ins.then_inc(*((q["nT_ready"], 1) if h + 1 < H else (q["spread_read"], 1)))
                        with dve.Fori(0, TB) as i:
                            t = b * TB + i
                            dve.wait_ge(q["spread_read"], b + 1)
                            lc = LoopChain(dve, q["chain_m"], 2, t)
                            lc.link(dve.tensor_scalar(mask[:, :], X[:, bass.ds(t, 1), :], mv[:, bass.ds(t, 1), 0],
                                                      rstd[:, bass.ds(t, 1)], ALU.subtract, ALU.mult))
                            lc.link(dve.tensor_scalar(mask[:, :], mask[:, :], -1.0, None, ALU.add))
                            dve.tensor_scalar(mask[:, :], mask[:, :], MASK, None, ALU.mult).then_inc(q["mask_ready"], 1)
                            lc.end()
                            with dve.Fori(0, H) as h:
                                n = t * H + h
                                dve.wait_ge(q["mask_ready"], t + 1)
                                lc = LoopChain(dve, q["chain_h"], 6, n)
                                lc.link(dve.tensor_scalar(sc[:, :], neigh[:, bass.ds(h, 1), :],
                                                          s_self[:, bass.ds(t, 1), bass.ds(h, 1)], None, ALU.add))
                                lc.link(dve.scalar_tensor_tensor(out=sc[:, :], in0=sc[:, :], scalar=SLOPE, in1=sc[:, :],
                                                                 op0=ALU.mult, op1=ALU.max))
                                lc.link(dve.tensor_tensor(sc[:, :], sc[:, :], mask[:, :], ALU.add))
                                dve.tensor_reduce(nmax[:, 0:1], sc[:, :], AX.X, ALU.max,
                                                  negate=True).then_inc(q["sc_ready"], 1)
                                dve.wait_ge(q["al_turned"], n + 1)
                                dve.tensor_copy(alT[:, :, :], ps[:, 3, :].rearrange("p (m n) -> p m n", m=TB)
                                                ).then_inc(q["alT_ready"], 1)
                                lc.link(dve.reciprocal(den[:, :], den[:, :]))
                                dve.wait_ge(q["mixed"], n + 1)
                                lc.link(dve.tensor_scalar(z[:, bass.ds(h * FO, FO)], ps[:, 4, 0:FO], den[:, 0:1], None,
                                                          ALU.mult))
                                lc.link(dve.tensor_copy(tmp[:, 0:1], den[:, 0:1]))
                                lc.end()
                            lc = LoopChain(dve, q["chain_z"], 3 if layer == 0 else 4, t)
                            lc.link(dve.tensor_tensor(z[:, :], z[:, :], bias[:, layer, :], ALU.add))
                            dve.tensor_scalar(ez[:, :], z[:, :], 0.0, None, ALU.min).then_inc(q["z_ready"], 1)
                            dve.wait_ge(q["ez_ready"], t + 1)
                            lc.link(dve.tensor_scalar(ez[:, :], ez[:, :], -1.0, None, ALU.add))
                            if layer == 0:
                                dve.scalar_tensor_tensor(out=z[:, :], in0=z[:, :], scalar=0.0, in1=ez[:, :],
                                                         op0=ALU.max, op1=ALU.add).then_inc(q["y_ready"], 1)
                                dve.wait_ge(q["y_turned"], t + 1)
                                lc.link(dve.tensor_copy(hT[:, :, bass.ds(t * P, P)],
                                                        ps[:, 5, :].rearrange("p (m n) -> p m n", m=DC)))
                            else:
                                lc.link(dve.scalar_tensor_tensor(out=z[:, :], in0=z[:, :], scalar=0.0, in1=ez[:, :],
                                                                 op0=ALU.max, op1=ALU.add))
                                lc.link(dve.tensor_tensor(X[:, bass.ds(t, 1), :], X[:, bass.ds(t, 1), :], z[:, :], ALU.add))
                            lc.end()
        nc.clear_and_free_semaphores(sems)
        nc.all_engine_barrier()


class Units:

    def __init__(self, tag, outer, U, R, slots, w_hi, w_lo, x_hi, x_lo, hid_hi, hid_lo, los):
        ps = outer["ps"]
        self.U, self.R, self.slots, self.los = U, R, slots, los
        self.w_hi, self.w_lo, self.x_hi, self.x_lo, self.hid_hi, self.hid_lo = w_hi, w_lo, x_hi, x_lo, hid_hi, hid_lo
        self.raw_gu, self.raw_dn, self.ld_gu, self.ld_dn = (outer[k] for k in ("raw_gu", "raw_dn", "ld_gu", "ld_dn"))
        self.GATE = [ps[:, 0, :], ps[:, 1, :]]
        self.UP = [ps[:, 2, :], ps[:, 3, :]]
        self.ACC = [ps[:, 4 + i, :] for i in range(TB)]
        sem = outer["sem"]
        self.gate_up_hi, self.gate_up_lo = sem(tag + "gate_up_hi"), sem(tag + "gate_up_lo")
        self.down_hi, self.down_lo = sem(tag + "down_hi"), sem(tag + "down_lo")
        self.products = sem(tag + "products")
        self.silu, self.hid_made = sem(tag + "silu"), sem(tag + "hid_made")
        self.hid_hi_done, self.hid_lo_done = sem(tag + "hid_hi_done"), sem(tag + "hid_lo_done")
        self.acc_done, self.acc_free = sem(tag + "acc_done"), sem(tag + "acc_free")

    def at(self, u, c, r):
        return self.R * 4 * u + (self.R * c + r)

    def bank(self, c, r):
        return (self.R * c + r) % 2


    def load_gate_up(self, sp, src, u, r):
        sp.wait_ge(self.gate_up_lo, self.R * u + (r - self.slots + 1))
        sp.dma_start(self.raw_gu[:, r % self.slots, :, :],
                     src[bass.ds(self.R * u + r, 1)].rearrange("o p k n -> (o p) k n")
                     ).then_inc(self.ld_gu[r % self.slots], 16)

    def load_down(self, sp, src, u, r):
        sp.wait_ge(self.down_lo, self.R * u + (r - self.R + 1))
        sp.dma_start(self.raw_dn[:, r, :], src[bass.ds(self.R * u + r, 1)].rearrange("o p n -> (o p) n")
                     ).then_inc(self.ld_dn[r], 16)


    def act_gate_up(self, act, u, r, first=False):
        uses = self.R // self.slots
        act.wait_ge(self.ld_gu[r % self.slots], 16 * uses * u + 16 * (r // self.slots + 1))
        if not first:
            act.wait_ge(self.products, self.at(u - 1, 3, r) + 1)
        act.copy(self.w_hi[:, r, 0:2, :], self.raw_gu[:, r % self.slots, :, :]).then_inc(self.gate_up_hi, 1)

    def act_down(self, act, u, r, first=False):
        act.wait_ge(self.ld_dn[r], 16 * u + 16)
        if not first:
            act.wait_ge(self.acc_done, 16 * u)
        act.copy(self.w_hi[:, r, 2, :], self.raw_dn[:, r, :]).then_inc(self.down_hi, 1)

    def pool_gate_up(self, pool, u, r):
        pool.wait_ge(self.gate_up_hi, self.R * u + (r + 1))
        pool.tensor_tensor(self.w_lo[:, r, 0:2, :], self.raw_gu[:, r % self.slots, :, :],
                           self.w_hi[:, r, 0:2, :].bitcast(F32), ALU.subtract).then_inc(self.gate_up_lo, 1)

    def pool_down(self, pool, u, r):
        pool.wait_ge(self.down_hi, self.R * u + (r + 1))
        pool.tensor_tensor(self.w_lo[:, r, 2, :], self.raw_dn[:, r, :], self.w_hi[:, r, 2, :].bitcast(F32),
                           ALU.subtract).then_inc(self.down_lo, 1)


    def pe_gate_up(self, pe, u, c, first=False, between=None):
        s = slice(N * c, N * c + N)
        for r in range(self.R):
            if c == 0:
                pe.wait_ge(self.gate_up_lo, self.R * u + (r + 1))
            if not (first and r < 2):
                pe.wait_ge(self.hid_made, self.at(u, c, r) - 1)
            for k, bank in ((0, self.GATE), (1, self.UP)):
                for d in range(DC):
                    w = slice(P * d, P * d + P)
                    ins = product3(pe, bank[self.bank(c, r)], self.w_hi[:, r, k, w], self.w_lo[:, r, k, w],
                                   self.x_hi[:, d, s], self.x_lo[:, d, s], d == 0, d == DC - 1)
                if k == 1:
                    ins.then_inc(self.products, 1)
                if between:
                    between()

    def pe_down(self, pe, u, c):
        pe.wait_ge(self.hid_lo_done, 4 * self.los * u + self.los * (c + 1))
        if c == 0:
            pe.wait_ge(self.down_lo, self.R * u + self.R)
        h = c % self.hid_hi.shape[1]
        for i in range(TB):
            pe.wait_ge(self.acc_free, 16 * u + (4 * c + i + 1))
            s = slice(P * i, P * i + P)
            for r in range(self.R):
                ins = product3(pe, self.ACC[i], self.hid_hi[:, h, r, s], self.hid_lo[:, h, r, s],
                               self.w_hi[:, r, 2, :], self.w_lo[:, r, 2, :], r == 0, r == self.R - 1)
            ins.then_inc(self.acc_done, 1)

    def pe_rest(self, pe):
        with pe.Fori(0, self.U - 1) as u:
            for c in range(4):
                self.pe_gate_up(pe, *((u, c + 1) if c < 3 else (u + 1, 0)))
                self.pe_down(pe, u, c)
        for c in range(4):
            if c < 3:
                self.pe_gate_up(pe, self.U - 1, c + 1)
            self.pe_down(pe, self.U - 1, c)


    def act_silu(self, act, u, c, r, sg, first=False):
        act.wait_ge(self.products, self.at(u, c, r) + 1)
        if not (first and r < 2):
            act.wait_ge(self.hid_made, self.at(u, c, r) - 1)
        k = self.bank(c, r)
        act.activation(sg[:, k, :], self.GATE[k], ACT.Silu).then_inc(self.silu, 1)

    def dve_hid(self, dve, u, c, r, sg, out):
        dve.wait_ge(self.silu, self.at(u, c, r) + 1)
        k = self.bank(c, r)
        dve.tensor_tensor(out, sg[:, k, :], self.UP[k], ALU.mult).then_inc(self.hid_made, 1)

    def dve_wait_acc(self, dve, u, c, i):
        dve.wait_ge(self.acc_done, 16 * u + (4 * c + i + 1))


def route(nc, outer, dram):
    X, ident, negh, ps, sem, rt = (outer[k] for k in ("X", "ident", "negh", "ps", "sem", "route"))
    J = 2 * T
    XN = 4
    with ExitStack() as ctx:
        def sb(name, shape, dt=F32):
            return ctx.enter_context(nc.sbuf_tensor("r_" + name, shape, dt))

        x_hi = sb("x_hi", [P, DC, N], F32R)
        x_lo = sb("x_lo", [P, DC, N], F32R)
        gw_raw = sb("gw_raw", [P, DC, E])
        gw_hi = sb("gw_hi", [P, DC, E], F32R)
        gw_lo = sb("gw_lo", [P, DC, E], F32R)
        lgT = sb("lgT", [E, B * N])
        lg = sb("lg", [P, T, E])
        lmax = sb("lmax", [P, T])
        ex = sb("ex", [P, T, E])
        gt = sb("gt", [P, T, E, E])
        eq = sb("eq", [P, T, E, E])
        before_e = sb("before_e", [P, E, E])
        rank = sb("rank", [P, T, E])
        keep = sb("keep", [P, T, E])
        den = sb("den", [P, T])
        tw = sb("tw", [P, T, E])
        before_p = sb("before_p", [P, P])
        ones = sb("ones", [P, P])
        totals = sb("totals", [P, T, E])
        cum = sb("cum", [P, 2, T, E])
        steps = sb("steps", [P, T])
        above = sb("above", [P, E, T])
        blocks = sb("blocks", [P, E])
        cumb = sb("cumb", [P, 2, E])
        start = sb("start", [P, E])
        pos = sb("pos", [P, T, E])
        low = sb("low", [P, T, E])
        high = sb("high", [P, T, E])
        pos2 = sb("pos2", [P, T, 2])
        at2 = sb("at2", [P, 2, J], I32)
        at2f = sb("at2f", [P, 2, J])
        iota_i = sb("iota_i", [P, P], I32)
        iota_f = sb("iota_f", [P, P])
        tok_i = sb("tok_i", [P, T], I32)
        tok_f = sb("tok_f", [P, T])
        off_hot = sb("off_hot", [P, J, P])
        blk_hot = sb("blk_hot", [P, J, REAL])
        tabf = sb("tabf", [1, 3, REAL])
        tcmp = sb("tcmp", [1, REAL, E])
        norm = Norm("r_", sb, sem, X, ident, negh, [ps[:, 0, :], ps[:, 1, :]], XN)
        LG, LT, PRE, TOT, IDX = ps[:, 2, :], ps[:, 3, :], ps[:, 4, :], ps[:, 5, :], ps[:, 6, :]

        ld_gw, gw_hi_done, gw_lo_done, const = sem("r_ld_gw"), sem("r_gw_hi_done"), sem("r_gw_lo_done"), sem("r_const")
        lg_done, lgT_done, lt_done, shifted, exped = (
            sem("r_" + n) for n in ("lg_done", "lgT_done", "lt_done", "shifted", "exped"))
        kept, counted, hot, idx_done, dve_chain = (
            sem("r_" + n) for n in ("kept", "counted", "hot", "idx_done", "dve_chain"))
        xn_stored = [sem(f"r_xn_stored{k}") for k in range(XN)]

        with nc.Block() as block:
            @block.sync
            def _(sp):
                sp.dma_start(gw_raw[:, :, :], dram["gate_w"]).then_inc(ld_gw, 16)
                for t in range(T):
                    sp.wait_ge(norm.xn_ready, t + 1)
                    sp.dma_start(rt["xn_dram"][P * t:P * t + P, :], norm.xn[:, t % XN, :]).then_inc(xn_stored[t % XN], 16)
                for k in range(XN):
                    sp.wait_ge(xn_stored[k], 16 * T // XN)

            @block.gpsimd
            def _(pool):
                pool.memset(before_e[:, :, :], 1.0).then_inc(const, 1)
                pool.memset(before_p[:, :], 1.0).then_inc(const, 1)
                pool.memset(ones[:, :], 1.0).then_inc(const, 1)
                pool.iota(iota_i[:, :], [[1, P]], base=0, channel_multiplier=0).then_inc(const, 1)
                pool.iota(tok_i[:, :], [[P, T]], base=0, channel_multiplier=1).then_inc(const, 1)
                pool.wait_ge(const, 5)
                pool.affine_select(out=before_e[:, :, :], in_=before_e[:, :, :], compare_op=ALU.is_gt, fill=0.0, base=0,
                                   pattern=[[1, E], [-1, E]], channel_multiplier=0).then_inc(const, 1)
                pool.affine_select(out=before_p[:, :], in_=before_p[:, :], compare_op=ALU.is_gt, fill=0.0, base=0,
                                   pattern=[[1, P]], channel_multiplier=-1).then_inc(const, 1)
                for c in range(B):
                    norm.pool_rstd(pool, c)
                pool.wait_ge(rt["gu_hi"], DC)
                pool.tensor_tensor(rt["gu_w_lo"][:, 0], rt["raw_gu"], rt["gu_w_hi"][:, 0].bitcast(F32),
                                   ALU.subtract)
                pool.wait_ge(rt["dn_hi"], 1)
                pool.tensor_tensor(rt["dn_w_lo"][:, 0], rt["raw_dn"], rt["dn_w_hi"][:, 0].bitcast(F32),
                                   ALU.subtract)

            @block.tensor
            def _(pe):
                for c in range(B):
                    for i in range(TB):
                        norm.pe_turn(pe, TB * c + i)
                    pe.wait_ge(norm.lo_done, TB * (c + 1))
                    if c == 0:
                        pe.wait_ge(gw_lo_done, 1)
                    if c >= 1:
                        pe.wait_ge(lgT_done, c)
                    for d in range(DC):
                        ins = product3(pe, LG[0:E, :], gw_hi[:, d, :], gw_lo[:, d, :], x_hi[:, d, :], x_lo[:, d, :],
                                       d == 0, d == DC - 1)
                    ins.then_inc(lg_done, 1)
                pe.wait_ge(lgT_done, B)
                for t in range(T):
                    ins = pe.transpose(LT[:, E * t:E * t + E], lgT[:, P * t:P * t + P], ident[0:E, 0:E])
                ins.then_inc(lt_done, 1)
                pe.wait_ge(const, 7)
                pe.wait_ge(kept, 1)
                k = keep[:, :, :].rearrange("p t e -> p (t e)")
                pe.matmul(PRE[:, 0:T * E], before_p[:, :], k, start=True, stop=True)
                pe.matmul(TOT[:, 0:T * E], ones[:, :], k, start=True, stop=True).then_inc(counted, 1)
                pe.wait_ge(hot, 1)
                for j in range(J):
                    ins = pe.matmul(IDX[:, 0:REAL], off_hot[:, j, :], blk_hot[:, j, :], start=(j == 0),
                                    stop=(j == J - 1))
                ins.then_inc(idx_done, 1)

            @block.scalar
            def _(act):
                act.wait_ge(ld_gw, 16)
                act.copy(gw_hi[:, :, :], gw_raw[:, :, :]).then_inc(gw_hi_done, 1)
                for c in range(B):
                    for i in range(TB):
                        if i == 0 and c >= 1:
                            act.wait_ge(lg_done, c)
                        norm.act_hi(act, TB * c + i, x_hi[:, :, P * i:P * i + P])
                    act.wait_ge(lg_done, c + 1)
                    act.copy(lgT[:, N * c:N * c + N], LG[0:E, :]).then_inc(lgT_done, 1)
                    if c == 0:
                        act.wait_ge(rt["ld_gu"], 16 * DC)
                        act.copy(rt["gu_w_hi"][:, 0], rt["raw_gu"]).then_inc(rt["gu_hi"], DC)
                        act.wait_ge(rt["ld_dn"], 16 * RE)
                        act.copy(rt["dn_w_hi"][:, 0], rt["raw_dn"]).then_inc(rt["dn_hi"], 1)
                act.wait_ge(shifted, 1)
                act.activation(ex[:, :, :], lg[:, :, :], ACT.Exp).then_inc(exped, 1)

            @block.vector
            def _(dve):
                chain = Chain(dve, dve_chain)
                link = chain.link

                def per_e(a, shape=(P, T, E)):
                    return a.unsqueeze(2).broadcast_to(list(shape))

                dve.wait_ge(gw_hi_done, 1)
                dve.tensor_tensor(gw_lo[:, :, :], gw_raw[:, :, :], gw_hi[:, :, :].bitcast(F32),
                                  ALU.subtract).then_inc(gw_lo_done, 1)
                norm.dve_stats(chain, 0)
                for c in range(B):
                    if c + 1 < B:
                        norm.dve_stats(chain, c + 1)
                    for i in range(TB + 1):
                        t = TB * c + i
                        if i < TB:
                            if t >= XN:
                                dve.wait_ge(xn_stored[t % XN], 16 * (t // XN))
                            norm.dve_norm(dve, t)
                        if i >= 1:
                            norm.dve_lo(dve, t - 1, x_hi[:, :, P * (i - 1):P * i], x_lo[:, :, P * (i - 1):P * i])
                dve.wait_ge(lt_done, 1)
                link(dve.tensor_copy(lg[:, :, :], LT[:, 0:T * E].rearrange("p (t e) -> p t e", e=E)))
                link(dve.tensor_reduce(lmax[:, :], lg[:, :, :], AX.X, ALU.max))
                of_e = lg[:, :, :].unsqueeze(3).broadcast_to([P, T, E, E])
                of_j = lg[:, :, :].unsqueeze(2).broadcast_to([P, T, E, E])
                dve.tensor_tensor(gt[:, :, :, :], of_j, of_e, ALU.is_gt)
                link(dve.tensor_tensor(eq[:, :, :, :], of_j, of_e, ALU.is_equal))
                dve.tensor_tensor(lg[:, :, :], lg[:, :, :], per_e(lmax[:, :]), ALU.subtract).then_inc(shifted, 1)
                dve.wait_ge(const, 7)
                link(dve.tensor_tensor(eq[:, :, :, :], eq[:, :, :, :],
                                       before_e[:, :, :].unsqueeze(1).broadcast_to([P, T, E, E]), ALU.mult))
                link(dve.tensor_tensor(gt[:, :, :, :], gt[:, :, :, :], eq[:, :, :, :], ALU.add))
                link(dve.tensor_reduce(rank[:, :, :], gt[:, :, :, :], AX.X, ALU.add))
                dve.tensor_scalar(keep[:, :, :], rank[:, :, :], 1.5, None, ALU.is_le).then_inc(kept, 1)
                dve.wait_ge(kept, 1)
                dve.wait_ge(exped, 1)
                link(dve.tensor_tensor(ex[:, :, :], keep[:, :, :], ex[:, :, :], ALU.mult))
                link(dve.tensor_reduce(den[:, :], ex[:, :, :], AX.X, ALU.add))
                link(dve.reciprocal(den[:, :], den[:, :]))
                link(dve.tensor_tensor(tw[:, :, :], ex[:, :, :], per_e(den[:, :]), ALU.mult))
                link(dve.tensor_copy(iota_f[:, :], iota_i[:, :]))
                link(dve.tensor_copy(tok_f[:, :], tok_i[:, :]))
                link(dve.tensor_scalar(steps[:, :], iota_f[:, 0:T], float(P), None, ALU.mult))
                dve.wait_ge(counted, 1)
                link(dve.tensor_copy(totals[:, :, :], TOT[:, 0:T * E].rearrange("p (t e) -> p t e", e=E)))
                link(dve.tensor_copy(cum[:, 0, :, :], totals[:, :, :]))
                k, a = 1, 0
                while k < T:
                    dve.tensor_copy(cum[:, 1 - a, 0:k, :], cum[:, a, 0:k, :])
                    link(dve.tensor_tensor(cum[:, 1 - a, k:T, :], cum[:, a, k:T, :], cum[:, a, 0:T - k, :], ALU.add))
                    k, a = 2 * k, 1 - a
                link(dve.tensor_tensor(above[:, :, :], cum[:, a, T - 1, :].unsqueeze(2).broadcast_to([P, E, T]),
                                       steps[:, :].unsqueeze(1).broadcast_to([P, E, T]), ALU.is_gt))
                link(dve.tensor_reduce(blocks[:, :], above[:, :, :], AX.X, ALU.add))
                link(dve.tensor_scalar(blocks[:, :], blocks[:, :], 1.0, None, ALU.max))
                link(dve.tensor_copy(cumb[:, 0, :], blocks[:, :]))
                k, z = 1, 0
                while k < E:
                    dve.tensor_copy(cumb[:, 1 - z, 0:k], cumb[:, z, 0:k])
                    link(dve.tensor_tensor(cumb[:, 1 - z, k:E], cumb[:, z, k:E], cumb[:, z, 0:E - k], ALU.add))
                    k, z = 2 * k, 1 - z
                link(dve.tensor_tensor(start[:, :], cumb[:, z, :], blocks[:, :], ALU.subtract))
                link(dve.tensor_tensor(pos[:, :, :], cum[:, a, :, :], totals[:, :, :], ALU.subtract))
                link(dve.tensor_tensor(pos[:, :, :], pos[:, :, :], PRE[:, 0:T * E].rearrange("p (t e) -> p t e", e=E),
                                       ALU.add))
                link(dve.tensor_scalar(cumb[:, z, :], start[:, :], float(P), 1.0, ALU.mult, ALU.add))
                link(dve.tensor_tensor(pos[:, :, :], pos[:, :, :], cumb[:, z, :].unsqueeze(1).broadcast_to([P, T, E]),
                                       ALU.add))
                link(dve.tensor_tensor(high[:, :, :], keep[:, :, :], pos[:, :, :], ALU.mult))
                link(dve.tensor_scalar(high[:, :, :], high[:, :, :], -1.0, None, ALU.add))
                link(dve.tensor_scalar(low[:, :, :], keep[:, :, :], -BIG, BIG - 1.0, ALU.mult, ALU.add))
                link(dve.tensor_tensor(low[:, :, :], low[:, :, :], pos[:, :, :], ALU.add))
                link(dve.tensor_reduce(pos2[:, :, 0], low[:, :, :], AX.X, ALU.min))
                link(dve.tensor_reduce(pos2[:, :, 1], high[:, :, :], AX.X, ALU.max))
                link(dve.tensor_copy(rt["slot"][:, :], pos2[:, :, :].rearrange("p t k -> p (t k)")))
                dve.tensor_scalar(at2[:, 0, :], rt["slot"][:, :], 7, None, ALU.arith_shift_right)
                link(dve.tensor_scalar(at2[:, 1, :], rt["slot"][:, :], P - 1, None, ALU.bitwise_and))
                link(dve.tensor_copy(at2f[:, :, :], at2[:, :, :]))
                dve.tensor_tensor(off_hot[:, :, :], at2f[:, 1, :].unsqueeze(2).broadcast_to([P, J, P]),
                                  iota_f[:, :].unsqueeze(1).broadcast_to([P, J, P]), ALU.is_equal)
                link(dve.tensor_tensor(blk_hot[:, :, :], at2f[:, 0, :].unsqueeze(2).broadcast_to([P, J, REAL]),
                                       iota_f[:, 0:REAL].unsqueeze(1).broadcast_to([P, J, REAL]), ALU.is_equal))
                dve.tensor_tensor(blk_hot[:, :, :].rearrange("p (t k) b -> p t (k b)", k=2),
                                  blk_hot[:, :, :].rearrange("p (t k) b -> p t (k b)", k=2),
                                  tok_f[:, :].unsqueeze(2).broadcast_to([P, T, 2 * REAL]), ALU.mult).then_inc(hot, 1)
                link(dve.tensor_tensor(low[:, :, :], low[:, :, :], per_e(pos2[:, :, 0]), ALU.is_equal))
                link(dve.tensor_tensor(low[:, :, :], low[:, :, :], tw[:, :, :], ALU.mult))
                link(dve.tensor_reduce(rt["weight"][:, :, 0], low[:, :, :], AX.X, ALU.add))
                link(dve.tensor_tensor(high[:, :, :], high[:, :, :], per_e(pos2[:, :, 1]), ALU.is_equal))
                link(dve.tensor_tensor(high[:, :, :], high[:, :, :], tw[:, :, :], ALU.mult))
                link(dve.tensor_reduce(rt["weight"][:, :, 1], high[:, :, :], AX.X, ALU.add))
                row_b = iota_f[0:1, 0:REAL].unsqueeze(2).broadcast_to([1, REAL, E])
                row_s = start[0:1, :].unsqueeze(1).broadcast_to([1, REAL, E])
                link(dve.tensor_tensor(tcmp[:, :, :], row_b, row_s, ALU.is_ge))
                link(dve.tensor_reduce(tabf[:, 0, :], tcmp[:, :, :], AX.X, ALU.add))
                link(dve.tensor_tensor(tcmp[:, :, :], row_b, row_s, ALU.is_equal))
                link(dve.tensor_reduce(tabf[:, 1, :], tcmp[:, :, 0:E - 1], AX.X, ALU.add))
                link(dve.tensor_reduce(tabf[:, 2, :], tcmp[:, :, 0:E - 2], AX.X, ALU.add))
                for row, bit in ((1, NEXT), (2, MORE)):
                    link(dve.scalar_tensor_tensor(out=tabf[:, 0, :], in0=tabf[:, row, :], scalar=float(bit),
                                                  in1=tabf[:, 0, :], op0=ALU.mult, op1=ALU.add))
                dve.tensor_copy(rt["table"][:, :], tabf[:, 0, :])
                dve.memset(rt["token"][:, REAL:REAL + 1], 0)
                dve.wait_ge(idx_done, 1)
                dve.tensor_copy(rt["token"][:, 0:REAL], IDX[:, 0:REAL])


def moe(nc, outer, dram):
    X, ident, ps, sem, rt = (outer[k] for k in ("X", "ident", "ps", "sem", "route"))
    FP = RE * P
    with ExitStack() as ctx:
        def sb(name, shape, dt=F32):
            return ctx.enter_context(nc.sbuf_tensor("m_" + name, shape, dt))

        rows = [sb(f"rows{k}", [P, D]) for k in range(4)]
        index = [sb(f"index{k}", [P, 1], I32) for k in range(4)]
        spacer = sb("spacer", [P, 1])
        xT_hi = sb("xT_hi", [P, 2, DC, P], F32R)
        xT_lo = sb("xT_lo", [P, 2, DC, P], F32R)
        sg = sb("sg", [P, 2, FE])
        hid = sb("hid", [P, 2, FP])
        hT_hi = sb("hT_hi", [P, 2, RE, P], F32R)
        hT_lo = sb("hT_lo", [P, 2, RE, P], F32R)
        y = sb("y", [P, 2, D])

        GATE = [ps[:, 0, 0:FE], ps[:, 1, 0:FE]]
        UP = [ps[:, 2, 0:FE], ps[:, 3, 0:FE]]
        XB, HB = ps[:, 4, :], ps[:, 5, 0:FP]
        ACC = [ps[:, 6, :], ps[:, 7, :]]

        got = [sem(f"m_got{k}") for k in range(4)]
        x_turned, x_hi_done, x_lo_done = sem("m_x_turned"), sem("m_x_hi_done"), sem("m_x_lo_done")
        gate_done, up_done, silu = sem("m_gate_done"), sem("m_up_done"), sem("m_silu")
        hid_made = sem("m_hid_made")
        h_turned, h_hi_done, h_lo_done = sem("m_h_turned"), sem("m_h_hi_done"), sem("m_h_lo_done")
        down_done = sem("m_down_done")
        y_done = sem("m_y_done")
        stored = [sem(f"m_stored{k}") for k in range(2)]
        gu_lo, dn_lo = sem("m_gu_lo"), sem("m_dn_lo")
        index_ready = sem("m_index_ready")
        gu_hi, dn_hi, ld_gu, ld_dn = rt["gu_hi"], rt["dn_hi"], rt["ld_gu"], rt["ld_dn"]

        def table(eng, g):
            at = slice(g, g + 1) if isinstance(g, int) else bass.ds(g, 1)
            return eng.value_load(rt["table"][0:1, at], min_val=0, max_val=2 * MORE - 1)

        def number(entry):
            return (entry & (NEXT - 1)).with_bounds(min_val=1, max_val=E)

        def other(entry):
            return bass.ds(entry & 1, 1)

        def pipeline(eng, body):
            with eng.Fori(0, (REAL - 1) // 4) as i:
                for j in range(4):
                    body(4 * i + j + 1, j, i)
            i = (REAL - 1) // 4
            for j in range((REAL - 1) % 4):
                body(4 * i + j + 1, j, i)

        def is_last(g):
            return isinstance(g, int) and g == REAL - 1

        with nc.Block() as block:
            @block.sync
            def _(sp):
                def reload(e1):
                    sp.wait_ge(gu_lo, e1 + 1)
                    load_expert(sp, rt, dram, e1 + 1, down=False)
                    sp.wait_ge(dn_lo, e1 + 1)
                    load_expert(sp, rt, dram, e1 + 1, gate_up=False)

                def body(g, j, i):
                    k = j % 2
                    sp.wait_ge(y_done, g + 2)
                    at = slice((g - 1) * P, g * P) if isinstance(g, int) else bass.ds((g - 1) * P, P)
                    sp.dma_start(rt["y_dram"][at, :], y[:, k, :]).then_inc(stored[k], 16)
                    entry = table(sp, g)
                    with sp.If((entry & MORE) != 0):
                        reload((entry & (NEXT - 1)).with_bounds(min_val=1, max_val=E - 2))

                load_expert(sp, rt, dram, 1)
                for k in range(2):
                    sp.sem_inc(stored[k], 16)
                reload(1)
                pipeline(sp, body)
                sp.wait_ge(y_done, REAL + 2)
                sp.dma_start(rt["y_dram"][(REAL - 1) * P:REAL * P, :], y[:, 0, :]).then_inc(stored[0], 16)

            @block.gpsimd
            def _(pool):
                def gather(g, b):
                    at = slice(g, g + 1) if isinstance(g, int) else bass.ds(g, 1)
                    pool.tensor_copy(index[b][:, :], rt["token"][:, at]).then_inc(index_ready, 1)
                    pool.wait_ge(index_ready, g + 1)
                    pool.tensor_tensor(spacer[:, :], ident[:, 0:1], ident[:, 0:1], ALU.mult)
                    pool.indirect_dma_start(out=rows[b][:, :], out_offset=None, in_=rt["xn_dram"],
                                            in_offset=bass.IndirectOffsetOnAxis(ap=index[b][:, 0:1], axis=0)
                                            ).then_inc(got[b], 16)

                def split_down(e1, at):
                    pool.wait_ge(dn_hi, e1 + 1)
                    pool.tensor_tensor(rt["dn_w_lo"][:, at], rt["raw_dn"], rt["dn_w_hi"][:, at].bitcast(F32),
                                       ALU.subtract).then_inc(dn_lo, 1)

                def body(g, j, i):
                    if not isinstance(g, int):
                        pool.wait_ge(x_turned, g)
                        gather(g + 3, j % 4)
                    entry = table(pool, g)
                    with pool.If((entry & NEXT) != 0):
                        split_down(number(entry), other(entry))

                pool.sem_inc(dn_lo, 1)
                for g in range(4):
                    gather(g, g)
                split_down(1, slice(1, 2))
                pipeline(pool, body)
                pool.wait_ge(got[REAL % 4], 16 * (REAL // 4 + 1))
                for k in range(2):
                    pool.wait_ge(stored[k], 16 * (1 + (REAL + 1 - k) // 2))

            @block.tensor
            def _(pe):
                def turn_rows(b, loads):
                    pe.wait_ge(got[b], 16 * loads)
                    for d in range(DC):
                        ins = pe.transpose(XB[:, P * d:P * d + P], rows[b][:, P * d:P * d + P], ident[:, :])
                    ins.then_inc(x_turned, 1)

                def product(bank, k, w, which):
                    for d in range(DC):
                        ins = product3(pe, bank[k], xT_hi[:, k, d, :], xT_lo[:, k, d, :],
                                       rt["gu_w_hi"][:, w, d, which, :], rt["gu_w_lo"][:, w, d, which, :],
                                       d == 0, d == DC - 1)
                    return ins

                def turn_hidden(g, k):
                    pe.wait_ge(hid_made, g + 3)
                    for r in range(RE):
                        ins = pe.transpose(HB[:, P * r:P * r + P], hid[:, k, P * r:P * r + P], ident[:, :])
                    ins.then_inc(h_turned, 1)

                def down(g, k, entry):
                    w = bass.ds((entry + 1) & 1, 1)
                    pe.wait_ge(h_lo_done, g + 1)
                    pe.wait_ge(y_done, g + 1)
                    pe.wait_ge(dn_lo, number(entry))
                    for r in range(RE):
                        ins = product3(pe, ACC[k], hT_hi[:, k, r, :], hT_lo[:, k, r, :], rt["dn_w_hi"][:, w, r, :],
                                       rt["dn_w_lo"][:, w, r, :], r == 0, r == RE - 1)
                    ins.then_inc(down_done, 1)

                entries = {}

                def body(g, j, i):
                    k = (j + 1) % 2
                    if j == 0:
                        entries["last"] = table(pe, g - 1)
                    entry, last = table(pe, g), entries["last"]
                    entries["last"] = entry
                    w = bass.ds((entry + 1) & 1, 1)
                    pe.wait_ge(gu_lo, number(entry))
                    pe.wait_ge(x_lo_done, g + 1)
                    pe.wait_ge(hid_made, g + 1)
                    product(GATE, k, w, 0).then_inc(gate_done, 1)
                    turn_hidden(g - 1, 1 - k)
                    product(UP, k, w, 1).then_inc(up_done, 1)
                    if not is_last(g):
                        turn_rows((j + 2) % 4, i + (j + 2) // 4 + 1)
                    down(g - 1, 1 - k, last)

                turn_rows(0, 1)
                pe.wait_ge(x_lo_done, 1)
                product(GATE, 0, slice(0, 1), 0).then_inc(gate_done, 1)
                product(UP, 0, slice(0, 1), 1).then_inc(up_done, 1)
                turn_rows(1, 1)
                pipeline(pe, body)
                turn_hidden(REAL - 1, 0)
                down(REAL - 1, 0, entries["last"])

            @block.scalar
            def _(act):
                def act_silu(g, k):
                    act.wait_ge(gate_done, g + 1)
                    act.activation(sg[:, k, :], GATE[k], ACT.Silu).then_inc(silu, 1)

                def hidden_hi(g, k):
                    act.wait_ge(h_turned, g + 1)
                    act.copy(hT_hi[:, k, :, :], HB.rearrange("p (r n) -> p r n", r=RE)).then_inc(h_hi_done, 1)

                def rows_hi(g, k):
                    act.wait_ge(x_turned, g + 1)
                    act.copy(xT_hi[:, k, :, :], XB.rearrange("p (d n) -> p d n", d=DC)).then_inc(x_hi_done, 1)

                def result(g, k, stores):
                    act.wait_ge(down_done, g + 1)
                    act.wait_ge(stored[k], 16 * stores)
                    act.copy(y[:, k, :], ACC[k]).then_inc(y_done, 1)

                def split(e1, at, ds):
                    act.wait_ge(ld_gu, 16 * DC * e1 + 16 * DC)
                    for d in ds:
                        act.copy(rt["gu_w_hi"][:, at, d], rt["raw_gu"][:, d].unsqueeze(1)).then_inc(gu_hi, 1)

                def body(g, j, i):
                    k = (j + 1) % 2
                    entry = table(act, g)
                    act_silu(g, k)
                    hidden_hi(g - 1, 1 - k)
                    with act.If((entry & NEXT) != 0):
                        split(number(entry), other(entry), (0, 1))
                    if not is_last(g):
                        rows_hi(g + 1, 1 - k)
                    with act.If((entry & NEXT) != 0):
                        split(number(entry), other(entry), (2, 3))
                    result(g - 1, 1 - k, 2 * i + j // 2 + 1)

                act.sem_inc(y_done, 2)
                rows_hi(0, 0)
                act_silu(0, 0)
                rows_hi(1, 1)
                split(1, slice(1, 2), range(DC))
                pipeline(act, body)
                hidden_hi(REAL - 1, 0)
                result(REAL - 1, 0, (REAL - 1) // 2 + 1)

            @block.vector
            def _(dve):
                def rows_lo(g, k):
                    dve.wait_ge(x_hi_done, g + 1)
                    dve.tensor_tensor(xT_lo[:, k, :, :], XB.rearrange("p (d n) -> p d n", d=DC),
                                      xT_hi[:, k, :, :].bitcast(F32), ALU.subtract).then_inc(x_lo_done, 1)

                def hidden(g, k):
                    dve.wait_ge(silu, g + 1)
                    dve.wait_ge(up_done, g + 1)
                    dve.tensor_tensor(hid[:, k, 0:FE], sg[:, k, :], UP[k], ALU.mult).then_inc(hid_made, 1)

                def hidden_lo(g, k):
                    dve.wait_ge(h_hi_done, g + 1)
                    dve.tensor_tensor(hT_lo[:, k, :, :], HB.rearrange("p (r n) -> p r n", r=RE),
                                      hT_hi[:, k, :, :].bitcast(F32), ALU.subtract).then_inc(h_lo_done, 1)

                def split(e1, at):
                    for d in range(DC):
                        dve.wait_ge(gu_hi, DC * e1 + d + 1)
                        ins = dve.tensor_tensor(rt["gu_w_lo"][:, at, d], rt["raw_gu"][:, d].unsqueeze(1),
                                                rt["gu_w_hi"][:, at, d].bitcast(F32), ALU.subtract)
                    ins.then_inc(gu_lo, 1)

                def split_down(e1, at):
                    dve.wait_ge(ld_dn, 16 * RE * e1 + 16 * RE)
                    dve.tensor_copy(rt["dn_w_hi"][:, at], rt["raw_dn"].unsqueeze(1)).then_inc(dn_hi, 1)

                def body(g, j, i):
                    k = (j + 1) % 2
                    entry = table(dve, g)
                    hidden_lo(g - 1, 1 - k)
                    hidden(g, k)
                    if not is_last(g):
                        rows_lo(g + 1, 1 - k)
                    with dve.If((entry & NEXT) != 0):
                        split(number(entry), other(entry))
                        dve.wait_ge(down_done, g)
                        split_down(number(entry), other(entry))

                dve.memset(hid[:, :, :], 0.0).then_inc(hid_made, 2)
                dve.wait_ge(hid_made, 2)
                dve.sem_inc(gu_lo, 1)
                rows_lo(0, 0)
                hidden(0, 0)
                rows_lo(1, 1)
                split(1, slice(1, 2))
                split_down(1, slice(1, 2))
                pipeline(dve, body)
                hidden_lo(REAL - 1, 0)


def image_attention(nc, outer, dram):
    X, ident, negh, ps, sem, rt = (outer[k] for k in ("X", "ident", "negh", "ps", "sem", "route"))
    with ExitStack() as ctx:
        def sb(name, shape, dt=F32):
            return ctx.enter_context(nc.sbuf_tensor("a_" + name, shape, dt))

        pair = [sb(f"pair{k}", [P, D]) for k in range(2 * TB)]
        x_hi = sb("x_hi", [P, 2, DC, N], F32R)
        x_lo = sb("x_lo", [P, 2, DC, N], F32R)
        c_raw = sb("c_raw", [P, B * N])
        c_hi = sb("c_hi", [P, B * N], F32R)
        c_lo = sb("c_lo", [P, B * N], F32R)
        wk_raw = sb("wk_raw", [P, CTX])
        wk_hi = sb("wk_hi", [P, CTX], F32R)
        wk_lo = sb("wk_lo", [P, CTX], F32R)
        bk = sb("bk", [P, 1])
        gamma = sb("gamma", [P, N])
        beta = sb("beta", [P, N])
        kvT = sb("kvT", [P, N])
        kvT_hi = sb("kvT_hi", [P, B, N], F32R)
        kvT_lo = sb("kvT_lo", [P, B, N], F32R)
        kv_hi = sb("kv_hi", [P, B, TB, CTX], F32R)
        kv_lo = sb("kv_lo", [P, B, TB, CTX], F32R)
        o_hi = sb("o_hi", [P, N], F32R)
        o_lo = sb("o_lo", [P, N], F32R)
        st = sb("st", [P, 2, 6])
        mv = sb("mv", [P, T, 2])
        ve = sb("ve", [P, T])
        rs = sb("rs", [P, T])
        y = sb("y", [P, 2, N])
        nmax = sb("nmax", [P, T])
        prob = sb("prob", [P, 2, N])
        den = sb("den", [P, T])
        rden = sb("rden", [P, T])
        norm = Norm("a_", sb, sem, X, ident, negh, [ps[:, 0, :], ps[:, 1, :]])
        KVB, KTB, OB = ps[:, 2, :], ps[:, 3, :], ps[:, 4, :]
        SIM = [ps[:, 5, :], ps[:, 6, :], ps[:, 7, :]]

        ld_c, ld_wk, ld_row = sem("a_ld_c"), sem("a_ld_wk"), sem("a_ld_row")
        in_hi, in_lo = sem("a_in_hi"), sem("a_in_lo")
        kvT_done, kvT_made, kvT_hi_done, kvT_lo_done = (
            sem("a_" + n) for n in ("kvT_done", "kvT_made", "kvT_hi_done", "kvT_lo_done"))
        kv_turned, kv_hi_done, kv_lo_done = sem("a_kv_turned"), sem("a_kv_hi_done"), sem("a_kv_lo_done")
        o_done, o_hi_done, o_lo_done = sem("a_o_done"), sem("a_o_hi_done"), sem("a_o_lo_done")
        sim_done, sim_free = sem("a_sim_done"), sem("a_sim_free")
        var_ready, rs_ready, y_ready, prob_ready, x_added = (
            sem("a_" + n) for n in ("svar_ready", "srs_ready", "y_ready", "prob_ready", "x_added"))
        dve_chain = sem("a_dve_chain")
        paired = [sem(f"a_paired{k}") for k in range(2 * TB)]
        added = sem("a_added")

        with nc.Block() as block:
            @block.sync
            def _(sp):
                sp.dma_start(wk_raw[:, :], dram["wkT"]).then_inc(ld_wk, 16)
                sp.dma_start(bk[:, :], dram["bk"]).then_inc(ld_wk, 16)
                sp.dma_start(c_raw[:, :], dram["ctxT"]).then_inc(ld_c, 16)
                sp.dma_start(gamma[:, :], dram["gamma"].broadcast_to([P, N])).then_inc(ld_row, 16)
                sp.dma_start(beta[:, :], dram["beta"].broadcast_to([P, N])).then_inc(ld_row, 16)
                sp.wait_ge(added, 4 * TB)
                for r in range(2):
                    sp.dma_start(outer["raw_gu"][:, r, :, :], dram["ffn_gu"][r]).then_inc(outer["ld_gu"][r], 16)
                for r in range(RQ):
                    sp.dma_start(outer["raw_dn"][:, r, :], dram["ffn_dn"][r]).then_inc(outer["ld_dn"][r], 16)

            @block.gpsimd
            def _(pool):
                def gather(c, i):
                    for k in range(2):
                        if c >= 1:
                            pool.wait_ge(added, TB * (2 * (c - 1) + k) + i + 1)
                        j = 2 * (TB * c + i) + k
                        pool.indirect_dma_start(out=pair[2 * i + k][:, :], out_offset=None, in_=rt["y_dram"],
                                                in_offset=bass.IndirectOffsetOnAxis(ap=rt["slot"][:, j:j + 1], axis=0)
                                                ).then_inc(paired[2 * i + k], 16)

                for i in range(TB):
                    gather(0, i)
                norm.pool_rstd(pool, 0)
                for i in range(TB):
                    gather(1, i)
                for b in range(B):
                    if b + 1 < B:
                        norm.pool_rstd(pool, b + 1)
                    for i in range(TB):
                        t = TB * b + i
                        pool.wait_ge(var_ready, t + 1)
                        pool.tensor_tensor(rs[:, t:t + 1], ve[:, t:t + 1], negh[:, 0:1], ALU.pow).then_inc(rs_ready, 1)
                        if b + 2 < B:
                            gather(b + 2, i)

            @block.tensor
            def _(pe):
                pe.wait_ge(in_lo, 2)
                for b in range(B):
                    if b >= 1:
                        pe.wait_ge(kvT_made, b)
                    product3(pe, KVB, wk_hi[:, :], wk_lo[:, :], c_hi[:, N * b:N * b + N], c_lo[:, N * b:N * b + N],
                             True, True).then_inc(kvT_done, 1)
                    pe.wait_ge(kvT_made, b + 1)
                    if b >= 1:
                        pe.wait_ge(kv_lo_done, b)
                    for i in range(TB):
                        ins = pe.transpose(KTB[:, P * i:P * i + P], kvT[:, P * i:P * i + P], ident[:, :])
                    ins.then_inc(kv_turned, 1)
                pe.wait_ge(kv_lo_done, B)
                for t in range(TB):
                    norm.pe_turn(pe, t)
                for b in range(B):
                    pe.wait_ge(norm.lo_done, TB * (b + 1))
                    if b >= 1:
                        pe.wait_ge(o_lo_done, b)
                    for j in range(TB):
                        ins = product3(pe, OB, kv_hi[:, b, j, :], kv_lo[:, b, j, :], x_hi[:, b % 2, j, :], x_lo[:, b % 2, j, :],
                                       j == 0, j == TB - 1)
                    ins.then_inc(o_done, 1)
                    pe.wait_ge(o_lo_done, b + 1)
                    for i in range(TB):
                        t = TB * b + i
                        if i == TB - 1 and b + 1 < B:
                            for n in range(TB * (b + 1), TB * (b + 2)):
                                norm.pe_turn(pe, n)
                        if t >= 3:
                            pe.wait_ge(sim_free, t - 2)
                        product3(pe, SIM[t % 3], o_hi[:, P * i:P * i + P], o_lo[:, P * i:P * i + P], kvT_hi[:, b, :],
                                 kvT_lo[:, b, :], True, True).then_inc(sim_done, 1)

            @block.scalar
            def _(act):
                act.wait_ge(ld_wk, 32)
                act.copy(wk_hi[:, :], wk_raw[:, :]).then_inc(in_hi, 1)
                act.wait_ge(ld_c, 16)
                act.copy(c_hi[:, :], c_raw[:, :]).then_inc(in_hi, 1)
                for b in range(B):
                    act.wait_ge(kvT_made, b + 1)
                    act.copy(kvT_hi[:, b, :], kvT[:, :]).then_inc(kvT_hi_done, 1)
                    act.wait_ge(kv_turned, b + 1)
                    act.copy(kv_hi[:, b, :, :], KTB.rearrange("p (j d) -> p j d", j=TB)).then_inc(kv_hi_done, 1)
                def x_hi_of(c):
                    if c >= 2:
                        act.wait_ge(o_done, c - 1)
                    for i in range(TB):
                        norm.act_hi(act, TB * c + i, x_hi[:, c % 2, :, P * i:P * i + P])

                x_hi_of(0)
                for b in range(B):
                    act.wait_ge(o_done, b + 1)
                    if b >= 1:
                        act.wait_ge(sim_done, TB * b)
                    act.copy(o_hi[:, :], OB).then_inc(o_hi_done, 1)
                    if b + 1 < B:
                        x_hi_of(b + 1)
                    for i in range(TB):
                        t = TB * b + i
                        act.wait_ge(y_ready, t + 1)
                        if t >= 2:
                            act.wait_ge(x_added, t - 1)
                        act.activation(prob[:, t % 2, :], y[:, t % 2, :], ACT.Exp, bias=nmax[:, t:t + 1],
                                       accum_out=den[:, t:t + 1]).then_inc(prob_ready, 1)

            @block.vector
            def _(dve):
                chain = Chain(dve, dve_chain)
                def add_pairs(c, slots=(0, 1)):
                    for k in slots:
                        for i in range(TB):
                            t = TB * c + i
                            dve.wait_ge(paired[2 * i + k], 16 * (c + 1))
                            if k == 1:
                                dve.wait_ge(added, 2 * TB * c + i + 1)
                            dve.scalar_tensor_tensor(out=X[:, t, :], in0=pair[2 * i + k][:, :],
                                                     scalar=rt["weight"][:, t, k:k + 1], in1=X[:, t, :],
                                                     op0=ALU.mult, op1=ALU.add).then_inc(added, 1)
                    dve.wait_ge(added, TB * (2 * c + slots[-1] + 1))

                def ready(c):
                    for i in range(TB + 1):
                        if i < TB:
                            norm.dve_norm(dve, TB * c + i)
                        if i >= 1:
                            s = slice(P * (i - 1), P * i)
                            norm.dve_lo(dve, TB * c + i - 1, x_hi[:, c % 2, :, s], x_lo[:, c % 2, :, s])

                dve.wait_ge(in_hi, 2)
                dve.tensor_tensor(wk_lo[:, :], wk_raw[:, :], wk_hi[:, :].bitcast(F32), ALU.subtract).then_inc(in_lo, 1)
                dve.tensor_tensor(c_lo[:, :], c_raw[:, :], c_hi[:, :].bitcast(F32), ALU.subtract).then_inc(in_lo, 1)
                for b in range(B):
                    dve.wait_ge(kvT_done, b + 1)
                    if b >= 1:
                        dve.wait_ge(kv_turned, b)
                        dve.wait_ge(kvT_lo_done, b)
                    dve.tensor_scalar(kvT[:, :], KVB, bk[:, 0:1], None, ALU.add).then_inc(kvT_made, 1)
                    if b < 2:
                        add_pairs(0, (b,))
                    if b == 2:
                        norm.dve_stats(chain, 0)
                    dve.wait_ge(kvT_hi_done, b + 1)
                    dve.tensor_tensor(kvT_lo[:, b, :], kvT[:, :], kvT_hi[:, b, :].bitcast(F32),
                                      ALU.subtract).then_inc(kvT_lo_done, 1)
                    dve.wait_ge(kv_hi_done, b + 1)
                    dve.tensor_tensor(kv_lo[:, b, :, :], KTB.rearrange("p (j d) -> p j d", j=TB),
                                      kv_hi[:, b, :, :].bitcast(F32), ALU.subtract).then_inc(kv_lo_done, 1)

                def scores_norm(t):
                    sim, yt = SIM[t % 3], y[:, t % 2, :]
                    dve.wait_ge(sim_done, t + 1)
                    chain.link(dve.bn_stats(st[:, t % 2, :], sim))
                    chain.link(dve.bn_aggr(mv[:, t, :], st[:, t % 2, :]))
                    dve.tensor_scalar(ve[:, t:t + 1], mv[:, t, 1:2], EPS_ATT / SCALE ** 2, None,
                                      ALU.add).then_inc(var_ready, 1)
                    if t >= 2:
                        dve.wait_ge(prob_ready, t - 1)
                    chain.n += 1
                    dve.scalar_tensor_tensor(out=yt, in0=sim, scalar=mv[:, t, 0:1], in1=gamma[:, :], op0=ALU.subtract,
                                             op1=ALU.mult).then_inc(chain.sem, 1)
                    dve.wait_ge(rs_ready, t + 1)
                    dve.wait_ge(chain.sem, chain.n)
                    chain.n += 1
                    dve.scalar_tensor_tensor(out=yt, in0=yt, scalar=rs[:, t:t + 1], in1=beta[:, :], op0=ALU.mult,
                                             op1=ALU.add).then_inc(chain.sem, 1)
                    dve.wait_ge(chain.sem, chain.n)
                    dve.tensor_reduce(nmax[:, t:t + 1], yt, AX.X, ALU.max, negate=True).then_inc(y_ready, 1)

                def add_prob(t):
                    dve.wait_ge(prob_ready, t + 1)
                    chain.link(dve.reciprocal(rden[:, t:t + 1], den[:, t:t + 1]))
                    dve.scalar_tensor_tensor(out=X[:, t, :], in0=prob[:, t % 2, :], scalar=rden[:, t:t + 1],
                                             in1=X[:, t, :], op0=ALU.mult, op1=ALU.add).then_inc(x_added, 1)

                dve.wait_ge(ld_row, 32)
                ready(0)
                for b in range(B):
                    if b + 1 < B:
                        add_pairs(b + 1)
                        norm.dve_stats(chain, b + 1)
                    dve.wait_ge(o_hi_done, b + 1)
                    dve.tensor_tensor(o_lo[:, :], OB, o_hi[:, :].bitcast(F32), ALU.subtract).then_inc(o_lo_done, 1)
                    if b + 1 < B:
                        ready(b + 1)
                    for i in range(TB):
                        t = TB * b + i
                        scores_norm(t)
                        dve.sem_inc(sim_free, 1)
                        if t >= 1:
                            add_prob(t - 1)
                add_prob(T - 1)


def ffn(nc, outer, dram, out):
    X, ident, negh, ps, sem = (outer[k] for k in ("X", "ident", "negh", "ps", "sem"))
    HN = N // 2
    with ExitStack() as ctx:
        def sb(name, shape, dt=F32):
            return ctx.enter_context(nc.sbuf_tensor("f_" + name, shape, dt))

        x_hi = sb("x_hi", [P, DC, B * N], F32R)
        x_lo = sb("x_lo", [P, DC, B * N], F32R)
        w_hi = sb("w_hi", [P, RQ, 3, D], F32R)
        w_lo = sb("w_lo", [P, RQ, 3, D], F32R)
        hid_hi = sb("hid_hi", [P, 1, RQ, N], F32R)
        hid_lo = sb("hid_lo", [P, 1, RQ, N], F32R)
        sg = sb("sg", [P, 2, N])
        hid = sb("hid", [P, RQ, N])
        mag = sb("mag", [P, RQ, N])
        beats = sb("beats", [P, 6, HN], BF16)
        tally = sb("tally", [P, RQ, HN], BF16)
        norm = Norm("f_", sb, sem, X, ident, negh, [ps[:, 4 + i, :] for i in range(TB)])
        mag_ready, mag_free, masked, dve_chain = sem("f_mag_ready"), sem("f_mag_free"), sem("f_masked"), sem("f_dve_chain")
        step_chain, stored = sem("f_step_chain"), sem("f_stored")
        u = Units("f_", outer, Q, RQ, 2, w_hi, w_lo, x_hi, x_lo, hid_hi, hid_lo, los=2)
        LINKS = 2 * 4

        with nc.Block() as block:
            @block.sync
            def _(sp):
                for r in range(2, RQ):
                    u.load_gate_up(sp, dram["ffn_gu"], 0, r)
                with sp.Fori(1, Q) as q:
                    for r in range(2):
                        u.load_gate_up(sp, dram["ffn_gu"], q, r)
                    for r in range(RQ):
                        u.load_down(sp, dram["ffn_dn"], q, r)
                    for r in range(2, RQ):
                        u.load_gate_up(sp, dram["ffn_gu"], q, r)
                for c in range(B):
                    sp.wait_ge(u.acc_free, TB + 16 * (Q - 1) + 4 * (c + 1))
                    sp.dma_start(out[c], X[:, TB * c:TB * c + TB, :]).then_inc(stored, 16)
                sp.wait_ge(stored, 16 * B)

            @block.gpsimd
            def _(pool):
                norm.pool_rstd(pool, 0)
                for r in range(RQ):
                    u.pool_gate_up(pool, 0, r)
                    if r + 1 < B:
                        norm.pool_rstd(pool, r + 1)
                for r in range(RQ):
                    u.pool_down(pool, 0, r)
                with pool.Fori(1, Q) as q:
                    for r in range(RQ):
                        u.pool_gate_up(pool, q, r)
                    for r in range(RQ):
                        u.pool_down(pool, q, r)

            @block.tensor
            def _(pe):
                for t in range(TB):
                    norm.pe_turn(pe, t)
                pe.wait_ge(norm.lo_done, TB)
                turns = iter(range(TB, T))

                def turn_two():
                    for t in islice(turns, 2):
                        norm.pe_turn(pe, t)

                u.pe_gate_up(pe, 0, 0, first=True, between=turn_two)
                pe.wait_ge(norm.lo_done, T)
                u.pe_rest(pe)

            @block.scalar
            def _(act):
                def x_hi_of(t):
                    norm.act_hi(act, t, x_hi[:, :, P * t:P * t + P])

                for r in range(2):
                    u.act_gate_up(act, 0, r, first=True)
                for t in range(TB):
                    x_hi_of(t)
                def sparsify(q, c, first=False):
                    s = 8 * q + 2 * c
                    act.wait_ge(u.hid_made, u.at(q, c, RQ))
                    for h in range(2):
                        half = slice(HN * h, HN * h + HN)
                        if not first:
                            act.wait_ge(mag_free, s + (h - 1))
                        act.activation(mag[:, :, half], hid[:, :, half], ACT.Abs).then_inc(mag_ready, 1)
                    if not first:
                        act.wait_ge(u.acc_done, 16 * q + 4 * c)
                    for h in range(2):
                        half = slice(HN * h, HN * h + HN)
                        act.wait_ge(masked, s + (h + 1))
                        act.copy(hid_hi[:, 0, :, half], hid[:, :, half]).then_inc(u.hid_hi_done, 1)

                for r in range(RQ):
                    for t in range(TB + 4 * r, min(TB + 4 * r + 4, T)):
                        x_hi_of(t)
                        if t % 4 == 1 and r < 2:
                            u.act_gate_up(act, 0, r + 2, first=True)
                    u.act_silu(act, 0, 0, r, sg, first=True)
                sparsify(0, 0, first=True)
                for r in range(RQ):
                    u.act_down(act, 0, r, first=True)
                with act.Fori(0, Q - 1) as q:
                    for c in (1, 2, 3):
                        for r in range(RQ):
                            u.act_silu(act, q, c, r, sg)
                            if c == 3:
                                u.act_gate_up(act, q + 1, r)
                        sparsify(q, c)
                    for r in range(RQ):
                        u.act_silu(act, q + 1, 0, r, sg)
                    sparsify(q + 1, 0)
                    for r in range(RQ):
                        u.act_down(act, q + 1, r)
                for c in (1, 2, 3):
                    for r in range(RQ):
                        u.act_silu(act, Q - 1, c, r, sg)
                    sparsify(Q - 1, c)

            @block.vector
            def _(dve):
                chain = Chain(dve, dve_chain)

                def x_lo_of(t):
                    s = slice(P * t, P * t + P)
                    norm.dve_lo(dve, t, x_hi[:, :, s], x_lo[:, :, s])

                def norm_chunk(c):
                    for i in range(0, TB, 2):
                        for t in (TB * c + i, TB * c + i + 1):
                            norm.dve_norm(dve, t)
                        if i == 0 and c + 1 < B:
                            norm.dve_stats(chain, c + 1)
                        for t in (TB * c + i, TB * c + i + 1):
                            x_lo_of(t)

                norm.dve_stats(chain, 0)
                norm_chunk(0)
                dve.sem_inc(u.acc_free, TB)

                def hidden(q, c, first=False):
                    if not first:
                        dve.wait_ge(u.hid_lo_done, 8 * q + 2 * c)
                    for r in range(RQ):
                        if first and r + 1 < B:
                            norm_chunk(r + 1)
                        u.dve_hid(dve, q, c, r, sg, hid[:, r, :])
                    for h in range(2):
                        keep_two(q, c, h)
                    for h in range(2):
                        split(q, c, h)

                def keep_two(q, c, h):
                    links = LINKS * 4 * q + LINKS * c + 4 * h
                    half = slice(HN * h, HN * h + HN)
                    dve.wait_ge(mag_ready, 8 * q + (2 * c + h + 1))
                    for i, j0, j1, at in ((0, 1, 4, 0), (1, 2, 4, 3), (2, 3, 4, 5)):
                        n = j1 - j0
                        ins = dve.tensor_tensor(beats[:, at:at + n, :],
                                                mag[:, i, half].unsqueeze(1).broadcast_to([P, n, HN]),
                                                mag[:, j0:j1, half], ALU.is_ge)
                    ins.then_inc(step_chain, 1)
                    dve.wait_ge(step_chain, links + 1)
                    dve.sem_inc(mag_free, 1)
                    b = [beats[:, k, :] for k in range(6)]
                    dve.tensor_tensor(tally[:, 0, :], b[0], b[1], ALU.add)
                    dve.tensor_tensor(tally[:, 1, :], b[0], b[3], ALU.subtract)
                    dve.tensor_tensor(tally[:, 2, :], b[1], b[3], ALU.add)
                    dve.tensor_tensor(tally[:, 3, :], b[2], b[4], ALU.add).then_inc(step_chain, 1)
                    dve.wait_ge(step_chain, links + 2)
                    dve.tensor_tensor(tally[:, 0, :], tally[:, 0, :], b[2], ALU.add)
                    dve.tensor_tensor(tally[:, 1, :], tally[:, 1, :], b[4], ALU.subtract)
                    dve.tensor_tensor(tally[:, 2, :], tally[:, 2, :], b[5], ALU.subtract)
                    dve.tensor_tensor(tally[:, 3, :], tally[:, 3, :], b[5], ALU.add).then_inc(step_chain, 1)
                    dve.wait_ge(step_chain, links + 3)
                    for r, (bound, op) in enumerate(((1.5, ALU.is_ge), (-0.5, ALU.is_le), (0.5, ALU.is_le),
                                                     (1.5, ALU.is_le))):
                        ins = dve.scalar_tensor_tensor(out=hid[:, r, half], in0=tally[:, r, :], scalar=bound,
                                                       in1=hid[:, r, half], op0=op, op1=ALU.mult)
                    ins.then_inc(step_chain, 1)
                    dve.wait_ge(step_chain, links + 4)
                    dve.sem_inc(masked, 1)

                def split(q, c, h):
                    half = slice(HN * h, HN * h + HN)
                    dve.wait_ge(u.hid_hi_done, 8 * q + (2 * c + h + 1))
                    dve.tensor_tensor(hid_lo[:, 0, :, half], hid[:, :, half], hid_hi[:, 0, :, half].bitcast(F32),
                                      ALU.subtract).then_inc(u.hid_lo_done, 1)

                def evac(q, c):
                    for i in range(TB):
                        u.dve_wait_acc(dve, q, c, i)
                        dve.tensor_tensor(X[:, TB * c + i, :], u.ACC[i], X[:, TB * c + i, :],
                                          ALU.add).then_inc(u.acc_free, 1)

                hidden(0, 0, first=True)
                with dve.Fori(0, Q - 1) as q:
                    for c in range(4):
                        hidden(*((q, c + 1) if c < 3 else (q + 1, 0)))
                        evac(q, c)
                for c in range(4):
                    if c < 3:
                        hidden(Q - 1, c + 1)
                    evac(Q - 1, c)


def build(nc, dram, out):
    with ExitStack() as ctx:
        def sem(name):
            return ctx.enter_context(nc.semaphore(name))

        def sb(name, shape, dt=F32):
            return ctx.enter_context(nc.sbuf_tensor(name, shape, dt))

        outer = {
            "sem": sem,
            "X": sb("x", [P, T, D]),
            "ident": sb("ident", [P, P]),
            "negh": sb("minus_half", [P, TB]),
            "flag": sb("flag", [1, 1], I32),
            "ps": ctx.enter_context(nc.psum_tensor("ps", [P, 8, 512], F32)),
            "ld_gu": [sem(f"ld_gate_up{r}") for r in range(2)],
            "ld_dn": [sem(f"ld_down{r}") for r in range(RQ)],
            "pool_const": sem("pool_const"),
        }
        raw = sb("raw", [P, (2 * DC * FE) + RE * D])
        gu, dn = 2 * DC * FE, RE * D
        outer["raw_gu"] = raw[:, 0:4 * D].rearrange("p (s k n) -> p s k n", s=2, k=2)
        outer["raw_dn"] = raw[:, 4 * D:8 * D].rearrange("p (s n) -> p s n", s=RQ)
        route_ = outer["route"] = {
            "raw_gu": raw[:, 0:gu].rearrange("p (d k f) -> p d k f", d=DC, k=2),
            "raw_dn": raw[:, gu:gu + dn].rearrange("p (r n) -> p r n", r=RE),
            "slot": sb("slot", [P, 2 * T], I32),
            "weight": sb("weight", [P, T, 2]),
            "token": sb("token", [P, REAL + 1], I32),
            "table": sb("table", [1, REAL], I32),
            "xn_dram": nc.dram_tensor("xn_scratch", (B * N, D), F32, kind="Internal").ap(),
            "y_dram": nc.dram_tensor("y_scratch", (REAL * P, D), F32, kind="Internal").ap(),
            **{k: sem("e_" + k) for k in ("ld_gu", "ld_dn", "gu_hi", "dn_hi")},
        }
        gat_one_hot(nc, outer, dram)
        holds = nc.values_load(outer["flag"][0:1, 0:1], min_val=0, max_val=1)
        with nc.If(holds == 0):
            gat_general(nc, outer, dram)
        with ExitStack() as experts:
            for name, shape in (("gu_w", [P, 2, DC, 2, FE]), ("dn_w", [P, 2, RE, D])):
                for part in ("_hi", "_lo"):
                    route_[name + part] = experts.enter_context(nc.sbuf_tensor(name + part, shape, F32R))
            route(nc, outer, dram)
            moe(nc, outer, dram)
        image_attention(nc, outer, dram)
        ffn(nc, outer, dram, out)


def kernel(x, ctx_512, L0_xattn_W0, L0_xattn_a_self0, L0_xattn_a_neigh0, L0_xattn_b0, L0_xattn_W1,
           L0_xattn_a_self1, L0_xattn_a_neigh1, L0_xattn_b1, L0_ffn_gate_w, L0_ffn_gate_proj, L0_ffn_up_proj,
           L0_ffn_down_proj, L1_xattn_W_k, L1_xattn_b_k, L1_xattn_ln_gamma, L1_xattn_ln_beta, L1_ffn_w_gate,
           L1_ffn_w_up, L1_ffn_w_down):
    import numpy as np
    from concourse import bacc
    from concourse.bass_utils import run_bass_kernel_spmd

    def tokens(a):
        return a.reshape(-1, P, a.shape[-1]).transpose(1, 0, 2)

    def heads(w):
        return w.transpose(1, 0, 2).reshape(-1, P, H * FO).transpose(1, 0, 2)

    pad = ((0, 0), (0, RE * P - FE), (0, 0))

    def expert_in(w):
        return w.reshape(E, FE, DC, P).transpose(0, 3, 2, 1)

    def quartet_in(w):
        return w.reshape(DC, P, Q, P, RQ).transpose(2, 4, 1, 0, 3).reshape(Q * RQ, P, D)

    a = {k: np.asarray(v) for k, v in locals().items() if hasattr(v, "shape")}
    arrays = {
        "x": a["x"].reshape(B, TB, P, D).transpose(0, 2, 1, 3),
        "ctx": tokens(a["ctx_512"]),
        "ctxT": a["ctx_512"].reshape(B * N, CTX).T,
        "gat_w": np.concatenate([heads(a["L0_xattn_W0"]), heads(a["L0_xattn_W1"])], axis=1),
        "att0": np.stack([a["L0_xattn_a_self0"].ravel(), a["L0_xattn_a_neigh0"].ravel()]),
        "att1": np.stack([a["L0_xattn_a_self1"].ravel(), a["L0_xattn_a_neigh1"].ravel()]),
        "b0_col": a["L0_xattn_b0"].reshape(DC, P).T,
        "b0": a["L0_xattn_b0"].reshape(1, D),
        "b1": a["L0_xattn_b1"].reshape(1, D),
        "gate_w": a["L0_ffn_gate_w"].reshape(E, DC, P).transpose(2, 1, 0),
        "moe_gu": np.stack([expert_in(a["L0_ffn_gate_proj"]), expert_in(a["L0_ffn_up_proj"])], axis=3),
        "moe_dn": np.pad(a["L0_ffn_down_proj"].transpose(0, 2, 1), pad).reshape(E, RE, P, D).transpose(0, 2, 1, 3),
        "wkT": a["L1_xattn_W_k"].T,
        "bk": a["L1_xattn_b_k"].reshape(CTX, 1),
        "gamma": a["L1_xattn_ln_gamma"].reshape(1, N),
        "beta": a["L1_xattn_ln_beta"].reshape(1, N),
        "ffn_gu": np.stack([quartet_in(a["L1_ffn_w_gate"]), quartet_in(a["L1_ffn_w_up"])], axis=2),
        "ffn_dn": a["L1_ffn_w_down"].reshape(Q, P, RQ, D).transpose(0, 2, 1, 3).reshape(Q * RQ, P, D),
    }
    nc = bacc.Bacc("TRN2", target_bir_lowering=False, num_devices=1)
    in_map, dram = {}, {}
    for name, v in arrays.items():
        in_map["in_" + name] = np.ascontiguousarray(v)
        dram[name] = nc.dram_tensor("in_" + name, v.shape, mybir.dt.from_np(v.dtype), kind="ExternalInput").ap()
    out = nc.dram_tensor("out", (B, P, TB, D), F32, kind="ExternalOutput").ap()
    build(nc, dram, out)
    r = run_bass_kernel_spmd(nc, [in_map], core_ids=[0])
    return r.results[0]["out"].reshape(B, P, TB, D).transpose(0, 2, 1, 3).reshape(B, N, D)
```

```python
from contextlib import ExitStack
from itertools import islice

import concourse.bass as bass
from concourse import mybir

F32 = mybir.dt.float32
F32R = mybir.dt.float32r
BF16 = mybir.dt.bfloat16
I32 = mybir.dt.int32
ALU = mybir.AluOpType
ACT = mybir.ActivationFunctionType
AX = mybir.AxisListType

P = 128
B, N, D = 4, 512, 512
T = B * N // P
TB = N // P
DC = D // P
CTX = 128
H, FO = 8, 64
E, FE = 8, 352
RE = -(-FE // P)
I = 2048
Q, RQ = I // (4 * P), 4
EPS = 1e-5
EPS_ATT = 1e-6
SCALE = float(D) ** -0.5
SLOPE = 0.2
MASK = 1e10
GAP_MIN = 16384.0
BOUND_MAX = 4000.0
REAL = 2 * B * N // P + E - 1
NEXT, MORE = 16, 32
BIG = 65536.0


def load_expert(sp, rt, dram, e, gate_up=True, down=True):
    at = slice(e, e + 1) if isinstance(e, int) else bass.ds(e, 1)
    for d in range(DC if gate_up else 0):
        sp.dma_start(rt["raw_gu"][:, d], dram["moe_gu"][at, :, d].rearrange("o p k f -> (o p) k f")
                     ).then_inc(rt["ld_gu"], 16)
    for r in range(RE if down else 0):
        sp.dma_start(rt["raw_dn"][:, r], dram["moe_dn"][at, :, r].rearrange("o p n -> (o p) n")
                     ).then_inc(rt["ld_dn"], 16)


class Chain:

    def __init__(self, eng, sem):
        self.eng, self.sem, self.n = eng, sem, 0

    def link(self, ins):
        self.n += 1
        ins.then_inc(self.sem, 1)
        self.eng.wait_ge(self.sem, self.n)


def product3(eng, out, lhs_hi, lhs_lo, rhs_hi, rhs_lo, start, stop):
    eng.matmul(out, lhs_hi, rhs_lo, start=start, stop=False)
    eng.matmul(out, lhs_lo, rhs_hi, start=False, stop=False)
    return eng.matmul(out, lhs_hi, rhs_hi, start=False, stop=stop)


class Norm:

    def __init__(self, tag, sb, sem, X, ident, negh, banks, buffers=2, order=None):
        self.order = order or [t % len(banks) for t in range(T)]
        self.X, self.ident, self.negh, self.banks, self.nb = X, ident, negh, banks, buffers
        self.stats = sb(tag + "stats", [P, TB, 6], F32)
        self.mv = sb(tag + "mean_var", [P, T, 2], F32)
        self.ve = sb(tag + "var_eps", [P, T], F32)
        self.rstd = sb(tag + "rstd", [P, T], F32)
        self.nmean = sb(tag + "minus_mean", [P, T], F32)
        self.xn = sb(tag + "xn", [P, buffers, D], F32)
        self.var_ready = sem(tag + "var_ready")
        self.rstd_ready = sem(tag + "rstd_ready")
        self.xn_ready = sem(tag + "xn_ready")
        self.turned = sem(tag + "turned")
        self.hi_done = sem(tag + "hi_done")
        self.lo_done = sem(tag + "lo_done")

    def bank(self, t):
        return self.banks[self.order[t]]

    def dve_stats(self, chain, c):
        for i in range(TB):
            ins = chain.eng.bn_stats(self.stats[:, i, :], self.X[:, TB * c + i, :])
        chain.link(ins)
        for i in range(TB):
            ins = chain.eng.bn_aggr(self.mv[:, TB * c + i, :], self.stats[:, i, :])
        chain.link(ins)
        chain.eng.tensor_scalar(self.ve[:, TB * c:TB * c + TB], self.mv[:, TB * c:TB * c + TB, 1], EPS, None,
                                ALU.add).then_inc(self.var_ready, 1)

    def pool_rstd(self, eng, c):
        eng.wait_ge(self.var_ready, c + 1)
        s = slice(TB * c, TB * c + TB)
        eng.tensor_tensor(self.rstd[:, s], self.ve[:, s], self.negh[:, 0:TB], ALU.pow).then_inc(self.rstd_ready, 1)

    def dve_stats_for_act(self, chain, c):
        for i in range(TB):
            ins = chain.eng.bn_stats(self.stats[:, i, :], self.X[:, TB * c + i, :])
        chain.link(ins)
        for i in range(TB):
            ins = chain.eng.bn_aggr(self.mv[:, TB * c + i, :], self.stats[:, i, :])
        chain.link(ins)
        s = slice(TB * c, TB * c + TB)
        chain.eng.tensor_scalar(self.nmean[:, s], self.mv[:, s, 0], -1.0, None, ALU.mult)
        chain.eng.tensor_scalar(self.ve[:, s], self.mv[:, s, 1], EPS, None, ALU.add).then_inc(self.var_ready, 1)

    def pool_rstd_for_act(self, eng, c):
        eng.wait_ge(self.var_ready, c + 1)
        s = slice(TB * c, TB * c + TB)
        eng.tensor_tensor(self.rstd[:, s], self.ve[:, s], self.negh[:, 0:TB], ALU.pow).then_inc(self.rstd_ready, 1)
        eng.wait_ge(self.rstd_ready, 2 * c + 1)
        eng.tensor_tensor(self.nmean[:, s], self.nmean[:, s], self.rstd[:, s], ALU.mult).then_inc(self.rstd_ready, 1)

    def act_norm(self, eng, t):
        if t % TB == 0:
            eng.wait_ge(self.rstd_ready, 2 * (t // TB) + 2)
        if t >= self.nb:
            eng.wait_ge(self.turned, t - self.nb + 1)
        eng.activation(self.xn[:, t % self.nb, :], self.X[:, t, :], ACT.Identity, bias=self.nmean[:, t:t + 1],
                       scale=self.rstd[:, t:t + 1]).then_inc(self.xn_ready, 1)

    def dve_norm(self, eng, t):
        if t % TB == 0:
            eng.wait_ge(self.rstd_ready, t // TB + 1)
        if t >= self.nb:
            eng.wait_ge(self.turned, t - self.nb + 1)
        eng.tensor_scalar(self.xn[:, t % self.nb, :], self.X[:, t, :], self.mv[:, t, 0:1], self.rstd[:, t:t + 1],
                          ALU.subtract, ALU.mult).then_inc(self.xn_ready, 1)

    def pe_turn(self, eng, t):
        bank = self.bank(t)
        eng.wait_ge(self.xn_ready, t + 1)
        before = [n for n in range(t) if self.order[n] == self.order[t]]
        if before:
            eng.wait_ge(self.lo_done, before[-1] + 1)
        for d in range(DC):
            ins = eng.transpose(bank[:, P * d:P * d + P], self.xn[:, t % self.nb, P * d:P * d + P], self.ident[:, :])
        ins.then_inc(self.turned, 1)

    def act_hi(self, eng, t, hi):
        eng.wait_ge(self.turned, t + 1)
        eng.copy(hi, self.bank(t).rearrange("p (d n) -> p d n", d=DC)).then_inc(self.hi_done, 1)

    def dve_lo(self, eng, t, hi, lo):
        eng.wait_ge(self.hi_done, t + 1)
        eng.tensor_tensor(lo, self.bank(t).rearrange("p (d n) -> p d n", d=DC), hi.bitcast(F32),
                          ALU.subtract).then_inc(self.lo_done, 1)


def gat_one_hot(nc, outer, dram):
    X, ident, negh, flag = outer["X"], outer["ident"], outer["negh"], outer["flag"]
    with ExitStack() as ctx:
        def sb(name, shape, dt=F32):
            return ctx.enter_context(nc.sbuf_tensor("g_" + name, shape, dt))

        sems = []

        def sem(name):
            sems.append(nc.alloc_semaphore(name=name))
            return sems[-1]

        ps = outer["ps"]

        ctx_raw = sb("ctx_raw", [P, T, CTX])
        ctx_hi = sb("ctx_hi", [P, T, CTX], F32R)
        ctx_lo = sb("ctx_lo", [P, T, CTX], F32R)
        w_raw = sb("w_raw", [P, 1 + DC, H * FO])
        w_hi = sb("w_hi", [P, 1 + DC, H * FO], F32R)
        w_lo = sb("w_lo", [P, 1 + DC, H * FO], F32R)
        att = sb("att", [P, 2, H * FO])
        b0_col = sb("b0_col", [P, DC])
        b1_row = sb("b1_row", [P, D])
        stats = sb("stats", [P, TB, 6])
        mv = sb("mean_var", [P, T, 2])
        ve = sb("var_eps", [P, T])
        rstd = sb("rstd", [P, T])
        adj = sb("adj", [P, 2, N])
        top = sb("top", [P, T, 8])
        pick = sb("pick", [P, 2, TB, N], F32R)
        g_hi = sb("g_hi", [P, N], F32R)
        g_lo = sb("g_lo", [P, N], F32R)
        ebuf = sb("ebuf", [P, 2, N])
        rbuf = sb("rbuf", [P, 2, N])
        hbuf = sb("hbuf", [P, 2, N])
        h_hi = sb("h_hi", [P, 2, DC, N], F32R)
        h_lo = sb("h_lo", [P, 2, DC, N], F32R)
        f_hi = sb("f_hi", [P, TB, D], F32R)
        f_lo = sb("f_lo", [P, TB, D], F32R)
        wsum = sb("wsum", [P, 1 + DC, H])
        wmax = sb("wmax", [P, 1 + DC])
        csum = sb("csum", [P, T])
        hmax = sb("hmax", [P, T])
        hcol = sb("hcol", [P, DC])
        hw = sb("hw", [P, DC])
        tops = sb("tops", [P, T, 2])
        gap = sb("gap", [P, T])
        per_part = sb("per_part", [P, 4])
        red = sb("red", [1, 8])
        zbuf = sb("zbuf", [P, 2, N])
        zexp = sb("zexp", [P, 2, N])

        TBANK = [ps[:, 0, :], ps[:, 1, :]]
        GBANK = ps[:, 2, :]
        HBANK = [ps[:, 3, :], ps[:, 4, :]]
        RING = [ps[:, 5, :], ps[:, 6, :], ps[:, 7, :]]

        ld_x = [sem(f"ga_ld_x{b}") for b in range(B)]
        ld_ctx, ld_w, ld_att0, ld_att1, ld_b = (sem("ga_" + n) for n in ("ld_ctx", "ld_w", "ld_att0", "ld_att1", "ld_b"))
        ctx_hi_done, ctx_lo_done = sem("ga_ctx_hi_done"), sem("ga_ctx_lo_done")
        w_hi_done, w_lo_done = sem("ga_w_hi_done"), sem("ga_w_lo_done")
        att_abs, att_free = sem("ga_att_abs"), sem("ga_att_free")
        var_ready, rstd_ready = sem("ga_var_ready"), sem("ga_rstd_ready")
        hot_ready, turned, pick_done = sem("ga_hot_ready"), sem("ga_turned"), sem("ga_pick_done")
        g_done, g_hi_done, g_lo_done = sem("ga_g_done"), sem("ga_g_hi_done"), sem("ga_g_lo_done")
        h_done, h_act, h_exp1, h_sum, h_hi_done, h_lo_done = (
            sem("ga_" + n) for n in ("h_done", "h_act", "h_exp1", "h_sum", "h_hi_done", "h_lo_done"))
        f_done, f_hi_done, ring_free = sem("ga_f_done"), sem("ga_f_hi_done"), sem("ga_ring_free")
        o_done, z_exp, y_ready, x_added = sem("ga_o_done"), sem("ga_z_exp"), sem("ga_y_ready"), sem("ga_x_added")
        dve_chain = sem("ga_dve_chain")
        bounds_ready, bounds_turned = sem("ga_bounds_ready"), sem("ga_bounds_turned")
        pool_const = outer["pool_const"]

        steps = [(b if b < B else None, b - 1 if b >= 1 else None) for b in range(B + 1)]

        with nc.Block() as block:
            @block.sync
            def _(sp):
                sp.dma_start(X[:, 0:TB, :], dram["x"][0]).then_inc(ld_x[0], 16)
                sp.dma_start(w_raw[:, :, :], dram["gat_w"]).then_inc(ld_w, 16)
                sp.dma_start(ctx_raw[:, :, :], dram["ctx"]).then_inc(ld_ctx, 16)
                sp.dma_start(b0_col[:, :], dram["b0_col"]).then_inc(ld_b, 16)
                sp.dma_start(b1_row[:, :], dram["b1"].broadcast_to([P, D])).then_inc(ld_b, 16)
                for b in range(1, B):
                    sp.dma_start(X[:, TB * b:TB * b + TB, :], dram["x"][b]).then_inc(ld_x[b], 16)
                for j in range(2):
                    sp.dma_start(att[:, j, :], dram["att0"][j:j + 1, :].broadcast_to([P, D])).then_inc(ld_att0, 16)
                load_expert(sp, outer["route"], dram, 0)
                sp.wait_ge(att_free, 1)
                for j in range(2):
                    sp.dma_start(att[:, j, :], dram["att1"][j:j + 1, :].broadcast_to([P, D])).then_inc(ld_att1, 16)

            @block.gpsimd
            def _(pool):
                pool.memset(ident[:, :], 0.0).then_inc(pool_const, 1)
                pool.memset(negh[:, :], -0.5).then_inc(pool_const, 1)
                pool.wait_ge(pool_const, 2)
                pool.affine_select(out=ident[:, :], in_=ident[:, :], compare_op=ALU.not_equal, fill=1.0, base=0,
                                   pattern=[[-1, P]], channel_multiplier=1).then_inc(pool_const, 1)

                def rstd_of(b):
                    pool.wait_ge(var_ready, b + 1)
                    s = slice(TB * b, TB * b + TB)
                    pool.tensor_tensor(rstd[:, s], ve[:, s], negh[:, 0:TB], ALU.pow).then_inc(rstd_ready, 1)

                def layer1_sum(b, fc):
                    j = DC * b + fc
                    pool.wait_ge(h_exp1, j + 1)
                    if j >= 2:
                        pool.wait_ge(h_lo_done, j - 1)
                    pool.tensor_tensor(hbuf[:, j % 2, :], ebuf[:, j % 2, :], rbuf[:, j % 2, :],
                                       ALU.add).then_inc(h_sum, 1)

                def add_x(b, i):
                    t = TB * b + i
                    pool.wait_ge(y_ready, t + 1)
                    pool.tensor_tensor(X[:, t, :], X[:, t, :], zbuf[:, t % 2, :], ALU.add).then_inc(x_added, 1)

                rstd_of(0)
                pool.wait_ge(w_hi_done, 1)
                pool.tensor_tensor(w_lo[:, :, :], w_raw[:, :, :], w_hi[:, :, :].bitcast(F32),
                                   ALU.subtract).then_inc(w_lo_done, 1)
                for new, old in steps:
                    if new is not None and new + 1 < B:
                        rstd_of(new + 1)
                    for k in range(TB + 1):
                        if new is not None and k < TB:
                            layer1_sum(new, k)
                        if old is not None and k >= 1:
                            add_x(old, k - 1)

            @block.tensor
            def _(pe):
                pe.wait_ge(pool_const, 3)

                def turn_hot(b, i):
                    t = TB * b + i
                    pe.wait_ge(hot_ready, t + 1)
                    if t >= 2:
                        pe.wait_ge(pick_done, t - 1)
                    for m in range(TB):
                        ins = pe.transpose(TBANK[t % 2][:, P * m:P * m + P], adj[:, t % 2, P * m:P * m + P],
                                           ident[:, :])
                    ins.then_inc(turned, 1)

                def context_rows(b):
                    if b == 0:
                        pe.wait_ge(ctx_lo_done, 1)
                    pe.wait_ge(pick_done, TB * (b + 1))
                    if b >= 1:
                        pe.wait_ge(g_lo_done, b)
                    for m in range(TB):
                        pe.matmul(GBANK, ctx_lo[:, TB * b + m, :], pick[:, b % 2, m, :], start=(m == 0), stop=False)
                        ins = pe.matmul(GBANK, ctx_hi[:, TB * b + m, :], pick[:, b % 2, m, :], start=False,
                                        stop=(m == TB - 1))
                    ins.then_inc(g_done, 1)

                def hidden(b, fc):
                    if fc == 0:
                        pe.wait_ge(g_lo_done, b + 1)
                    if b == 0:
                        pe.wait_ge(w_lo_done, 1)
                    j = DC * b + fc
                    if j >= 2:
                        pe.wait_ge(h_act, j - 1)
                    product3(pe, HBANK[j % 2], w_hi[:, 0, P * fc:P * fc + P], w_lo[:, 0, P * fc:P * fc + P],
                             g_hi[:, :], g_lo[:, :], True, True).then_inc(h_done, 1)

                def features(b, m):
                    if m == 0:
                        pe.wait_ge(h_lo_done, DC * (b + 1))
                    u = 2 * TB * b + m
                    if u >= 3:
                        pe.wait_ge(ring_free, u - 2)
                    for d in range(DC):
                        ins = product3(pe, RING[u % 3], h_hi[:, b % 2, d, P * m:P * m + P],
                                       h_lo[:, b % 2, d, P * m:P * m + P], w_hi[:, 1 + d, :], w_lo[:, 1 + d, :],
                                       d == 0, d == DC - 1)
                    ins.then_inc(f_done, 1)

                def picked(b, n):
                    u = 2 * TB * b + TB + n
                    pe.wait_ge(ring_free, max(u - 2, 2 * TB * b + TB))
                    for m in range(TB):
                        lhs = pick[:, b % 2, m, P * n:P * n + P]
                        pe.matmul(RING[u % 3], lhs, f_lo[:, m, :], start=(m == 0), stop=False)
                        ins = pe.matmul(RING[u % 3], lhs, f_hi[:, m, :], start=False, stop=(m == TB - 1))
                    ins.then_inc(o_done, 1)

                for new, old in steps:
                    for k in range(TB + 1):
                        if new is not None:
                            if k == 0:
                                turn_hot(new, 0)
                            if k < TB - 1:
                                turn_hot(new, k + 1)
                            if k == TB - 1:
                                context_rows(new)
                        if old is not None and k < TB:
                            features(old, k)
                    if new is None:
                        pe.wait_ge(bounds_ready, 1)
                        for j in range(4):
                            ins = pe.transpose(TBANK[0][0:1, P * j:P * j + P], per_part[:, j:j + 1], ident[:, :])
                        ins.then_inc(bounds_turned, 1)
                    for k in range(TB):
                        if old is not None:
                            picked(old, k)
                        if new is not None:
                            hidden(new, k)

            @block.scalar
            def _(act):
                act.wait_ge(ld_w, 16)
                act.copy(w_hi[:, :, :], w_raw[:, :, :]).then_inc(w_hi_done, 1)
                act.wait_ge(ld_ctx, 16)
                act.copy(ctx_hi[:, :, :], ctx_raw[:, :, :]).then_inc(ctx_hi_done, 1)

                def bound_part(layer):
                    act.wait_ge([ld_att0, ld_att1][layer], 32)
                    act.activation(att[:, :, :], att[:, :, :], ACT.Abs).then_inc(att_abs, 1)

                def pick_of(b, i):
                    t = TB * b + i
                    act.wait_ge(turned, t + 1)
                    if b >= 2 and i == 0:
                        act.wait_ge(o_done, TB * (b - 1))
                    act.copy(pick[:, b % 2, :, P * i:P * i + P],
                             TBANK[t % 2].rearrange("p (m n) -> p m n", m=TB)).then_inc(pick_done, 1)

                def g_hi_of(b):
                    act.wait_ge(g_done, b + 1)
                    act.copy(g_hi[:, :], GBANK).then_inc(g_hi_done, 1)

                def elu_parts(b, fc):
                    j = DC * b + fc
                    act.wait_ge(h_done, j + 1)
                    if j >= 2:
                        act.wait_ge(h_sum, j - 1)
                    act.activation(ebuf[:, j % 2, :], HBANK[j % 2], ACT.Exp, bias=b0_col[:, fc:fc + 1])
                    act.activation(rbuf[:, j % 2, :], HBANK[j % 2], ACT.Relu, bias=b0_col[:, fc:fc + 1]).then_inc(h_act, 1)

                def h_hi_of(b, fc):
                    j = DC * b + fc
                    act.wait_ge(h_sum, j + 1)
                    act.copy(h_hi[:, b % 2, fc, :], hbuf[:, j % 2, :]).then_inc(h_hi_done, 1)

                def f_hi_of(b, m):
                    act.wait_ge(f_done, TB * b + m + 1)
                    act.copy(f_hi[:, m, :], RING[(2 * TB * b + m) % 3]).then_inc(f_hi_done, 1)

                def z_exp_of(b, n):
                    t = TB * b + n
                    act.wait_ge(ring_free, 2 * TB * b + TB + n + 1)
                    act.activation(zexp[:, t % 2, :], zbuf[:, t % 2, :], ACT.Exp).then_inc(z_exp, 1)

                act.wait_ge(ld_b, 32)
                for new, old in steps:
                    for k in range(TB):
                        if new is not None:
                            if k == 0:
                                pick_of(new, 0)
                            if k < TB - 1:
                                pick_of(new, k + 1)
                            if k == TB - 1:
                                g_hi_of(new)
                        if old is not None:
                            f_hi_of(old, k)
                    for k in range(TB + 1):
                        if new is not None and k < TB:
                            elu_parts(new, k)
                        if old is not None and k < TB:
                            z_exp_of(old, k)
                        if new is not None and k >= 1:
                            h_hi_of(new, k - 1)
                    if new in (0, 1):
                        bound_part(new)

            @block.vector
            def _(dve):
                chain = Chain(dve, dve_chain)
                dve.wait_ge(pool_const, 3)

                def norm_stats(b):
                    dve.wait_ge(ld_x[b], 16)
                    for i in range(TB):
                        ins = dve.bn_stats(stats[:, i, :], X[:, TB * b + i, :])
                    chain.link(ins)
                    for i in range(TB):
                        ins = dve.bn_aggr(mv[:, TB * b + i, :], stats[:, i, :])
                    chain.link(ins)
                    dve.tensor_scalar(ve[:, TB * b:TB * b + TB], mv[:, TB * b:TB * b + TB, 1], EPS, None,
                                      ALU.add).then_inc(var_ready, 1)

                def one_hot(t):
                    if t % TB == 0:
                        dve.wait_ge(rstd_ready, t // TB + 1)
                    if t >= 2:
                        dve.wait_ge(turned, t - 1)
                    a = adj[:, t % 2, :]
                    chain.link(dve.tensor_scalar(a, X[:, t, :], mv[:, t, 0:1], rstd[:, t:t + 1], ALU.subtract,
                                                 ALU.mult))
                    chain.link(dve.tensor_scalar(a, a, -1.0, None, ALU.add))
                    chain.link(dve.max(top[:, t, :], a))
                    dve.tensor_scalar(a, a, top[:, t, 0:1], None, ALU.is_ge).then_inc(hot_ready, 1)

                def split_ctx():
                    dve.wait_ge(ctx_hi_done, 1)
                    dve.tensor_tensor(ctx_lo[:, :, :], ctx_raw[:, :, :], ctx_hi[:, :, :].bitcast(F32),
                                      ALU.subtract).then_inc(ctx_lo_done, 1)
                    chain.link(dve.tensor_reduce(csum[:, :], ctx_raw[:, :, :], AX.X, ALU.add,
                                                 apply_absolute_value=True))

                def bound_part(layer):
                    dve.wait_ge(att_abs, layer + 1)
                    chain.link(dve.tensor_tensor(att[:, 0, :], att[:, 0, :], att[:, 1, :], ALU.add))
                    if layer == 0:
                        dve.wait_ge(w_lo_done, 1)
                    for k in ([0] if layer == 0 else range(1, 1 + DC)):
                        ins = dve.tensor_tensor(w_raw[:, k, :], w_raw[:, k, :], att[:, 0, :], ALU.mult)
                    chain.link(ins)
                    s = slice(0, 1) if layer == 0 else slice(1, 1 + DC)
                    chain.link(dve.tensor_reduce(wsum[:, s, :],
                                                 w_raw[:, s, :].rearrange("p k (h o) -> p k h o", h=H), AX.X, ALU.add,
                                                 apply_absolute_value=True))
                    if layer == 0:
                        dve.tensor_reduce(wmax[:, s], wsum[:, s, :], AX.X, ALU.max).then_inc(att_free, 1)
                    else:
                        dve.tensor_reduce(wmax[:, s], wsum[:, s, :], AX.X, ALU.max)

                def g_lo_of(b):
                    dve.wait_ge(g_hi_done, b + 1)
                    dve.tensor_tensor(g_lo[:, :], GBANK, g_hi[:, :].bitcast(F32), ALU.subtract).then_inc(g_lo_done, 1)

                def exp_less_1(b, fc):
                    j = DC * b + fc
                    dve.wait_ge(h_act, j + 1)
                    dve.tensor_reduce(hmax[:, j:j + 1], rbuf[:, j % 2, :], AX.X, ALU.max)
                    dve.tensor_scalar(ebuf[:, j % 2, :], ebuf[:, j % 2, :], 1.0, -1.0, ALU.min,
                                      ALU.add).then_inc(h_exp1, 1)

                def h_lo_of(b, fc):
                    j = DC * b + fc
                    dve.wait_ge(h_hi_done, j + 1)
                    dve.tensor_tensor(h_lo[:, b % 2, fc, :], hbuf[:, j % 2, :], h_hi[:, b % 2, fc, :].bitcast(F32),
                                      ALU.subtract).then_inc(h_lo_done, 1)

                def f_lo_of(b, m):
                    dve.wait_ge(f_hi_done, TB * b + m + 1)
                    dve.tensor_tensor(f_lo[:, m, :], RING[(2 * TB * b + m) % 3], f_hi[:, m, :].bitcast(F32),
                                      ALU.subtract).then_inc(ring_free, 1)

                def z_of(b, n):
                    t = TB * b + n
                    dve.wait_ge(o_done, t + 1)
                    if t >= 2:
                        dve.wait_ge(x_added, t - 1)
                    dve.tensor_tensor(zbuf[:, t % 2, :], RING[(2 * TB * b + TB + n) % 3], b1_row[:, :],
                                      ALU.add).then_inc(ring_free, 1)

                def elu_z(b, n):
                    k = (TB * b + n) % 2
                    dve.wait_ge(z_exp, TB * b + n + 1)
                    chain.link(dve.tensor_scalar(zexp[:, k, :], zexp[:, k, :], 1.0, -1.0, ALU.min, ALU.add))
                    dve.scalar_tensor_tensor(out=zbuf[:, k, :], in0=zbuf[:, k, :], scalar=0.0,
                                             in1=zexp[:, k, :], op0=ALU.max, op1=ALU.add).then_inc(y_ready, 1)

                def bounds():
                    chain.link(dve.tensor_scalar(tops[:, :, :], top[:, :, 0:2], MASK, None, ALU.mult))
                    chain.link(dve.tensor_tensor(gap[:, :], tops[:, :, 0], tops[:, :, 1], ALU.subtract))
                    chain.link(dve.tensor_scalar(gap[:, :], gap[:, :], GAP_MIN, None, ALU.is_ge))
                    chain.link(dve.tensor_reduce(per_part[:, 0:1], gap[:, :], AX.X, ALU.min))
                    chain.link(dve.tensor_reduce(per_part[:, 1:2], csum[:, :], AX.X, ALU.max))
                    chain.link(dve.tensor_copy(per_part[:, 2:3], wmax[:, 0:1]))
                    chain.link(dve.tensor_reduce(hcol[:, :], hmax[:, :].rearrange("p (b f) -> p f b", b=B), AX.X, ALU.max))
                    chain.link(dve.tensor_scalar(hcol[:, :], hcol[:, :], 1.0, None, ALU.max))
                    chain.link(dve.tensor_tensor(hw[:, :], hcol[:, :], wmax[:, 1:1 + DC], ALU.mult))
                    dve.tensor_reduce(per_part[:, 3:4], hw[:, :], AX.X, ALU.add).then_inc(bounds_ready, 1)

                def set_flag():
                    dve.wait_ge(bounds_turned, 1)
                    row = TBANK[0]
                    dve.tensor_reduce(red[:, 0:1], row[0:1, 0:P], AX.X, ALU.min)
                    dve.tensor_reduce(red[:, 1:2], row[0:1, P:2 * P], AX.X, ALU.max)
                    dve.tensor_reduce(red[:, 2:3], row[0:1, 2 * P:3 * P], AX.X, ALU.max)
                    chain.link(dve.tensor_reduce(red[:, 3:4], row[0:1, 3 * P:4 * P], AX.X, ALU.add))
                    chain.link(dve.tensor_tensor(red[:, 4:5], red[:, 1:2], red[:, 2:3], ALU.mult))
                    chain.link(dve.tensor_scalar(red[:, 5:7], red[:, 3:5], BOUND_MAX, None, ALU.is_le))
                    chain.link(dve.tensor_tensor(red[:, 5:6], red[:, 5:6], red[:, 6:7], ALU.mult))
                    chain.link(dve.tensor_tensor(red[:, 5:6], red[:, 5:6], red[:, 0:1], ALU.mult))
                    dve.tensor_copy(flag[:, :], red[:, 5:6])

                norm_stats(0)
                one_hot(0)
                one_hot(1)
                for new, old in steps:
                    if new is None:
                        bounds()
                    for k in range(TB):
                        if new is not None:
                            if k < 2:
                                one_hot(TB * new + k + 2)
                            if k == 0 and new == 0:
                                split_ctx()
                            if k == 2 and new + 1 < B:
                                norm_stats(new + 1)
                            if k == TB - 1:
                                g_lo_of(new)
                        if old is not None:
                            f_lo_of(old, k)
                    if new is None:
                        set_flag()
                    for k in range(TB + 1):
                        if old is not None and k < TB:
                            z_of(old, k)
                        if new is not None and k < TB:
                            exp_less_1(new, k)
                        if old is not None and k >= 1:
                            elu_z(old, k - 1)
                        if new is not None and k >= 1:
                            h_lo_of(new, k - 1)
                        if new is not None and new + 1 < B and k in (1, 2):
                            one_hot(TB * (new + 1) + k - 1)
                    if new in (0, 1):
                        bound_part(new)

        nc.clear_and_free_semaphores(sems)
        nc.all_engine_barrier()


class LoopChain:

    def __init__(self, eng, sem, per, turn):
        self.eng, self.sem, self.per, self.turn, self.n = eng, sem, per, turn, 0

    def link(self, ins):
        self.n += 1
        ins.then_inc(self.sem, 1)
        self.eng.wait_ge(self.sem, self.per * self.turn + self.n)

    def end(self):
        assert self.n == self.per, self.n


def gat_general(nc, outer, dram):
    X, ident, negh, ps = (outer[k] for k in ("X", "ident", "negh", "ps"))
    with ExitStack() as ctx:
        def sb(name, shape, dt=F32):
            return ctx.enter_context(nc.sbuf_tensor("gg_" + name, shape, dt))

        sems = []

        def sem(name):
            sems.append(nc.alloc_semaphore(name="gg_" + name))
            return sems[-1]

        cT = sb("ctxT", [P, 1, B * N])
        hT = sb("hT", [P, DC, B * N])
        w = sb("w", [P, 1 + DC, D])
        att = sb("att", [P, 2, 2, D])
        bias = sb("bias", [P, 2, D])
        pick_head = sb("pick_head", [H, H, P])
        lhs = sb("lhs", [P, DC, P])
        feat = sb("feat", [P, T, D])
        tmp = sb("tmp", [P, D])
        s_self = sb("s_self", [P, T, H])
        s_neigh = sb("s_neigh", [P, H])
        nT = sb("nT", [H, B * N])
        nTb = sb("nTb", [H, N])
        neigh = sb("neigh", [P, H, N])
        mv = sb("mv", [P, T, 2])
        st = sb("st", [P, 6])
        rstd = sb("rstd", [P, T])
        mask = sb("mask", [P, N])
        sc = sb("sc", [P, N])
        al = sb("al", [P, N])
        alT = sb("alT", [P, TB, P])
        nmax = sb("nmax", [P, 1])
        den = sb("den", [P, 1])
        z = sb("z", [P, D])
        ez = sb("ez", [P, D])

        ld, ld_x = sem("ld"), sem("ld_x")
        head_const, var_ready, rstd_ready, chain0 = sem("head_const"), sem("var_ready"), sem("rstd_ready"), sem("chain0")
        L = [{k: sem(f"{k}{layer}") for k in
              ("lhs_ready", "feat_done", "neigh_ready", "neigh_turned", "nT_ready", "spread", "spread_read",
               "sc_ready", "al_ready", "al_turned", "alT_ready", "mixed", "z_ready", "ez_ready", "y_ready", "y_turned",
               "chain_f", "chain_h", "chain_m", "chain_z", "mask_ready")} for layer in range(2)]

        with nc.Block() as block:
            @block.sync
            def _(sp):
                sp.dma_start(X[:, :, :].rearrange("p (b i) n -> p b i n", b=B),
                             dram["x"].rearrange("b p i n -> p b i n")).then_inc(ld_x, 16)
                sp.dma_start(cT[:, 0, :], dram["ctxT"]).then_inc(ld, 16)
                sp.dma_start(w[:, :, :], dram["gat_w"]).then_inc(ld, 16)
                for layer in range(2):
                    for j in range(2):
                        sp.dma_start(att[:, layer, j, :], dram[f"att{layer}"][j:j + 1, :].broadcast_to([P, D])
                                     ).then_inc(ld, 16)
                    sp.dma_start(bias[:, layer, :], dram[f"b{layer}"].broadcast_to([P, D])).then_inc(ld, 16)

            @block.gpsimd
            def _(pool):
                pool.memset(pick_head[:, :, :], 0.0).then_inc(head_const, 1)
                pool.wait_ge(head_const, 1)
                pool.affine_select(out=pick_head[:, :, :], in_=pick_head[:, :, :], compare_op=ALU.not_equal, fill=1.0,
                                   base=0, pattern=[[-1, H], [0, P]], channel_multiplier=1).then_inc(head_const, 1)
                pool.wait_ge(var_ready, 1)
                for c in range(B):
                    s = slice(TB * c, TB * c + TB)
                    pool.tensor_tensor(rstd[:, s], rstd[:, s], negh[:, 0:TB], ALU.pow).then_inc(rstd_ready, 1)

            @block.tensor
            def _(pe):
                pe.wait_ge(ld, 16 * 8)
                pe.wait_ge(head_const, 2)
                for layer in range(2):
                    q = L[layer]
                    first, chunks = (0, 1) if layer == 0 else (1, DC)
                    with pe.Fori(0, T) as t:
                        pe.wait_ge(q["lhs_ready"], t + 1)
                        for k in range(chunks):
                            ins = pe.matmul(ps[:, 0, :], lhs[:, k, :], w[:, first + k, :], start=(k == 0),
                                            stop=(k == chunks - 1))
                        ins.then_inc(q["feat_done"], 1)
                        pe.wait_ge(q["neigh_ready"], t + 1)
                        pe.transpose(ps[0:H, 1, 0:P], s_neigh[:, :], ident[:, :]).then_inc(q["neigh_turned"], 1)
                    with pe.Fori(0, B) as b:
                        for h in range(H):
                            pe.wait_ge(q["nT_ready"], H * b + (h + 1))
                            pe.matmul(ps[:, 2, :], pick_head[:, h, :], nTb[:, :], start=True, stop=True).then_inc(q["spread"], 1)
                        with pe.Fori(0, TB) as i:
                            with pe.Fori(0, H) as h:
                                n = (b * TB + i) * H + h
                                pe.wait_ge(q["al_ready"], n + 1)
                                for m in range(TB):
                                    ins = pe.transpose(ps[:, 3, P * m:P * m + P], al[:, P * m:P * m + P], ident[:, :])
                                ins.then_inc(q["al_turned"], 1)
                                pe.wait_ge(q["alT_ready"], n + 1)
                                for m in range(TB):
                                    ins = pe.matmul(ps[:, 4, 0:FO], alT[:, m, :],
                                                    feat[:, bass.ds(b * TB + m, 1), bass.ds(h * FO, FO)],
                                                    start=(m == 0), stop=(m == TB - 1))
                                ins.then_inc(q["mixed"], 1)
                            if layer == 0:
                                pe.wait_ge(q["y_ready"], b * TB + i + 1)
                                for m in range(DC):
                                    ins = pe.transpose(ps[:, 5, P * m:P * m + P], z[:, P * m:P * m + P], ident[:, :])
                                ins.then_inc(q["y_turned"], 1)

            @block.scalar
            def _(act):
                for layer in range(2):
                    q = L[layer]
                    with act.Fori(0, T) as t:
                        with act.Fori(0, H) as h:
                            n = t * H + h
                            act.wait_ge(q["sc_ready"], n + 1)
                            act.activation(al[:, :], sc[:, :], ACT.Exp, bias=nmax[:, 0:1],
                                           accum_out=den[:, 0:1]).then_inc(q["al_ready"], 1)
                        act.wait_ge(q["z_ready"], t + 1)
                        act.activation(ez[:, :], ez[:, :], ACT.Exp).then_inc(q["ez_ready"], 1)

            @block.vector
            def _(dve):
                chain = Chain(dve, chain0)
                dve.wait_ge(ld_x, 16)
                dve.wait_ge(ld, 16 * 8)
                for t in range(T):
                    chain.link(dve.bn_stats(st[:, :], X[:, t, :]))
                    chain.link(dve.bn_aggr(mv[:, t, :], st[:, :]))
                dve.tensor_scalar(rstd[:, :], mv[:, :, 1], EPS, None, ALU.add).then_inc(var_ready, 1)
                dve.wait_ge(rstd_ready, B)
                for layer in range(2):
                    q = L[layer]
                    src, chunks = (cT, 1) if layer == 0 else (hT, DC)
                    with dve.Fori(0, T) as t:
                        lc = LoopChain(dve, q["chain_f"], 6, t)
                        dve.tensor_copy(lhs[:, 0:chunks, :], src[:, :, bass.ds(t * P, P)]).then_inc(q["lhs_ready"], 1)
                        dve.wait_ge(q["feat_done"], t + 1)
                        lc.link(dve.tensor_copy(feat[:, bass.ds(t, 1), :], ps[:, 0:1, :]))
                        lc.link(dve.tensor_tensor(tmp[:, :], ps[:, 0, :], att[:, layer, 0, :], ALU.mult))
                        lc.link(dve.tensor_reduce(s_self[:, bass.ds(t, 1), :], tmp[:, :].rearrange("p (h o) -> p h o", h=H),
                                                  AX.X, ALU.add))
                        lc.link(dve.tensor_tensor(tmp[:, :], ps[:, 0, :], att[:, layer, 1, :], ALU.mult))
                        lc.link(dve.tensor_reduce(s_neigh[:, :], tmp[:, :].rearrange("p (h o) -> p h o", h=H), AX.X,
                                                  ALU.add))
                        dve.sem_inc(q["neigh_ready"], 1)
                        dve.wait_ge(q["neigh_turned"], t + 1)
                        lc.link(dve.tensor_copy(nT[:, bass.ds(t * P, P)], ps[0:H, 1, 0:P]))
                        lc.end()
                    with dve.Fori(0, B) as b:
                        dve.tensor_copy(nTb[:, :], nT[:, bass.ds(b * N, N)]).then_inc(q["nT_ready"], 1)
                        for h in range(H):
                            dve.wait_ge(q["spread"], H * b + (h + 1))
                            ins = dve.tensor_copy(neigh[:, h, :], ps[:, 2, :])
                            ins.then_inc(*((q["nT_ready"], 1) if h + 1 < H else (q["spread_read"], 1)))
                        with dve.Fori(0, TB) as i:
                            t = b * TB + i
                            dve.wait_ge(q["spread_read"], b + 1)
                            lc = LoopChain(dve, q["chain_m"], 2, t)
                            lc.link(dve.tensor_scalar(mask[:, :], X[:, bass.ds(t, 1), :], mv[:, bass.ds(t, 1), 0],
                                                      rstd[:, bass.ds(t, 1)], ALU.subtract, ALU.mult))
                            lc.link(dve.tensor_scalar(mask[:, :], mask[:, :], -1.0, None, ALU.add))
                            dve.tensor_scalar(mask[:, :], mask[:, :], MASK, None, ALU.mult).then_inc(q["mask_ready"], 1)
                            lc.end()
                            with dve.Fori(0, H) as h:
                                n = t * H + h
                                dve.wait_ge(q["mask_ready"], t + 1)
                                lc = LoopChain(dve, q["chain_h"], 6, n)
                                lc.link(dve.tensor_scalar(sc[:, :], neigh[:, bass.ds(h, 1), :],
                                                          s_self[:, bass.ds(t, 1), bass.ds(h, 1)], None, ALU.add))
                                lc.link(dve.scalar_tensor_tensor(out=sc[:, :], in0=sc[:, :], scalar=SLOPE, in1=sc[:, :],
                                                                 op0=ALU.mult, op1=ALU.max))
                                lc.link(dve.tensor_tensor(sc[:, :], sc[:, :], mask[:, :], ALU.add))
                                dve.tensor_reduce(nmax[:, 0:1], sc[:, :], AX.X, ALU.max,
                                                  negate=True).then_inc(q["sc_ready"], 1)
                                dve.wait_ge(q["al_turned"], n + 1)
                                dve.tensor_copy(alT[:, :, :], ps[:, 3, :].rearrange("p (m n) -> p m n", m=TB)
                                                ).then_inc(q["alT_ready"], 1)
                                lc.link(dve.reciprocal(den[:, :], den[:, :]))
                                dve.wait_ge(q["mixed"], n + 1)
                                lc.link(dve.tensor_scalar(z[:, bass.ds(h * FO, FO)], ps[:, 4, 0:FO], den[:, 0:1], None,
                                                          ALU.mult))
                                lc.link(dve.tensor_copy(tmp[:, 0:1], den[:, 0:1]))
                                lc.end()
                            lc = LoopChain(dve, q["chain_z"], 3 if layer == 0 else 4, t)
                            lc.link(dve.tensor_tensor(z[:, :], z[:, :], bias[:, layer, :], ALU.add))
                            dve.tensor_scalar(ez[:, :], z[:, :], 0.0, None, ALU.min).then_inc(q["z_ready"], 1)
                            dve.wait_ge(q["ez_ready"], t + 1)
                            lc.link(dve.tensor_scalar(ez[:, :], ez[:, :], -1.0, None, ALU.add))
                            if layer == 0:
                                dve.scalar_tensor_tensor(out=z[:, :], in0=z[:, :], scalar=0.0, in1=ez[:, :],
                                                         op0=ALU.max, op1=ALU.add).then_inc(q["y_ready"], 1)
                                dve.wait_ge(q["y_turned"], t + 1)
                                lc.link(dve.tensor_copy(hT[:, :, bass.ds(t * P, P)],
                                                        ps[:, 5, :].rearrange("p (m n) -> p m n", m=DC)))
                            else:
                                lc.link(dve.scalar_tensor_tensor(out=z[:, :], in0=z[:, :], scalar=0.0, in1=ez[:, :],
                                                                 op0=ALU.max, op1=ALU.add))
                                lc.link(dve.tensor_tensor(X[:, bass.ds(t, 1), :], X[:, bass.ds(t, 1), :], z[:, :], ALU.add))
                            lc.end()
        nc.clear_and_free_semaphores(sems)
        nc.all_engine_barrier()


class Units:

    def __init__(self, tag, outer, U, R, slots, w_hi, w_lo, x_hi, x_lo, los):
        ps = outer["ps"]
        self.U, self.R, self.slots, self.los = U, R, slots, los
        self.w_hi, self.w_lo, self.x_hi, self.x_lo = w_hi, w_lo, x_hi, x_lo
        self.raw_gu, self.raw_dn, self.ld_gu, self.ld_dn = (outer[k] for k in ("raw_gu", "raw_dn", "ld_gu", "ld_dn"))
        self.GATE = [ps[:, 0, :], ps[:, 1, :]]
        self.UP = [ps[:, 2, :], ps[:, 3, :]]
        self.ACC = [ps[:, 4 + i, :] for i in range(TB)]
        sem = outer["sem"]
        self.gate_up_hi, self.gate_up_lo = sem(tag + "gate_up_hi"), sem(tag + "gate_up_lo")
        self.down_hi, self.down_lo = sem(tag + "down_hi"), sem(tag + "down_lo")
        self.products = sem(tag + "products")
        self.silu, self.hid_made = sem(tag + "silu"), sem(tag + "hid_made")
        self.hid_hi_done, self.hid_lo_done = sem(tag + "hid_hi_done"), sem(tag + "hid_lo_done")
        self.acc_done, self.acc_free = sem(tag + "acc_done"), sem(tag + "acc_free")

    def at(self, u, c, r):
        return self.R * 4 * u + (self.R * c + r)

    def bank(self, c, r):
        return (self.R * c + r) % 2


    def load_gate_up(self, sp, src, u, r):
        sp.wait_ge(self.gate_up_lo, self.R * u + (r - self.slots + 1))
        sp.dma_start(self.raw_gu[:, r % self.slots, :, :],
                     src[bass.ds(self.R * u + r, 1)].rearrange("o p k n -> (o p) k n")
                     ).then_inc(self.ld_gu[r % self.slots], 16)

    def load_down(self, sp, src, u, r):
        sp.wait_ge(self.down_lo, self.R * u + (r - self.R + 1))
        sp.dma_start(self.raw_dn[:, r, :], src[bass.ds(self.R * u + r, 1)].rearrange("o p n -> (o p) n")
                     ).then_inc(self.ld_dn[r], 16)


    def act_gate_up(self, act, u, r, first=False):
        uses = self.R // self.slots
        act.wait_ge(self.ld_gu[r % self.slots], 16 * uses * u + 16 * (r // self.slots + 1))
        if not first:
            act.wait_ge(self.products, self.at(u - 1, 3, r) + 1)
        act.copy(self.w_hi[r][:, 0:2, :], self.raw_gu[:, r % self.slots, :, :]).then_inc(self.gate_up_hi, 1)

    def act_down(self, act, u, r, first=False):
        act.wait_ge(self.ld_dn[r], 16 * u + 16)
        if not first:
            act.wait_ge(self.acc_done, 16 * u)
        act.copy(self.w_hi[r][:, 2, :], self.raw_dn[:, r, :]).then_inc(self.down_hi, 1)

    def pool_gate_up(self, pool, u, r):
        pool.wait_ge(self.gate_up_hi, self.R * u + (r + 1))
        pool.tensor_tensor(self.w_lo[r][:, 0:2, :], self.raw_gu[:, r % self.slots, :, :],
                           self.w_hi[r][:, 0:2, :].bitcast(F32), ALU.subtract).then_inc(self.gate_up_lo, 1)

    def pool_down(self, pool, u, r):
        pool.wait_ge(self.down_hi, self.R * u + (r + 1))
        pool.tensor_tensor(self.w_lo[r][:, 2, :], self.raw_dn[:, r, :], self.w_hi[r][:, 2, :].bitcast(F32),
                           ALU.subtract).then_inc(self.down_lo, 1)


    def pe_gate_up(self, pe, u, c, tiles=None, first=False, between=None):
        for r in tiles or range(self.R):
            if c == 0:
                pe.wait_ge(self.gate_up_lo, self.R * u + (r + 1))
            if not (first and r < 2):
                pe.wait_ge(self.hid_made, self.at(u, c, r) - 1)
            for k, bank in ((0, self.GATE), (1, self.UP)):
                for d in range(DC):
                    w = slice(P * d, P * d + P)
                    ins = product3(pe, bank[self.bank(c, r)], self.w_hi[r][:, k, w], self.w_lo[r][:, k, w],
                                   self.x_hi[c][:, d, :], self.x_lo[c][:, d, :], d == 0, d == DC - 1)
                if k == 1:
                    ins.then_inc(self.products, 1)
                if between:
                    between()

    def pe_down(self, pe, u, c):
        pe.wait_ge(self.hid_lo_done, 4 * self.los * u + self.los * (c + 1))
        if c == 0:
            pe.wait_ge(self.down_lo, self.R * u + self.R)
        h = c % self.hid_hi.shape[1]
        for i in range(TB):
            pe.wait_ge(self.acc_free, 16 * u + (4 * c + i + 1))
            s = slice(P * i, P * i + P)
            for r in range(self.R):
                ins = product3(pe, self.ACC[i], self.hid_hi[:, h, r, s], self.hid_lo[:, h, r, s],
                               self.w_hi[r][:, 2, :], self.w_lo[r][:, 2, :], r == 0, r == self.R - 1)
            ins.then_inc(self.acc_done, 1)

    def pe_rest(self, pe):
        with pe.Fori(0, self.U - 1) as u:
            for c in range(4):
                self.pe_gate_up(pe, *((u, c + 1) if c < 3 else (u + 1, 0)))
                self.pe_down(pe, u, c)
        for c in range(4):
            if c < 3:
                self.pe_gate_up(pe, self.U - 1, c + 1)
            self.pe_down(pe, self.U - 1, c)


    def act_silu(self, act, u, c, r, sg, first=False):
        act.wait_ge(self.products, self.at(u, c, r) + 1)
        if not (first and r < 2):
            act.wait_ge(self.hid_made, self.at(u, c, r) - 1)
        k = self.bank(c, r)
        act.activation(sg[:, k, :], self.GATE[k], ACT.Silu).then_inc(self.silu, 1)

    def dve_hid(self, dve, u, c, r, sg, out):
        dve.wait_ge(self.silu, self.at(u, c, r) + 1)
        k = self.bank(c, r)
        dve.tensor_tensor(out, sg[:, k, :], self.UP[k], ALU.mult).then_inc(self.hid_made, 1)

    def dve_wait_acc(self, dve, u, c, i):
        dve.wait_ge(self.acc_done, 16 * u + (4 * c + i + 1))


def route(nc, outer, dram):
    X, ident, negh, ps, sem, rt = (outer[k] for k in ("X", "ident", "negh", "ps", "sem", "route"))
    J = 2 * T
    XN = 4
    with ExitStack() as ctx:
        def sb(name, shape, dt=F32):
            return ctx.enter_context(nc.sbuf_tensor("r_" + name, shape, dt))

        x_hi = sb("x_hi", [P, DC, N], F32R)
        x_lo = sb("x_lo", [P, DC, N], F32R)
        gw_raw = sb("gw_raw", [P, DC, E])
        gw_hi = sb("gw_hi", [P, DC, E], F32R)
        gw_lo = sb("gw_lo", [P, DC, E], F32R)
        lgT = outer["kv"]["c_raw"][0:E, :]
        lg = sb("lg", [P, T, E])
        lmax = sb("lmax", [P, T])
        ex = sb("ex", [P, T, E])
        gt = sb("gt", [P, T, E, E])
        eq = sb("eq", [P, T, E, E])
        before_e = sb("before_e", [P, E, E])
        rank = sb("rank", [P, T, E])
        keep = sb("keep", [P, T, E])
        den = sb("den", [P, T])
        tw = sb("tw", [P, T, E])
        before_p = sb("before_p", [P, P])
        ones = sb("ones", [P, P])
        totals = sb("totals", [P, T, E])
        cum = sb("cum", [P, 2, T, E])
        steps = sb("steps", [P, T])
        above = sb("above", [P, E, T])
        blocks = sb("blocks", [P, E])
        cumb = sb("cumb", [P, 2, E])
        start = sb("start", [P, E])
        pos = sb("pos", [P, T, E])
        low = sb("low", [P, T, E])
        high = sb("high", [P, T, E])
        pos2 = sb("pos2", [P, T, 2])
        at2 = sb("at2", [P, 2, J], I32)
        iota_i = sb("iota_i", [P, P], I32)
        iota_f = sb("iota_f", [P, P])
        tok_i = sb("tok_i", [P, T], I32)
        tok_f = sb("tok_f", [P, T])
        at2b = sb("at2b", [P, 2, J], BF16)
        iota_b = sb("iota_b", [P, P], BF16)
        tile_b = sb("tile_b", [P, T], BF16)
        lane_b = sb("lane_b", [P, 1], BF16)
        off_hot = sb("off_hot", [P, J, P], BF16)
        blk_hot = sb("blk_hot", [P, J, REAL], BF16)
        blk_tok = sb("blk_tok", [P, J, 2, REAL], BF16)
        tok_sum = sb("tok_sum", [P, REAL])
        tabf = sb("tabf", [1, 3, REAL])
        tcmp = sb("tcmp", [1, REAL, E])
        norm = Norm("r_", sb, sem, X, ident, negh, [ps[:, k, :] for k in (0, 1, 6, 7)], XN)
        LG, LT, PRE, TOT, IDX = ps[:, 2, :], ps[:, 3, :], ps[:, 4, :], ps[:, 5, :], ps[:, 6, :]

        ld_gw, gw_hi_done, gw_lo_done, const = sem("r_ld_gw"), sem("r_gw_hi_done"), sem("r_gw_lo_done"), sem("r_const")
        lg_done, lgT_done, lt_done, shifted, exped = (
            sem("r_" + n) for n in ("lg_done", "lgT_done", "lt_done", "shifted", "exped"))
        kept, counted, hot, idx_done, dve_chain = (
            sem("r_" + n) for n in ("kept", "counted", "hot", "idx_done", "dve_chain"))
        xn_stored = [sem(f"r_xn_stored{k}") for k in range(XN)]

        with nc.Block() as block:
            @block.sync
            def _(sp):
                sp.dma_start(gw_raw[:, :, :], dram["gate_w"]).then_inc(ld_gw, 16)
                for t in range(T):
                    sp.wait_ge(norm.xn_ready, t + 1)
                    sp.dma_start(rt["xn_dram"][P * t:P * t + P, :], norm.xn[:, t % XN, :]).then_inc(xn_stored[t % XN], 16)
                for k in range(XN):
                    sp.wait_ge(xn_stored[k], 16 * T // XN)

            @block.gpsimd
            def _(pool):
                pool.memset(before_e[:, :, :], 1.0).then_inc(const, 1)
                pool.memset(before_p[:, :], 1.0).then_inc(const, 1)
                pool.memset(ones[:, :], 1.0).then_inc(const, 1)
                pool.iota(iota_i[:, :], [[1, P]], base=0, channel_multiplier=0).then_inc(const, 1)
                pool.iota(tok_i[:, :], [[P, T]], base=0, channel_multiplier=1).then_inc(const, 1)
                pool.wait_ge(const, 5)
                pool.affine_select(out=before_e[:, :, :], in_=before_e[:, :, :], compare_op=ALU.is_gt, fill=0.0, base=0,
                                   pattern=[[1, E], [-1, E]], channel_multiplier=0).then_inc(const, 1)
                pool.affine_select(out=before_p[:, :], in_=before_p[:, :], compare_op=ALU.is_gt, fill=0.0, base=0,
                                   pattern=[[1, P]], channel_multiplier=-1).then_inc(const, 1)
                for c in range(B):
                    norm.pool_rstd(pool, c)
                pool.wait_ge(rt["gu_hi"], DC)
                pool.tensor_tensor(rt["gu_w_lo"][:, 0], rt["raw_gu"], rt["gu_w_hi"][:, 0].bitcast(F32),
                                   ALU.subtract)
                pool.wait_ge(rt["dn_hi"], 1)
                pool.tensor_tensor(rt["dn_w_lo"][:, 0], rt["raw_dn"], rt["dn_w_hi"][:, 0].bitcast(F32),
                                   ALU.subtract)

            @block.tensor
            def _(pe):
                for c in range(B):
                    for i in range(TB):
                        norm.pe_turn(pe, TB * c + i)
                    pe.wait_ge(norm.lo_done, TB * (c + 1))
                    if c == 0:
                        pe.wait_ge(gw_lo_done, 1)
                    if c >= 1:
                        pe.wait_ge(lgT_done, c)
                    for d in range(DC):
                        ins = product3(pe, LG[0:E, :], gw_hi[:, d, :], gw_lo[:, d, :], x_hi[:, d, :], x_lo[:, d, :],
                                       d == 0, d == DC - 1)
                    ins.then_inc(lg_done, 1)
                pe.wait_ge(lgT_done, B)
                for t in range(T):
                    ins = pe.transpose(LT[:, E * t:E * t + E], lgT[:, P * t:P * t + P], ident[0:E, 0:E])
                ins.then_inc(lt_done, 1)
                pe.wait_ge(const, 7)
                pe.wait_ge(kept, 1)
                k = keep[:, :, :].rearrange("p t e -> p (t e)")
                pe.matmul(PRE[:, 0:T * E], before_p[:, :], k, start=True, stop=True)
                pe.matmul(TOT[:, 0:T * E], ones[:, :], k, start=True, stop=True).then_inc(counted, 1)
                pe.wait_ge(hot, 1)
                for j in range(J):
                    ins = pe.matmul(IDX[:, 0:2 * REAL], off_hot[:, j, :],
                                    blk_tok[:, j, :, :].rearrange("p w b -> p (w b)"), start=(j == 0),
                                    stop=(j == J - 1))
                ins.then_inc(idx_done, 1)

            @block.scalar
            def _(act):
                act.wait_ge(ld_gw, 16)
                act.copy(gw_hi[:, :, :], gw_raw[:, :, :]).then_inc(gw_hi_done, 1)
                for c in range(B):
                    for i in range(TB):
                        if i == 0 and c >= 1:
                            act.wait_ge(lg_done, c)
                        norm.act_hi(act, TB * c + i, x_hi[:, :, P * i:P * i + P])
                    act.wait_ge(lg_done, c + 1)
                    act.copy(lgT[:, N * c:N * c + N], LG[0:E, :]).then_inc(lgT_done, 1)
                    if c == B - 1:
                        act.wait_ge(rt["ld_gu"], 16 * DC)
                        act.copy(rt["gu_w_hi"][:, 0], rt["raw_gu"]).then_inc(rt["gu_hi"], DC)
                        act.wait_ge(rt["ld_dn"], 16 * RE)
                        act.copy(rt["dn_w_hi"][:, 0], rt["raw_dn"]).then_inc(rt["dn_hi"], 1)
                act.wait_ge(shifted, 1)
                act.activation(ex[:, :, :], lg[:, :, :], ACT.Exp).then_inc(exped, 1)

            @block.vector
            def _(dve):
                chain = Chain(dve, dve_chain)
                link = chain.link

                def per_e(a, shape=(P, T, E)):
                    return a.unsqueeze(2).broadcast_to(list(shape))

                norm.dve_stats(chain, 0)
                dve.wait_ge(gw_hi_done, 1)
                dve.tensor_tensor(gw_lo[:, :, :], gw_raw[:, :, :], gw_hi[:, :, :].bitcast(F32),
                                  ALU.subtract).then_inc(gw_lo_done, 1)
                for c in range(B):
                    if c + 1 < B:
                        norm.dve_stats(chain, c + 1)
                    for i in range(TB + 2):
                        t = TB * c + i
                        if i < TB:
                            if t >= XN:
                                dve.wait_ge(xn_stored[t % XN], 16 * (t // XN))
                            norm.dve_norm(dve, t)
                        if i >= 2:
                            norm.dve_lo(dve, t - 2, x_hi[:, :, P * (i - 2):P * (i - 1)], x_lo[:, :, P * (i - 2):P * (i - 1)])
                dve.wait_ge(lt_done, 1)
                link(dve.tensor_copy(lg[:, :, :], LT[:, 0:T * E].rearrange("p (t e) -> p t e", e=E)))
                link(dve.tensor_reduce(lmax[:, :], lg[:, :, :], AX.X, ALU.max))
                of_e = lg[:, :, :].unsqueeze(3).broadcast_to([P, T, E, E])
                of_j = lg[:, :, :].unsqueeze(2).broadcast_to([P, T, E, E])
                dve.tensor_tensor(gt[:, :, :, :], of_j, of_e, ALU.is_gt)
                link(dve.tensor_tensor(eq[:, :, :, :], of_j, of_e, ALU.is_equal))
                dve.tensor_tensor(lg[:, :, :], lg[:, :, :], per_e(lmax[:, :]), ALU.subtract).then_inc(shifted, 1)
                dve.wait_ge(const, 7)
                link(dve.tensor_tensor(eq[:, :, :, :], eq[:, :, :, :],
                                       before_e[:, :, :].unsqueeze(1).broadcast_to([P, T, E, E]), ALU.mult))
                link(dve.tensor_tensor(gt[:, :, :, :], gt[:, :, :, :], eq[:, :, :, :], ALU.add))
                link(dve.tensor_reduce(rank[:, :, :], gt[:, :, :, :], AX.X, ALU.add))
                dve.tensor_scalar(keep[:, :, :], rank[:, :, :], 1.5, None, ALU.is_le).then_inc(kept, 1)
                dve.wait_ge(kept, 1)
                dve.wait_ge(exped, 1)
                link(dve.tensor_tensor(ex[:, :, :], keep[:, :, :], ex[:, :, :], ALU.mult))
                link(dve.tensor_reduce(den[:, :], ex[:, :, :], AX.X, ALU.add))
                link(dve.reciprocal(den[:, :], den[:, :]))
                link(dve.tensor_tensor(tw[:, :, :], ex[:, :, :], per_e(den[:, :]), ALU.mult))
                link(dve.tensor_copy(iota_f[:, :], iota_i[:, :]))
                link(dve.tensor_copy(tok_f[:, :], tok_i[:, :]))
                link(dve.tensor_scalar(steps[:, :], iota_f[:, 0:T], float(P), None, ALU.mult))
                dve.tensor_copy(iota_b[:, :], iota_f[:, :])
                dve.tensor_copy(lane_b[:, :], tok_f[:, 0:1])
                link(dve.tensor_copy(tile_b[:, :], steps[:, :]))
                dve.wait_ge(counted, 1)
                link(dve.tensor_copy(totals[:, :, :], TOT[:, 0:T * E].rearrange("p (t e) -> p t e", e=E)))
                link(dve.tensor_copy(cum[:, 0, :, :], totals[:, :, :]))
                k, a = 1, 0
                while k < T:
                    dve.tensor_copy(cum[:, 1 - a, 0:k, :], cum[:, a, 0:k, :])
                    link(dve.tensor_tensor(cum[:, 1 - a, k:T, :], cum[:, a, k:T, :], cum[:, a, 0:T - k, :], ALU.add))
                    k, a = 2 * k, 1 - a
                link(dve.tensor_tensor(above[:, :, :], cum[:, a, T - 1, :].unsqueeze(2).broadcast_to([P, E, T]),
                                       steps[:, :].unsqueeze(1).broadcast_to([P, E, T]), ALU.is_gt))
                link(dve.tensor_reduce(blocks[:, :], above[:, :, :], AX.X, ALU.add))
                link(dve.tensor_scalar(blocks[:, :], blocks[:, :], 1.0, None, ALU.max))
                link(dve.tensor_copy(cumb[:, 0, :], blocks[:, :]))
                k, z = 1, 0
                while k < E:
                    dve.tensor_copy(cumb[:, 1 - z, 0:k], cumb[:, z, 0:k])
                    link(dve.tensor_tensor(cumb[:, 1 - z, k:E], cumb[:, z, k:E], cumb[:, z, 0:E - k], ALU.add))
                    k, z = 2 * k, 1 - z
                link(dve.tensor_tensor(start[:, :], cumb[:, z, :], blocks[:, :], ALU.subtract))
                link(dve.tensor_tensor(pos[:, :, :], cum[:, a, :, :], totals[:, :, :], ALU.subtract))
                link(dve.tensor_tensor(pos[:, :, :], pos[:, :, :], PRE[:, 0:T * E].rearrange("p (t e) -> p t e", e=E),
                                       ALU.add))
                link(dve.tensor_scalar(cumb[:, z, :], start[:, :], float(P), 1.0, ALU.mult, ALU.add))
                link(dve.tensor_tensor(pos[:, :, :], pos[:, :, :], cumb[:, z, :].unsqueeze(1).broadcast_to([P, T, E]),
                                       ALU.add))
                link(dve.tensor_tensor(high[:, :, :], keep[:, :, :], pos[:, :, :], ALU.mult))
                link(dve.tensor_scalar(high[:, :, :], high[:, :, :], -1.0, None, ALU.add))
                link(dve.tensor_scalar(low[:, :, :], keep[:, :, :], -BIG, BIG - 1.0, ALU.mult, ALU.add))
                link(dve.tensor_tensor(low[:, :, :], low[:, :, :], pos[:, :, :], ALU.add))
                link(dve.tensor_reduce(pos2[:, :, 0], low[:, :, :], AX.X, ALU.min))
                link(dve.tensor_reduce(pos2[:, :, 1], high[:, :, :], AX.X, ALU.max))
                link(dve.tensor_copy(rt["slot"][:, :], pos2[:, :, :].rearrange("p t k -> p (t k)")))
                dve.tensor_scalar(at2[:, 0, :], rt["slot"][:, :], 7, None, ALU.arith_shift_right)
                link(dve.tensor_scalar(at2[:, 1, :], rt["slot"][:, :], P - 1, None, ALU.bitwise_and))
                link(dve.tensor_copy(at2b[:, :, :], at2[:, :, :]))
                link(dve.tensor_tensor(blk_hot[:, :, :], at2b[:, 0, :].unsqueeze(2).broadcast_to([P, J, REAL]),
                                       iota_b[:, 0:REAL].unsqueeze(1).broadcast_to([P, J, REAL]), ALU.is_equal))
                dve.tensor_tensor(blk_tok[:, :, 0, :].rearrange("p (t k) b -> p t k b", k=2),
                                  blk_hot[:, :, :].rearrange("p (t k) b -> p t k b", k=2),
                                  tile_b[:, :].unsqueeze(2).unsqueeze(3).broadcast_to([P, T, 2, REAL]), ALU.mult)
                dve.tensor_tensor(blk_tok[:, :, 1, :], blk_hot[:, :, :],
                                  lane_b[:, :].unsqueeze(2).broadcast_to([P, J, REAL]), ALU.mult)
                dve.tensor_tensor(off_hot[:, :, :], at2b[:, 1, :].unsqueeze(2).broadcast_to([P, J, P]),
                                  iota_b[:, :].unsqueeze(1).broadcast_to([P, J, P]), ALU.is_equal).then_inc(hot, 1)
                link(dve.tensor_tensor(low[:, :, :], low[:, :, :], per_e(pos2[:, :, 0]), ALU.is_equal))
                link(dve.tensor_tensor(low[:, :, :], low[:, :, :], tw[:, :, :], ALU.mult))
                link(dve.tensor_reduce(rt["weight"][:, :, 0], low[:, :, :], AX.X, ALU.add))
                link(dve.tensor_tensor(high[:, :, :], high[:, :, :], per_e(pos2[:, :, 1]), ALU.is_equal))
                link(dve.tensor_tensor(high[:, :, :], high[:, :, :], tw[:, :, :], ALU.mult))
                link(dve.tensor_reduce(rt["weight"][:, :, 1], high[:, :, :], AX.X, ALU.add))
                row_b = iota_f[0:1, 0:REAL].unsqueeze(2).broadcast_to([1, REAL, E])
                row_s = start[0:1, :].unsqueeze(1).broadcast_to([1, REAL, E])
                link(dve.tensor_tensor(tcmp[:, :, :], row_b, row_s, ALU.is_ge))
                link(dve.tensor_reduce(tabf[:, 0, :], tcmp[:, :, :], AX.X, ALU.add))
                link(dve.tensor_tensor(tcmp[:, :, :], row_b, row_s, ALU.is_equal))
                link(dve.tensor_reduce(tabf[:, 1, :], tcmp[:, :, 0:E - 1], AX.X, ALU.add))
                link(dve.tensor_reduce(tabf[:, 2, :], tcmp[:, :, 0:E - 2], AX.X, ALU.add))
                for row, bit in ((1, NEXT), (2, MORE)):
                    link(dve.scalar_tensor_tensor(out=tabf[:, 0, :], in0=tabf[:, row, :], scalar=float(bit),
                                                  in1=tabf[:, 0, :], op0=ALU.mult, op1=ALU.add))
                dve.tensor_copy(rt["table"][:, :], tabf[:, 0, :])
                dve.memset(rt["token"][:, REAL:REAL + 1], 0)
                dve.wait_ge(idx_done, 1)
                link(dve.tensor_copy(tok_sum[:, :], IDX[:, 0:REAL]))
                link(dve.tensor_tensor(tok_sum[:, :], tok_sum[:, :], IDX[:, REAL:2 * REAL], ALU.add))
                dve.tensor_copy(rt["token"][:, 0:REAL], tok_sum[:, :])


def moe(nc, outer, dram):
    X, ident, ps, sem, rt = (outer[k] for k in ("X", "ident", "ps", "sem", "route"))
    FP = RE * P
    kd = outer["kv"]
    with ExitStack() as ctx:
        def sb(name, shape, dt=F32):
            return ctx.enter_context(nc.sbuf_tensor("m_" + name, shape, dt))

        rows = [sb(f"rows{k}", [P, D]) for k in range(4)]
        index = [sb(f"index{k}", [P, 1], I32) for k in range(4)]
        spacer = sb("spacer", [P, 1])
        xT_hi = sb("xT_hi", [P, 2, DC, P], F32R)
        xT_lo = sb("xT_lo", [P, 2, DC, P], F32R)
        sg = sb("sg", [P, 2, FE])
        hid = sb("hid", [P, 2, FP])
        hT_hi = sb("hT_hi", [P, 2, RE, P], F32R)
        hT_lo = sb("hT_lo", [P, 2, RE, P], F32R)
        y = sb("y", [P, 2, D])

        GATE = [ps[:, 0, 0:FE], ps[:, 1, 0:FE]]
        UP = [ps[:, 2, 0:FE], ps[:, 3, 0:FE]]
        XB, HB = ps[:, 4, :], ps[:, 5, 0:FP]
        ACC = [ps[:, 6, :], ps[:, 7, :]]

        got = [sem(f"m_got{k}") for k in range(4)]
        x_turned, x_hi_done, x_lo_done = sem("m_x_turned"), sem("m_x_hi_done"), sem("m_x_lo_done")
        gate_done, up_done, silu = sem("m_gate_done"), sem("m_up_done"), sem("m_silu")
        hid_made = sem("m_hid_made")
        h_turned, h_hi_done, h_lo_done = sem("m_h_turned"), sem("m_h_hi_done"), sem("m_h_lo_done")
        down_done = sem("m_down_done")
        y_done = sem("m_y_done")
        stored = [sem(f"m_stored{k}") for k in range(2)]
        gu_lo, dn_lo = sem("m_gu_lo"), sem("m_dn_lo")
        index_ready = sem("m_index_ready")
        gu_hi, dn_hi, ld_gu, ld_dn = rt["gu_hi"], rt["dn_hi"], rt["ld_gu"], rt["ld_dn"]

        def table(eng, g):
            at = slice(g, g + 1) if isinstance(g, int) else bass.ds(g, 1)
            return eng.value_load(rt["table"][0:1, at], min_val=0, max_val=2 * MORE - 1)

        def number(entry):
            return (entry & (NEXT - 1)).with_bounds(min_val=1, max_val=E)

        def other(entry):
            return bass.ds(entry & 1, 1)

        def pipeline(eng, body):
            with eng.Fori(0, (REAL - 1) // 4) as i:
                for j in range(4):
                    body(4 * i + j + 1, j, i)
            i = (REAL - 1) // 4
            for j in range((REAL - 1) % 4):
                body(4 * i + j + 1, j, i)

        def is_last(g):
            return isinstance(g, int) and g == REAL - 1

        with nc.Block() as block:
            @block.sync
            def _(sp):
                def reload(e1):
                    sp.wait_ge(gu_lo, e1 + 1)
                    load_expert(sp, rt, dram, e1 + 1, down=False)
                    sp.wait_ge(dn_lo, e1 + 1)
                    load_expert(sp, rt, dram, e1 + 1, gate_up=False)

                def body(g, j, i):
                    k = j % 2
                    sp.wait_ge(y_done, g + 2)
                    at = slice((g - 1) * P, g * P) if isinstance(g, int) else bass.ds((g - 1) * P, P)
                    sp.dma_start(rt["y_dram"][at, :], y[:, k, :]).then_inc(stored[k], 16)
                    entry = table(sp, g)
                    with sp.If((entry & MORE) != 0):
                        reload((entry & (NEXT - 1)).with_bounds(min_val=1, max_val=E - 2))

                load_expert(sp, rt, dram, 1)
                sp.dma_start(kd["wk_raw"][:, :], dram["wkT"]).then_inc(kd["loaded"], 16)
                sp.dma_start(kd["bk"][:, :], dram["bk"]).then_inc(kd["loaded"], 16)
                sp.dma_start(kd["c_raw"][:, :], dram["ctxT"]).then_inc(kd["loaded"], 16)
                for k in range(2):
                    sp.sem_inc(stored[k], 16)
                reload(1)
                pipeline(sp, body)
                sp.wait_ge(y_done, REAL + 2)
                sp.dma_start(rt["y_dram"][(REAL - 1) * P:REAL * P, :], y[:, 0, :]).then_inc(stored[0], 16)

            @block.gpsimd
            def _(pool):
                def gather(g, b):
                    at = slice(g, g + 1) if isinstance(g, int) else bass.ds(g, 1)
                    pool.tensor_copy(index[b][:, :], rt["token"][:, at]).then_inc(index_ready, 1)
                    pool.wait_ge(index_ready, g + 1)
                    pool.tensor_tensor(spacer[:, :], ident[:, 0:1], ident[:, 0:1], ALU.mult)
                    pool.indirect_dma_start(out=rows[b][:, :], out_offset=None, in_=rt["xn_dram"],
                                            in_offset=bass.IndirectOffsetOnAxis(ap=index[b][:, 0:1], axis=0)
                                            ).then_inc(got[b], 16)

                def split_down(e1, at):
                    pool.wait_ge(dn_hi, e1 + 1)
                    pool.tensor_tensor(rt["dn_w_lo"][:, at], rt["raw_dn"], rt["dn_w_hi"][:, at].bitcast(F32),
                                       ALU.subtract).then_inc(dn_lo, 1)

                def body(g, j, i):
                    if not isinstance(g, int):
                        pool.wait_ge(x_turned, g)
                        gather(g + 3, j % 4)
                    entry = table(pool, g)
                    with pool.If((entry & NEXT) != 0):
                        split_down(number(entry), other(entry))

                pool.sem_inc(dn_lo, 1)
                for g in range(4):
                    gather(g, g)
                split_down(1, slice(1, 2))
                pipeline(pool, body)
                pool.wait_ge(got[REAL % 4], 16 * (REAL // 4 + 1))
                for k in range(2):
                    pool.wait_ge(stored[k], 16 * (1 + (REAL + 1 - k) // 2))

            @block.tensor
            def _(pe):
                def turn_rows(b, loads):
                    pe.wait_ge(got[b], 16 * loads)
                    for d in range(DC):
                        ins = pe.transpose(XB[:, P * d:P * d + P], rows[b][:, P * d:P * d + P], ident[:, :])
                    ins.then_inc(x_turned, 1)

                def product(bank, k, w, which):
                    for d in range(DC):
                        ins = product3(pe, bank[k], xT_hi[:, k, d, :], xT_lo[:, k, d, :],
                                       rt["gu_w_hi"][:, w, d, which, :], rt["gu_w_lo"][:, w, d, which, :],
                                       d == 0, d == DC - 1)
                    return ins

                def turn_hidden(g, k):
                    pe.wait_ge(hid_made, g + 3)
                    for r in range(RE):
                        ins = pe.transpose(HB[:, P * r:P * r + P], hid[:, k, P * r:P * r + P], ident[:, :])
                    ins.then_inc(h_turned, 1)

                def down(g, k, entry):
                    w = bass.ds((entry + 1) & 1, 1)
                    pe.wait_ge(h_lo_done, g + 1)
                    pe.wait_ge(y_done, g + 1)
                    pe.wait_ge(dn_lo, number(entry))
                    for r in range(RE):
                        ins = product3(pe, ACC[k], hT_hi[:, k, r, :], hT_lo[:, k, r, :], rt["dn_w_hi"][:, w, r, :],
                                       rt["dn_w_lo"][:, w, r, :], r == 0, r == RE - 1)
                    ins.then_inc(down_done, 1)

                entries = {}

                def body(g, j, i):
                    k = (j + 1) % 2
                    if j == 0:
                        entries["last"] = table(pe, g - 1)
                    entry, last = table(pe, g), entries["last"]
                    entries["last"] = entry
                    w = bass.ds((entry + 1) & 1, 1)
                    pe.wait_ge(gu_lo, number(entry))
                    pe.wait_ge(x_lo_done, g + 1)
                    pe.wait_ge(hid_made, g + 1)
                    product(GATE, k, w, 0).then_inc(gate_done, 1)
                    turn_hidden(g - 1, 1 - k)
                    product(UP, k, w, 1).then_inc(up_done, 1)
                    if not is_last(g):
                        turn_rows((j + 2) % 4, i + (j + 2) // 4 + 1)
                    down(g - 1, 1 - k, last)

                turn_rows(0, 1)
                pe.wait_ge(x_lo_done, 1)
                product(GATE, 0, slice(0, 1), 0).then_inc(gate_done, 1)
                product(UP, 0, slice(0, 1), 1).then_inc(up_done, 1)
                turn_rows(1, 1)
                pipeline(pe, body)
                turn_hidden(REAL - 1, 0)
                down(REAL - 1, 0, entries["last"])

            @block.scalar
            def _(act):
                def act_silu(g, k):
                    act.wait_ge(gate_done, g + 1)
                    act.activation(sg[:, k, :], GATE[k], ACT.Silu).then_inc(silu, 1)

                def hidden_hi(g, k):
                    act.wait_ge(h_turned, g + 1)
                    act.copy(hT_hi[:, k, :, :], HB.rearrange("p (r n) -> p r n", r=RE)).then_inc(h_hi_done, 1)

                def rows_hi(g, k):
                    act.wait_ge(x_turned, g + 1)
                    act.copy(xT_hi[:, k, :, :], XB.rearrange("p (d n) -> p d n", d=DC)).then_inc(x_hi_done, 1)

                def result(g, k, stores):
                    act.wait_ge(down_done, g + 1)
                    act.wait_ge(stored[k], 16 * stores)
                    act.copy(y[:, k, :], ACC[k]).then_inc(y_done, 1)

                def split(e1, at, ds):
                    act.wait_ge(ld_gu, 16 * DC * e1 + 16 * DC)
                    for d in ds:
                        act.copy(rt["gu_w_hi"][:, at, d], rt["raw_gu"][:, d].unsqueeze(1)).then_inc(gu_hi, 1)

                def body(g, j, i):
                    k = (j + 1) % 2
                    entry = table(act, g)
                    act_silu(g, k)
                    hidden_hi(g - 1, 1 - k)
                    with act.If((entry & NEXT) != 0):
                        split(number(entry), other(entry), (0, 1))
                    if not is_last(g):
                        rows_hi(g + 1, 1 - k)
                    with act.If((entry & NEXT) != 0):
                        split(number(entry), other(entry), (2, 3))
                    result(g - 1, 1 - k, 2 * i + j // 2 + 1)

                act.sem_inc(y_done, 2)
                rows_hi(0, 0)
                act_silu(0, 0)
                rows_hi(1, 1)
                split(1, slice(1, 2), range(DC))
                pipeline(act, body)
                hidden_hi(REAL - 1, 0)
                act.wait_ge(kd["loaded"], 48)
                for name in ("wk", "c"):
                    act.copy(kd[name + "_hi"][:, :], kd[name + "_raw"][:, :]).then_inc(kd["hi"], 1)
                result(REAL - 1, 0, (REAL - 1) // 2 + 1)

            @block.vector
            def _(dve):
                def rows_lo(g, k):
                    dve.wait_ge(x_hi_done, g + 1)
                    dve.tensor_tensor(xT_lo[:, k, :, :], XB.rearrange("p (d n) -> p d n", d=DC),
                                      xT_hi[:, k, :, :].bitcast(F32), ALU.subtract).then_inc(x_lo_done, 1)

                def hidden(g, k):
                    dve.wait_ge(silu, g + 1)
                    dve.wait_ge(up_done, g + 1)
                    dve.tensor_tensor(hid[:, k, 0:FE], sg[:, k, :], UP[k], ALU.mult).then_inc(hid_made, 1)

                def hidden_lo(g, k):
                    dve.wait_ge(h_hi_done, g + 1)
                    dve.tensor_tensor(hT_lo[:, k, :, :], HB.rearrange("p (r n) -> p r n", r=RE),
                                      hT_hi[:, k, :, :].bitcast(F32), ALU.subtract).then_inc(h_lo_done, 1)

                def split(e1, at):
                    for d in range(DC):
                        dve.wait_ge(gu_hi, DC * e1 + d + 1)
                        ins = dve.tensor_tensor(rt["gu_w_lo"][:, at, d], rt["raw_gu"][:, d].unsqueeze(1),
                                                rt["gu_w_hi"][:, at, d].bitcast(F32), ALU.subtract)
                    ins.then_inc(gu_lo, 1)

                def split_down(e1, at):
                    dve.wait_ge(ld_dn, 16 * RE * e1 + 16 * RE)
                    dve.tensor_copy(rt["dn_w_hi"][:, at], rt["raw_dn"].unsqueeze(1)).then_inc(dn_hi, 1)

                def body(g, j, i):
                    k = (j + 1) % 2
                    entry = table(dve, g)
                    hidden_lo(g - 1, 1 - k)
                    hidden(g, k)
                    if not is_last(g):
                        rows_lo(g + 1, 1 - k)
                    with dve.If((entry & NEXT) != 0):
                        split(number(entry), other(entry))
                        dve.wait_ge(down_done, g)
                        split_down(number(entry), other(entry))

                dve.memset(hid[:, :, :], 0.0).then_inc(hid_made, 2)
                dve.wait_ge(hid_made, 2)
                dve.sem_inc(gu_lo, 1)
                rows_lo(0, 0)
                hidden(0, 0)
                rows_lo(1, 1)
                split(1, slice(1, 2))
                split_down(1, slice(1, 2))
                pipeline(dve, body)
                hidden_lo(REAL - 1, 0)
                for n, name in enumerate(("wk", "c")):
                    dve.wait_ge(kd["hi"], n + 1)
                    dve.tensor_tensor(kd[name + "_lo"][:, :], kd[name + "_raw"][:, :],
                                      kd[name + "_hi"][:, :].bitcast(F32), ALU.subtract)


def image_attention(nc, outer, dram):
    X, ident, negh, ps, sem, rt = (outer[k] for k in ("X", "ident", "negh", "ps", "sem", "route"))
    with ExitStack() as ctx:
        def sb(name, shape, dt=F32):
            return ctx.enter_context(nc.sbuf_tensor("a_" + name, shape, dt))

        pair = [sb(f"pair{k}", [P, D]) for k in range(2 * TB)]
        x_hi = sb("x_hi", [P, 2, DC, N], F32R)
        x_lo = sb("x_lo", [P, 2, DC, N], F32R)
        kd = outer["kv"]
        c_raw, c_hi, c_lo, wk_hi, wk_lo, bk = (kd[k] for k in ("c_raw", "c_hi", "c_lo", "wk_hi", "wk_lo", "bk"))
        gamma = sb("gamma", [P, N])
        beta = sb("beta", [P, N])
        kvT = sb("kvT", [P, N])
        kvT_hi = sb("kvT_hi", [P, B, N], F32R)
        kvT_lo = sb("kvT_lo", [P, B, N], F32R)
        kv_hi = sb("kv_hi", [P, B, TB, CTX], F32R)
        kv_lo = sb("kv_lo", [P, B, TB, CTX], F32R)
        o_hi = sb("o_hi", [P, N], F32R)
        o_lo = sb("o_lo", [P, N], F32R)
        st = sb("st", [P, 2, 6])
        mv = sb("mv", [P, T, 2])
        ve = sb("ve", [P, T])
        rs = sb("rs", [P, T])
        y = c_raw[:, 0:3 * N].rearrange("p (k n) -> p k n", k=3)
        nmax = sb("nmax", [P, T])
        prob = sb("prob", [P, 2, N])
        den = sb("den", [P, T])
        rden = sb("rden", [P, T])
        norm = Norm("a_", sb, sem, X, ident, negh, [ps[:, 0, :], ps[:, 1, :]])
        fnorm, u = outer["ffn_norm"], outer["units"]
        fx_hi, fx_lo = u.x_hi[0], u.x_lo[0]
        KVB, KTB, OB = ps[:, 2, :], ps[:, 3, :], ps[:, 4, :]
        SIM = [ps[:, 5, :], ps[:, 6, :], ps[:, 7, :]]

        ld_row = sem("a_ld_row")
        kvT_done, kvT_made, kvT_hi_done, kvT_lo_done = (
            sem("a_" + n) for n in ("kvT_done", "kvT_made", "kvT_hi_done", "kvT_lo_done"))
        kv_turned, kv_hi_done, kv_lo_done = sem("a_kv_turned"), sem("a_kv_hi_done"), sem("a_kv_lo_done")
        o_done, o_hi_done, o_lo_done = sem("a_o_done"), sem("a_o_hi_done"), sem("a_o_lo_done")
        sim_done, sim_free = sem("a_sim_done"), sem("a_sim_free")
        var_ready, rs_ready, y_ready, prob_ready, x_added = (
            sem("a_" + n) for n in ("svar_ready", "srs_ready", "y_ready", "prob_ready", "x_added"))
        dve_chain = sem("a_dve_chain")
        paired = [sem(f"a_paired{k}") for k in range(2 * TB)]
        added, scaled, summed = sem("a_added"), sem("a_scaled"), sem("a_summed")

        with nc.Block() as block:
            @block.sync
            def _(sp):
                sp.dma_start(gamma[:, :], dram["gamma"].broadcast_to([P, N])).then_inc(ld_row, 16)
                sp.dma_start(beta[:, :], dram["beta"].broadcast_to([P, N])).then_inc(ld_row, 16)
                sp.wait_ge(added, 4 * TB)
                for r in range(2):
                    sp.dma_start(outer["raw_gu"][:, r, :, :], dram["ffn_gu"][r]).then_inc(outer["ld_gu"][r], 16)
                for r in range(RQ):
                    sp.dma_start(outer["raw_dn"][:, r, :], dram["ffn_dn"][r]).then_inc(outer["ld_dn"][r], 16)

            @block.gpsimd
            def _(pool):
                def gather(c, i):
                    for k in range(2):
                        if c in (1, 2):
                            pool.wait_ge(added, TB * (2 * c - 2 + k) + i + 1)
                        if c == 3:
                            pool.wait_ge(summed, 2 * i + k + 1)
                        j = 2 * (TB * c + i) + k
                        pool.indirect_dma_start(out=pair[2 * i + k][:, :], out_offset=None, in_=rt["y_dram"],
                                                in_offset=bass.IndirectOffsetOnAxis(ap=rt["slot"][:, j:j + 1], axis=0)
                                                ).then_inc(paired[2 * i + k], 16)

                def add_pair(c, i):
                    t, n = TB * c + i, 2 * (TB * (c - 2) + i)
                    for k in range(2):
                        pool.wait_ge(scaled, n + k + 1)
                        if k == 1:
                            pool.wait_ge(summed, n + 1)
                        pool.tensor_tensor(X[:, t, :], X[:, t, :], pair[2 * i + k][:, :], ALU.add).then_inc(summed, 1)

                for i in range(TB):
                    gather(0, i)
                norm.pool_rstd_for_act(pool, 0)
                for i in range(TB):
                    gather(1, i)
                def rs_of(t):
                    pool.wait_ge(var_ready, t + 1)
                    pool.tensor_tensor(rs[:, t:t + 1], ve[:, t:t + 1], negh[:, 0:1], ALU.pow).then_inc(rs_ready, 1)

                rs_of(0)
                for b in range(B):
                    for i in range(TB):
                        if i == TB - 1 and b in (1, 2):
                            fnorm.pool_rstd(pool, b - 1)
                        if TB * b + i + 1 < T:
                            rs_of(TB * b + i + 1)
                        if b == B - 1 and i == 0:
                            u.pool_gate_up(pool, 0, 0)
                        if i == 0 and b + 1 < B:
                            norm.pool_rstd_for_act(pool, b + 1)
                        if b + 2 < B:
                            gather(b + 2, i)
                            if i >= 1:
                                add_pair(b + 2, i - 1)
                    if b + 2 < B:
                        add_pair(b + 2, TB - 1)

            @block.tensor
            def _(pe):
                for b in range(B):
                    if b >= 1:
                        pe.wait_ge(kvT_made, b)
                    product3(pe, KVB, wk_hi[:, :], wk_lo[:, :], c_hi[:, N * b:N * b + N], c_lo[:, N * b:N * b + N],
                             True, True).then_inc(kvT_done, 1)
                    pe.wait_ge(kvT_made, b + 1)
                    if b >= 1:
                        pe.wait_ge(kv_lo_done, b)
                    for i in range(TB):
                        ins = pe.transpose(KTB[:, P * i:P * i + P], kvT[:, P * i:P * i + P], ident[:, :])
                    ins.then_inc(kv_turned, 1)
                def turn_two(c, i):
                    for n in range(2):
                        norm.pe_turn(pe, TB * c + i + n)

                pe.wait_ge(kv_lo_done, B)
                turn_two(0, 0)
                turn_two(0, 2)
                for b in range(B):
                    pe.wait_ge(norm.lo_done, TB * (b + 1))
                    if b >= 1:
                        pe.wait_ge(o_lo_done, b)
                    for j in range(TB):
                        ins = product3(pe, OB, kv_hi[:, b, j, :], kv_lo[:, b, j, :], x_hi[:, b % 2, j, :], x_lo[:, b % 2, j, :],
                                       j == 0, j == TB - 1)
                    ins.then_inc(o_done, 1)
                    pe.wait_ge(o_lo_done, b + 1)
                    for i in range(TB):
                        t = TB * b + i
                        if i == TB - 1 and b + 1 < B:
                            turn_two(b + 1, 0)
                            if b == 2:
                                fnorm.pe_turn(pe, 0)
                                fnorm.pe_turn(pe, 1)
                        if t >= 3:
                            pe.wait_ge(sim_free, t - 2)
                        product3(pe, SIM[t % 3], o_hi[:, P * i:P * i + P], o_lo[:, P * i:P * i + P], kvT_hi[:, b, :],
                                 kvT_lo[:, b, :], True, True).then_inc(sim_done, 1)
                    if b + 1 < B:
                        turn_two(b + 1, 2)
                        if b == 2:
                            fnorm.pe_turn(pe, 2)
                            fnorm.pe_turn(pe, 3)
                pe.wait_ge(fnorm.lo_done, TB)
                u.pe_gate_up(pe, 0, 0, tiles=(0,), first=True)

            @block.scalar
            def _(act):
                for b in range(B):
                    act.wait_ge(kvT_made, b + 1)
                    act.copy(kvT_hi[:, b, :], kvT[:, :]).then_inc(kvT_hi_done, 1)
                    act.wait_ge(kv_turned, b + 1)
                    act.copy(kv_hi[:, b, :, :], KTB.rearrange("p (j d) -> p j d", j=TB)).then_inc(kv_hi_done, 1)
                def x_norm(c, i):
                    norm.act_norm(act, TB * c + i)

                def x_hi_of(c, i):
                    if c >= 2 and i == 0:
                        act.wait_ge(o_done, c - 1)
                    norm.act_hi(act, TB * c + i, x_hi[:, c % 2, :, P * i:P * i + P])

                def scale_pair(c, i):
                    for k in range(2):
                        t, pk = TB * c + i, pair[2 * i + k]
                        act.wait_ge(paired[2 * i + k], 16 * (c + 1))
                        act.activation(pk[:, :], pk[:, :], ACT.Identity,
                                       scale=rt["weight"][:, t, k:k + 1]).then_inc(scaled, 1)

                def exp_of(t):
                    act.wait_ge(y_ready, t + 1)
                    if t >= 2:
                        act.wait_ge(x_added, t - 1)
                    act.activation(prob[:, t % 2, :], y[:, t % 3, :], ACT.Exp, bias=nmax[:, t:t + 1],
                                   accum_out=den[:, t:t + 1]).then_inc(prob_ready, 1)

                for i in (0, 2):
                    x_norm(0, i)
                    x_norm(0, i + 1)
                    x_hi_of(0, i)
                    x_hi_of(0, i + 1)

                def o_hi_of(b):
                    act.wait_ge(o_done, b + 1)
                    if b >= 1:
                        act.wait_ge(sim_done, TB * b)
                    act.copy(o_hi[:, :], OB).then_inc(o_hi_done, 1)

                o_hi_of(0)
                for b in range(B):
                    for i in range(TB):
                        exp_of(TB * b + i)
                        if b == B - 1 and i == 0:
                            u.act_gate_up(act, 0, 0, first=True)
                        if b + 1 < B and i % 2 == 0:
                            x_norm(b + 1, i)
                            x_norm(b + 1, i + 1)
                            x_hi_of(b + 1, i)
                            x_hi_of(b + 1, i + 1)
                            if b == 2:
                                for n in (i, i + 1):
                                    fnorm.act_hi(act, n, fx_hi[:, :, P * n:P * n + P])
                        if b + 2 < B and i >= 1:
                            scale_pair(b + 2, i - 1)
                    if b + 1 < B:
                        o_hi_of(b + 1)
                    if b + 2 < B:
                        scale_pair(b + 2, TB - 1)

            @block.vector
            def _(dve):
                chain = Chain(dve, dve_chain)
                def add_pairs(c, k):
                    for i in range(TB):
                        t = TB * c + i
                        dve.wait_ge(paired[2 * i + k], 16 * (c + 1))
                        if k == 1:
                            dve.wait_ge(added, 2 * TB * c + i + 1)
                        dve.scalar_tensor_tensor(out=X[:, t, :], in0=pair[2 * i + k][:, :],
                                                 scalar=rt["weight"][:, t, k:k + 1], in1=X[:, t, :],
                                                 op0=ALU.mult, op1=ALU.add).then_inc(added, 1)
                    dve.wait_ge(added, TB * (2 * c + k + 1))

                def x_lo_of(c, i):
                    s = slice(P * i, P * i + P)
                    norm.dve_lo(dve, TB * c + i, x_hi[:, c % 2, :, s], x_lo[:, c % 2, :, s])

                for b in range(B):
                    dve.wait_ge(kvT_done, b + 1)
                    if b >= 1:
                        dve.wait_ge(kv_turned, b)
                        dve.wait_ge(kvT_lo_done, b)
                    dve.tensor_scalar(kvT[:, :], KVB, bk[:, 0:1], None, ALU.add).then_inc(kvT_made, 1)
                    if b >= 2:
                        add_pairs(0, b - 2)
                    dve.wait_ge(kvT_hi_done, b + 1)
                    dve.tensor_tensor(kvT_lo[:, b, :], kvT[:, :], kvT_hi[:, b, :].bitcast(F32),
                                      ALU.subtract).then_inc(kvT_lo_done, 1)
                    dve.wait_ge(kv_hi_done, b + 1)
                    dve.tensor_tensor(kv_lo[:, b, :, :], KTB.rearrange("p (j d) -> p j d", j=TB),
                                      kv_hi[:, b, :, :].bitcast(F32), ALU.subtract).then_inc(kv_lo_done, 1)

                def centre(t):
                    sim, yt = SIM[t % 3], y[:, t % 3, :]
                    dve.wait_ge(sim_done, t + 1)
                    chain.link(dve.bn_stats(st[:, t % 2, :], sim))
                    chain.link(dve.bn_aggr(mv[:, t, :], st[:, t % 2, :]))
                    dve.tensor_scalar(ve[:, t:t + 1], mv[:, t, 1:2], EPS_ATT / SCALE ** 2, None,
                                      ALU.add).then_inc(var_ready, 1)
                    if t >= 3:
                        dve.wait_ge(prob_ready, t - 2)
                    dve.scalar_tensor_tensor(out=yt, in0=sim, scalar=mv[:, t, 0:1], in1=gamma[:, :], op0=ALU.subtract,
                                             op1=ALU.mult).then_inc(sim_free, 1)

                def scores_norm(t):
                    yt = y[:, t % 3, :]
                    dve.wait_ge(rs_ready, t + 1)
                    dve.wait_ge(sim_free, t + 1)
                    chain.n += 1
                    dve.scalar_tensor_tensor(out=yt, in0=yt, scalar=rs[:, t:t + 1], in1=beta[:, :], op0=ALU.mult,
                                             op1=ALU.add).then_inc(chain.sem, 1)
                    dve.wait_ge(chain.sem, chain.n)
                    dve.tensor_reduce(nmax[:, t:t + 1], yt, AX.X, ALU.max, negate=True).then_inc(y_ready, 1)

                def add_prob(t):
                    dve.wait_ge(prob_ready, t + 1)
                    chain.link(dve.reciprocal(rden[:, t:t + 1], den[:, t:t + 1]))
                    dve.scalar_tensor_tensor(out=X[:, t, :], in0=prob[:, t % 2, :], scalar=rden[:, t:t + 1],
                                             in1=X[:, t, :], op0=ALU.mult, op1=ALU.add).then_inc(x_added, 1)

                norm.dve_stats_for_act(chain, 0)
                dve.wait_ge(ld_row, 32)
                for i in range(TB):
                    x_lo_of(0, i)
                def o_lo_of(b):
                    dve.wait_ge(o_hi_done, b + 1)
                    dve.tensor_tensor(o_lo[:, :], OB, o_hi[:, :].bitcast(F32), ALU.subtract).then_inc(o_lo_done, 1)

                add_pairs(1, 0)
                o_lo_of(0)
                centre(0)
                for b in range(B):
                    for i in range(TB):
                        t = TB * b + i
                        if i + 1 < TB:
                            centre(t + 1)
                        scores_norm(t)
                        if t >= 1:
                            add_prob(t - 1)
                        if b + 1 < B:
                            if i == 0:
                                if b == 0:
                                    add_pairs(1, 1)
                                else:
                                    dve.wait_ge(summed, 2 * TB * b)
                                norm.dve_stats_for_act(chain, b + 1)
                                if b == 2:
                                    fnorm.dve_norm(dve, 0)
                                    fnorm.dve_norm(dve, 1)
                            if i in (1, 2):
                                for n in (2 * i - 2, 2 * i - 1):
                                    x_lo_of(b + 1, n)
                                if b == 2:
                                    for n in (2 * i - 2, 2 * i - 1):
                                        if n < 2:
                                            fnorm.dve_norm(dve, n + 2)
                                        fnorm.dve_lo(dve, n, fx_hi[:, :, P * n:P * n + P], fx_lo[:, :, P * n:P * n + P])
                            if i == TB - 1 and b in (1, 2):
                                dve.wait_ge(x_added, TB * b)
                                fnorm.dve_stats(chain, b - 1)
                            if i == TB - 1:
                                o_lo_of(b + 1)
                                centre(t + 1)
                add_prob(T - 1)


def ffn(nc, outer, dram, out):
    X, ident, negh, ps, sem = (outer[k] for k in ("X", "ident", "negh", "ps", "sem"))
    HN = N // 2
    with ExitStack() as ctx:
        def sb(name, shape, dt=F32):
            return ctx.enter_context(nc.sbuf_tensor("f_" + name, shape, dt))

        u = outer["units"]
        for c in range(1, B):
            u.x_hi.append(sb(f"x_hi{c}", [P, DC, N], F32R))
            u.x_lo.append(sb(f"x_lo{c}", [P, DC, N], F32R))
        for r in range(1, RQ):
            u.w_hi.append(sb(f"w_hi{r}", [P, 3, D], F32R))
            u.w_lo.append(sb(f"w_lo{r}", [P, 3, D], F32R))
        hid_hi, hid_lo = (outer["kv"][name][:, :].rearrange("p (k r n) -> p k r n", k=1, r=RQ)
                          for name in ("c_hi", "c_lo"))
        u.hid_hi, u.hid_lo = hid_hi, hid_lo
        sg = sb("sg", [P, 2, N])
        hid = sb("hid", [P, RQ, N])
        mag = outer["kv"]["c_raw"][:, :].rearrange("p (r n) -> p r n", r=RQ)
        beats = sb("beats", [P, 6, HN], BF16)
        norm = outer["ffn_norm"]
        tally = norm.xn[:, 0, :].bitcast(BF16).rearrange("p (r n) -> p r n", r=RQ)
        mag_ready, mag_free, masked, dve_chain = sem("f_mag_ready"), sem("f_mag_free"), sem("f_masked"), sem("f_dve_chain")
        step_chain, stored = sem("f_step_chain"), sem("f_stored")
        LINKS = 2 * 4
        PAIRS = range(TB // 2, T // 2)
        hidden_behind = {2: 0, 4: 1, 6: 2, 7: 3}

        with nc.Block() as block:
            @block.sync
            def _(sp):
                for r in range(2, RQ):
                    u.load_gate_up(sp, dram["ffn_gu"], 0, r)
                with sp.Fori(1, Q) as q:
                    for r in range(2):
                        u.load_gate_up(sp, dram["ffn_gu"], q, r)
                    for r in range(RQ):
                        u.load_down(sp, dram["ffn_dn"], q, r)
                    for r in range(2, RQ):
                        u.load_gate_up(sp, dram["ffn_gu"], q, r)
                for c in range(B):
                    sp.wait_ge(u.acc_free, TB + 16 * (Q - 1) + 4 * (c + 1))
                    sp.dma_start(out[c], X[:, TB * c:TB * c + TB, :]).then_inc(stored, 16)
                sp.wait_ge(stored, 16 * B)

            @block.gpsimd
            def _(pool):
                for r in range(1, RQ):
                    u.pool_gate_up(pool, 0, r)
                    if r + 1 < B:
                        norm.pool_rstd(pool, r + 1)
                for r in range(RQ):
                    u.pool_down(pool, 0, r)
                with pool.Fori(1, Q) as q:
                    for r in range(RQ):
                        u.pool_gate_up(pool, q, r)
                    for r in range(RQ):
                        u.pool_down(pool, q, r)

            @block.tensor
            def _(pe):
                turns = iter(range(TB, T))

                def turn_two():
                    for t in islice(turns, 2):
                        norm.pe_turn(pe, t)

                turn_two()
                u.pe_gate_up(pe, 0, 0, tiles=range(1, RQ), first=True, between=turn_two)
                pe.wait_ge(norm.lo_done, T)
                u.pe_rest(pe)

            @block.scalar
            def _(act):
                u.act_gate_up(act, 0, 1, first=True)

                def sparsify(q, c, first=False):
                    s = 8 * q + 2 * c
                    act.wait_ge(u.hid_made, u.at(q, c, RQ))
                    for h in range(2):
                        half = slice(HN * h, HN * h + HN)
                        if not first:
                            act.wait_ge(mag_free, s + (h - 1))
                        act.activation(mag[:, :, half], hid[:, :, half], ACT.Abs).then_inc(mag_ready, 1)
                    if not first:
                        act.wait_ge(u.acc_done, 16 * q + 4 * c)
                    for h in range(2):
                        half = slice(HN * h, HN * h + HN)
                        act.wait_ge(masked, s + (h + 1))
                        act.copy(hid_hi[:, 0, :, half], hid[:, :, half]).then_inc(u.hid_hi_done, 1)

                for n in PAIRS:
                    for t in (2 * n, 2 * n + 1):
                        i = t % TB
                        norm.act_hi(act, t, u.x_hi[t // TB][:, :, P * i:P * i + P])
                    if n in (3, 5):
                        u.act_gate_up(act, 0, (n + 1) // 2, first=True)
                    if n == PAIRS[-1]:
                        for r in range(RQ):
                            u.act_down(act, 0, r, first=True)
                    if n in hidden_behind:
                        u.act_silu(act, 0, 0, hidden_behind[n], sg, first=True)
                sparsify(0, 0, first=True)
                with act.Fori(0, Q - 1) as q:
                    for c in (1, 2, 3):
                        for r in range(RQ):
                            u.act_silu(act, q, c, r, sg)
                            if c == 3:
                                u.act_gate_up(act, q + 1, r)
                        sparsify(q, c)
                    for r in range(RQ):
                        u.act_silu(act, q + 1, 0, r, sg)
                    sparsify(q + 1, 0)
                    for r in range(RQ):
                        u.act_down(act, q + 1, r)
                for c in (1, 2, 3):
                    for r in range(RQ):
                        u.act_silu(act, Q - 1, c, r, sg)
                    sparsify(Q - 1, c)

            @block.vector
            def _(dve):
                chain = Chain(dve, dve_chain)

                dve.sem_inc(u.acc_free, TB)

                def hidden(q, c, first=False):
                    if first:
                        for n in PAIRS:
                            for t in (2 * n, 2 * n + 1):
                                norm.dve_norm(dve, t)
                            if n in (2, 4):
                                norm.dve_stats(chain, n // 2 + 1)
                            for t in (2 * n, 2 * n + 1):
                                k, s = t // TB, slice(P * (t % TB), P * (t % TB) + P)
                                norm.dve_lo(dve, t, u.x_hi[k][:, :, s], u.x_lo[k][:, :, s])
                            if n in hidden_behind:
                                r = hidden_behind[n]
                                u.dve_hid(dve, q, c, r, sg, hid[:, r, :])
                    else:
                        dve.wait_ge(u.hid_lo_done, 8 * q + 2 * c)
                        for r in range(RQ):
                            u.dve_hid(dve, q, c, r, sg, hid[:, r, :])
                    for h in range(2):
                        keep_two(q, c, h)
                    for h in range(2):
                        split(q, c, h)

                def keep_two(q, c, h):
                    links = LINKS * 4 * q + LINKS * c + 4 * h
                    half = slice(HN * h, HN * h + HN)
                    dve.wait_ge(mag_ready, 8 * q + (2 * c + h + 1))
                    for i, j0, j1, at in ((0, 1, 4, 0), (1, 2, 4, 3), (2, 3, 4, 5)):
                        n = j1 - j0
                        ins = dve.tensor_tensor(beats[:, at:at + n, :],
                                                mag[:, i, half].unsqueeze(1).broadcast_to([P, n, HN]),
                                                mag[:, j0:j1, half], ALU.is_ge)
                    ins.then_inc(step_chain, 1)
                    dve.wait_ge(step_chain, links + 1)
                    dve.sem_inc(mag_free, 1)
                    b = [beats[:, k, :] for k in range(6)]
                    dve.tensor_tensor(tally[:, 0, :], b[0], b[1], ALU.add)
                    dve.tensor_tensor(tally[:, 1, :], b[0], b[3], ALU.subtract)
                    dve.tensor_tensor(tally[:, 2, :], b[1], b[3], ALU.add)
                    dve.tensor_tensor(tally[:, 3, :], b[2], b[4], ALU.add).then_inc(step_chain, 1)
                    dve.wait_ge(step_chain, links + 2)
                    dve.tensor_tensor(tally[:, 0, :], tally[:, 0, :], b[2], ALU.add)
                    dve.tensor_tensor(tally[:, 1, :], tally[:, 1, :], b[4], ALU.subtract)
                    dve.tensor_tensor(tally[:, 2, :], tally[:, 2, :], b[5], ALU.subtract)
                    dve.tensor_tensor(tally[:, 3, :], tally[:, 3, :], b[5], ALU.add).then_inc(step_chain, 1)
                    dve.wait_ge(step_chain, links + 3)
                    for r, (bound, op) in enumerate(((1.5, ALU.is_ge), (-0.5, ALU.is_le), (0.5, ALU.is_le),
                                                     (1.5, ALU.is_le))):
                        ins = dve.scalar_tensor_tensor(out=hid[:, r, half], in0=tally[:, r, :], scalar=bound,
                                                       in1=hid[:, r, half], op0=op, op1=ALU.mult)
                    ins.then_inc(step_chain, 1)
                    dve.wait_ge(step_chain, links + 4)
                    dve.sem_inc(masked, 1)

                def split(q, c, h):
                    half = slice(HN * h, HN * h + HN)
                    dve.wait_ge(u.hid_hi_done, 8 * q + (2 * c + h + 1))
                    dve.tensor_tensor(hid_lo[:, 0, :, half], hid[:, :, half], hid_hi[:, 0, :, half].bitcast(F32),
                                      ALU.subtract).then_inc(u.hid_lo_done, 1)

                def evac(q, c):
                    for i in range(TB):
                        u.dve_wait_acc(dve, q, c, i)
                        dve.tensor_tensor(X[:, TB * c + i, :], u.ACC[i], X[:, TB * c + i, :],
                                          ALU.add).then_inc(u.acc_free, 1)

                hidden(0, 0, first=True)
                with dve.Fori(0, Q - 1) as q:
                    for c in range(4):
                        hidden(*((q, c + 1) if c < 3 else (q + 1, 0)))
                        evac(q, c)
                for c in range(4):
                    if c < 3:
                        hidden(Q - 1, c + 1)
                    evac(Q - 1, c)


def build(nc, dram, out):
    with ExitStack() as ctx:
        def sem(name):
            return ctx.enter_context(nc.semaphore(name))

        def sb(name, shape, dt=F32):
            return ctx.enter_context(nc.sbuf_tensor(name, shape, dt))

        outer = {
            "sem": sem,
            "X": sb("x", [P, T, D]),
            "ident": sb("ident", [P, P]),
            "negh": sb("minus_half", [P, TB]),
            "flag": sb("flag", [1, 1], I32),
            "ps": ctx.enter_context(nc.psum_tensor("ps", [P, 8, 512], F32)),
            "ld_gu": [sem(f"ld_gate_up{r}") for r in range(2)],
            "ld_dn": [sem(f"ld_down{r}") for r in range(RQ)],
            "pool_const": sem("pool_const"),
        }
        raw = sb("raw", [P, (2 * DC * FE) + RE * D])
        gu, dn = 2 * DC * FE, RE * D
        outer["raw_gu"] = raw[:, 0:4 * D].rearrange("p (s k n) -> p s k n", s=2, k=2)
        outer["raw_dn"] = raw[:, 4 * D:8 * D].rearrange("p (s n) -> p s n", s=RQ)
        route_ = outer["route"] = {
            "raw_gu": raw[:, 0:gu].rearrange("p (d k f) -> p d k f", d=DC, k=2),
            "raw_dn": raw[:, gu:gu + dn].rearrange("p (r n) -> p r n", r=RE),
            "slot": sb("slot", [P, 2 * T], I32),
            "weight": sb("weight", [P, T, 2]),
            "token": sb("token", [P, REAL + 1], I32),
            "table": sb("table", [1, REAL], I32),
            "xn_dram": nc.dram_tensor("xn_scratch", (B * N, D), F32, kind="Internal").ap(),
            "y_dram": nc.dram_tensor("y_scratch", (REAL * P, D), F32, kind="Internal").ap(),
            **{k: sem("e_" + k) for k in ("ld_gu", "ld_dn", "gu_hi", "dn_hi")},
        }
        gat_one_hot(nc, outer, dram)
        holds = nc.values_load(outer["flag"][0:1, 0:1], min_val=0, max_val=1)
        with nc.If(holds == 0):
            gat_general(nc, outer, dram)
        with ExitStack() as kv_inputs, ExitStack() as experts:
            kv = outer["kv"] = {"loaded": sem("kv_loaded"), "hi": sem("kv_hi")}
            for name, shape, dt in (("c_raw", [P, B * N], F32), ("c_hi", [P, B * N], F32R), ("c_lo", [P, B * N], F32R),
                                    ("wk_raw", [P, CTX], F32), ("wk_hi", [P, CTX], F32R), ("wk_lo", [P, CTX], F32R),
                                    ("bk", [P, 1], F32)):
                kv[name] = kv_inputs.enter_context(nc.sbuf_tensor("kv_" + name, shape, dt))
            for name, shape in (("gu_w", [P, 2, DC, 2, FE]), ("dn_w", [P, 2, RE, D])):
                for part in ("_hi", "_lo"):
                    route_[name + part] = experts.enter_context(nc.sbuf_tensor(name + part, shape, F32R))
            route(nc, outer, dram)
            moe(nc, outer, dram)
            experts.close()
            with ExitStack() as last:
                def sb_last(name, shape, dt=F32):
                    return last.enter_context(nc.sbuf_tensor(name, shape, dt))

                ps = outer["ps"]
                outer["ffn_norm"] = Norm("f_", sb_last, sem, outer["X"], outer["ident"], outer["negh"],
                                         [ps[:, 2 + k, :] for k in range(6)],
                                         order=[0, 1, 0, 1] + [2 + t % TB for t in range(TB, T)])
                x_hi, x_lo = ([sb_last(f"f_{name}0", [P, DC, N], F32R)] for name in ("x_hi", "x_lo"))
                w_hi, w_lo = ([sb_last(f"f_{name}0", [P, 3, D], F32R)] for name in ("w_hi", "w_lo"))
                outer["units"] = Units("f_", outer, Q, RQ, 2, w_hi, w_lo, x_hi, x_lo, los=2)
                image_attention(nc, outer, dram)
                ffn(nc, outer, dram, out)


def kernel(x, ctx_512, L0_xattn_W0, L0_xattn_a_self0, L0_xattn_a_neigh0, L0_xattn_b0, L0_xattn_W1,
           L0_xattn_a_self1, L0_xattn_a_neigh1, L0_xattn_b1, L0_ffn_gate_w, L0_ffn_gate_proj, L0_ffn_up_proj,
           L0_ffn_down_proj, L1_xattn_W_k, L1_xattn_b_k, L1_xattn_ln_gamma, L1_xattn_ln_beta, L1_ffn_w_gate,
           L1_ffn_w_up, L1_ffn_w_down):
    import numpy as np
    from concourse import bacc
    from concourse.bass_utils import run_bass_kernel_spmd

    def tokens(a):
        return a.reshape(-1, P, a.shape[-1]).transpose(1, 0, 2)

    def heads(w):
        return w.transpose(1, 0, 2).reshape(-1, P, H * FO).transpose(1, 0, 2)

    pad = ((0, 0), (0, RE * P - FE), (0, 0))

    def expert_in(w):
        return w.reshape(E, FE, DC, P).transpose(0, 3, 2, 1)

    def quartet_in(w):
        return w.reshape(DC, P, Q, P, RQ).transpose(2, 4, 1, 0, 3).reshape(Q * RQ, P, D)

    a = {k: np.asarray(v) for k, v in locals().items() if hasattr(v, "shape")}
    arrays = {
        "x": a["x"].reshape(B, TB, P, D).transpose(0, 2, 1, 3),
        "ctx": tokens(a["ctx_512"]),
        "ctxT": a["ctx_512"].reshape(B * N, CTX).T,
        "gat_w": np.concatenate([heads(a["L0_xattn_W0"]), heads(a["L0_xattn_W1"])], axis=1),
        "att0": np.stack([a["L0_xattn_a_self0"].ravel(), a["L0_xattn_a_neigh0"].ravel()]),
        "att1": np.stack([a["L0_xattn_a_self1"].ravel(), a["L0_xattn_a_neigh1"].ravel()]),
        "b0_col": a["L0_xattn_b0"].reshape(DC, P).T,
        "b0": a["L0_xattn_b0"].reshape(1, D),
        "b1": a["L0_xattn_b1"].reshape(1, D),
        "gate_w": a["L0_ffn_gate_w"].reshape(E, DC, P).transpose(2, 1, 0),
        "moe_gu": np.stack([expert_in(a["L0_ffn_gate_proj"]), expert_in(a["L0_ffn_up_proj"])], axis=3),
        "moe_dn": np.pad(a["L0_ffn_down_proj"].transpose(0, 2, 1), pad).reshape(E, RE, P, D).transpose(0, 2, 1, 3),
        "wkT": a["L1_xattn_W_k"].T,
        "bk": a["L1_xattn_b_k"].reshape(CTX, 1),
        "gamma": a["L1_xattn_ln_gamma"].reshape(1, N),
        "beta": a["L1_xattn_ln_beta"].reshape(1, N),
        "ffn_gu": np.stack([quartet_in(a["L1_ffn_w_gate"]), quartet_in(a["L1_ffn_w_up"])], axis=2),
        "ffn_dn": a["L1_ffn_w_down"].reshape(Q, P, RQ, D).transpose(0, 2, 1, 3).reshape(Q * RQ, P, D),
    }
    nc = bacc.Bacc("TRN2", target_bir_lowering=False, num_devices=1)
    in_map, dram = {}, {}
    for name, v in arrays.items():
        in_map["in_" + name] = np.ascontiguousarray(v)
        dram[name] = nc.dram_tensor("in_" + name, v.shape, mybir.dt.from_np(v.dtype), kind="ExternalInput").ap()
    out = nc.dram_tensor("out", (B, P, TB, D), F32, kind="ExternalOutput").ap()
    build(nc, dram, out)
    r = run_bass_kernel_spmd(nc, [in_map], core_ids=[0])
    return r.results[0]["out"].reshape(B, P, TB, D).transpose(0, 2, 1, 3).reshape(B, N, D)
```
